# Optimizing a Trainium2 kernel written in Bass

```python
import numpy as np
import jax
import jax.numpy as jnp

def _softmax(x, axis=-1):
    return jax.nn.softmax(x, axis=axis)

def _gelu(x):
    return jax.nn.gelu(x, approximate=True)

def _silu(x):
    return jax.nn.silu(x)

def _sigmoid(x):
    return jax.nn.sigmoid(x)

def _layernorm(x, axis=-1, eps=1e-05):
    m = jnp.mean(x, axis=axis, keepdims=True)
    v = jnp.var(x, axis=axis, keepdims=True)
    return (x - m) / jnp.sqrt(v + eps)

def _scatter_add(tgt, idx, src, axis=0):
    return tgt.at[idx].add(src)

def _segment_sum(src, seg, n):
    return jax.ops.segment_sum(src, seg, n)
kernel_name = 'mk_seq_preln_d2_jaxref_r8_a04901'

def setup_inputs(seed: int=0):
    np.random.seed(seed)
    _w = jnp.asarray

    def _L0_attn_setup():
        import jax, jax.numpy as jnp
        import numpy as np
        D_MODEL = 256
        B, S = (2, 256)
        key = jax.random.key(seed)
        kx, kq, kk, kv, ko = jax.random.split(key, 5)
        std = 1.0 / np.sqrt(D_MODEL)
        return {'x': jax.random.normal(kx, (B, S, D_MODEL), dtype=jnp.float32), 'W_q': jax.random.normal(kq, (D_MODEL, D_MODEL), dtype=jnp.float32) * std, 'W_k': jax.random.normal(kk, (D_MODEL, D_MODEL), dtype=jnp.float32) * std, 'W_v': jax.random.normal(kv, (D_MODEL, D_MODEL), dtype=jnp.float32) * std, 'W_o': jax.random.normal(ko, (D_MODEL, D_MODEL), dtype=jnp.float32) * std}
    _L0_attn_in = _L0_attn_setup()

    def _L0_ffn_setup():
        import jax, jax.numpy as jnp
        import numpy as np
        E, K = (12, 3)
        B, S, H, I = (2, 256, 256, 640)

        def _forward(x, Wr, br, w1, b1, w2, b2, Wp1, bp1, Wp2, bp2):
            logits = jnp.einsum('bsh,he->bse', x, Wr) + br
            probs = jax.nn.softmax(logits, axis=-1)
            top_vals, top_idx = jax.lax.top_k(probs, K)
            ew = jax.nn.softmax(top_vals, axis=-1)
            out = jnp.zeros_like(x)
            for e in range(E):
                sel = top_idx == e
                mask = sel.any(axis=-1)
                cnt = sel.sum()
                w_e = jnp.sum(jnp.where(sel, ew, 0.0)) / jnp.maximum(cnt, 1).astype(ew.dtype)
                h = jax.nn.relu(jnp.einsum('bsh,hi->bsi', x, w1[e]) + b1[e])
                h = jnp.einsum('bsi,ih->bsh', h, w2[e]) + b2[e]
                out = out + mask[..., None].astype(x.dtype) * (w_e * h)
            pooled = out.mean(axis=1)
            phi = jax.nn.sigmoid(jax.nn.relu(pooled @ Wp1 + bp1) @ Wp2 + bp2)
            phi_mask = (phi > 0.7).astype(out.dtype)[:, :, None]
            return out * (1.0 - phi_mask * 0.8)
        key = jax.random.key(seed)
        ks = jax.random.split(key, 8)
        sH = np.float32(1.0 / np.sqrt(H))
        sI = np.float32(1.0 / np.sqrt(I))
        sH2 = np.float32(1.0 / np.sqrt(H // 2))
        return {'hidden_states': jax.random.normal(ks[0], (B, S, H), jnp.float32), 'Wr': jax.random.normal(ks[1], (H, E), jnp.float32) * sH, 'br': jnp.zeros((E,), jnp.float32), 'w1': jax.random.normal(ks[2], (E, H, I), jnp.float32) * sH, 'b1': jnp.zeros((E, I), jnp.float32), 'w2': jax.random.normal(ks[3], (E, I, H), jnp.float32) * sI, 'b2': jnp.zeros((E, H), jnp.float32), 'Wp1': jax.random.normal(ks[4], (H, H // 2), jnp.float32) * sH, 'bp1': jnp.zeros((H // 2,), jnp.float32), 'Wp2': jax.random.normal(ks[5], (H // 2, 1), jnp.float32) * sH2, 'bp2': jnp.zeros((1,), jnp.float32)}
    _L0_ffn_in = _L0_ffn_setup()

    def _L1_attn_setup():
        import jax, jax.numpy as jnp
        import numpy as np
        HIDDEN = 256
        HEADS = 16
        HEAD_DIM = HIDDEN // HEADS
        SCALE = 1.0 / np.sqrt(HEAD_DIM).astype(np.float32)
        key = jax.random.key(seed)
        k1, k2, k3, k4, k5 = jax.random.split(key, 5)
        B, QL = (8, 128)
        NB, BS = (32, 128)
        query = jax.random.normal(k1, (B, QL, HIDDEN), dtype=jnp.float32)
        kv_k = jax.random.normal(k2, (NB, BS, HIDDEN), dtype=jnp.float32)
        kv_v = jax.random.normal(k3, (NB, BS, HIDDEN), dtype=jnp.float32)
        Wq = jax.random.normal(k4, (HIDDEN, HIDDEN), dtype=jnp.float32) * (1.0 / np.sqrt(HIDDEN))
        Wo = jax.random.normal(k5, (HIDDEN, HIDDEN), dtype=jnp.float32) * (1.0 / np.sqrt(HIDDEN))
        return {'query': query, 'kv_k': kv_k, 'kv_v': kv_v, 'Wq': Wq, 'Wo': Wo}
    _L1_attn_in = _L1_attn_setup()

    def _L1_ffn_setup():
        import jax, jax.numpy as jnp
        import numpy as np
        B, L, D = (2, 128, 256)
        E, K = (8, 2)
        H, HS = (176, 352)
        key = jax.random.key(seed)
        ks = jax.random.split(key, 9)
        s = 0.02
        return {'x': jax.random.normal(ks[0], (B, L, D), dtype=jnp.float32), 'gate_w': jax.random.normal(ks[1], (E, D), dtype=jnp.float32) * s, 'w_gate': jax.random.normal(ks[2], (E, D, H), dtype=jnp.float32) * s, 'w_up': jax.random.normal(ks[3], (E, D, H), dtype=jnp.float32) * s, 'w_down': jax.random.normal(ks[4], (E, H, D), dtype=jnp.float32) * s, 'shgate_w': jax.random.normal(ks[5], (D,), dtype=jnp.float32) * s, 'shw_gate': jax.random.normal(ks[6], (D, HS), dtype=jnp.float32) * s, 'shw_up': jax.random.normal(ks[7], (D, HS), dtype=jnp.float32) * s, 'shw_down': jax.random.normal(ks[8], (HS, D), dtype=jnp.float32) * s}
    _L1_ffn_in = _L1_ffn_setup()
    _d = {'L0_attn_x': _L0_attn_in['x'], 'L0_attn_W_q': _L0_attn_in['W_q'], 'L0_attn_W_k': _L0_attn_in['W_k'], 'L0_attn_W_v': _L0_attn_in['W_v'], 'L0_attn_W_o': _L0_attn_in['W_o'], 'L0_ffn_Wr': _L0_ffn_in['Wr'], 'L0_ffn_br': _L0_ffn_in['br'], 'L0_ffn_w1': _L0_ffn_in['w1'], 'L0_ffn_b1': _L0_ffn_in['b1'], 'L0_ffn_w2': _L0_ffn_in['w2'], 'L0_ffn_b2': _L0_ffn_in['b2'], 'L0_ffn_Wp1': _L0_ffn_in['Wp1'], 'L0_ffn_bp1': _L0_ffn_in['bp1'], 'L0_ffn_Wp2': _L0_ffn_in['Wp2'], 'L0_ffn_bp2': _L0_ffn_in['bp2'], 'L1_attn_kv_k': _L1_attn_in['kv_k'], 'L1_attn_kv_v': _L1_attn_in['kv_v'], 'L1_attn_Wq': _L1_attn_in['Wq'], 'L1_attn_Wo': _L1_attn_in['Wo'], 'L1_ffn_gate_w': _L1_ffn_in['gate_w'], 'L1_ffn_w_gate': _L1_ffn_in['w_gate'], 'L1_ffn_w_up': _L1_ffn_in['w_up'], 'L1_ffn_w_down': _L1_ffn_in['w_down'], 'L1_ffn_shgate_w': _L1_ffn_in['shgate_w'], 'L1_ffn_shw_gate': _L1_ffn_in['shw_gate'], 'L1_ffn_shw_up': _L1_ffn_in['shw_up'], 'L1_ffn_shw_down': _L1_ffn_in['shw_down']}
    _x0 = _d['L0_attn_x']
    _d['L0_attn_x'] = jax.random.normal(jax.random.fold_in(jax.random.key(seed), 1), (4, 512, 256), dtype=_x0.dtype)
    del _x0
    return _d

def reference(L0_attn_x, L0_attn_W_q, L0_attn_W_k, L0_attn_W_v, L0_attn_W_o, L0_ffn_Wr, L0_ffn_br, L0_ffn_w1, L0_ffn_b1, L0_ffn_w2, L0_ffn_b2, L0_ffn_Wp1, L0_ffn_bp1, L0_ffn_Wp2, L0_ffn_bp2, L1_attn_kv_k, L1_attn_kv_v, L1_attn_Wq, L1_attn_Wo, L1_ffn_gate_w, L1_ffn_w_gate, L1_ffn_w_up, L1_ffn_w_down, L1_ffn_shgate_w, L1_ffn_shw_gate, L1_ffn_shw_up, L1_ffn_shw_down):

    def _L0_attn_ref(x, W_q, W_k, W_v, W_o):
        import jax, jax.numpy as jnp
        import numpy as np
        D_MODEL = 256
        B, S = (2, 256)
        scale = 1.0 / jnp.sqrt(jnp.asarray(x.shape[-1], x.dtype))
        Q = jnp.einsum('bsd,de->bse', x, W_q)
        K = jnp.einsum('bsd,de->bse', x, W_k)
        V = jnp.einsum('bsd,de->bse', x, W_v)
        scores = jnp.einsum('bqe,bke->bqk', Q, K) * scale
        attn = jax.nn.softmax(scores, axis=-1)
        out = jnp.einsum('bqk,bke->bqe', attn, V)
        return jnp.einsum('bse,ed->bsd', out, W_o)

    def _L0_ffn_ref(hidden_states, Wr, br, w1, b1, w2, b2, Wp1, bp1, Wp2, bp2):
        import jax, jax.numpy as jnp
        import numpy as np
        E, K = (12, 3)
        B, S, H, I = (2, 256, 256, 640)

        def _forward(x, Wr, br, w1, b1, w2, b2, Wp1, bp1, Wp2, bp2):
            logits = jnp.einsum('bsh,he->bse', x, Wr) + br
            probs = jax.nn.softmax(logits, axis=-1)
            top_vals, top_idx = jax.lax.top_k(probs, K)
            ew = jax.nn.softmax(top_vals, axis=-1)
            out = jnp.zeros_like(x)
            for e in range(E):
                sel = top_idx == e
                mask = sel.any(axis=-1)
                cnt = sel.sum()
                w_e = jnp.sum(jnp.where(sel, ew, 0.0)) / jnp.maximum(cnt, 1).astype(ew.dtype)
                h = jax.nn.relu(jnp.einsum('bsh,hi->bsi', x, w1[e]) + b1[e])
                h = jnp.einsum('bsi,ih->bsh', h, w2[e]) + b2[e]
                out = out + mask[..., None].astype(x.dtype) * (w_e * h)
            pooled = out.mean(axis=1)
            phi = jax.nn.sigmoid(jax.nn.relu(pooled @ Wp1 + bp1) @ Wp2 + bp2)
            phi_mask = (phi > 0.7).astype(out.dtype)[:, :, None]
            return out * (1.0 - phi_mask * 0.8)
        return _forward(hidden_states, Wr, br, w1, b1, w2, b2, Wp1, bp1, Wp2, bp2)

    def _L1_attn_ref(query, kv_k, kv_v, Wq, Wo):
        import jax, jax.numpy as jnp
        import numpy as np
        HIDDEN = 256
        HEADS = 16
        HEAD_DIM = HIDDEN // HEADS
        SCALE = 1.0 / np.sqrt(HEAD_DIM).astype(np.float32)
        B, QL, _ = query.shape
        NB, BS, _ = kv_k.shape
        KV = NB * BS
        Q = (query @ Wq.T).reshape(B, QL, HEADS, HEAD_DIM)
        K = kv_k.reshape(KV, HEADS, HEAD_DIM)
        V = kv_v.reshape(KV, HEADS, HEAD_DIM)
        scores = jnp.einsum('bqhd,khd->bhqk', Q, K) * SCALE
        attn = jax.nn.softmax(scores, axis=-1)
        out = jnp.einsum('bhqk,khd->bqhd', attn, V).reshape(B, QL, HIDDEN)
        return out @ Wo.T

    def _L1_ffn_ref(x, gate_w, w_gate, w_up, w_down, shgate_w, shw_gate, shw_up, shw_down):
        import jax, jax.numpy as jnp
        import numpy as np
        B, L, D = (2, 128, 256)
        E, K = (8, 2)
        H, HS = (176, 352)
        b, l, d = x.shape
        xf = x.reshape(-1, d)
        logits = jnp.einsum('td,ed->te', xf.astype(jnp.float32), gate_w)
        probs = jax.nn.softmax(logits.astype(jnp.float32), axis=-1)
        weights, indices = jax.lax.top_k(probs, K)
        weights = (weights / weights.sum(-1, keepdims=True)).astype(x.dtype)
        onehot = jax.nn.one_hot(indices, E, dtype=x.dtype)
        combine = jnp.einsum('tk,tke->te', weights, onehot)
        g = jnp.einsum('td,edh->teh', xf, w_gate)
        u = jnp.einsum('td,edh->teh', xf, w_up)
        h = jax.nn.silu(g) * u
        out = jnp.einsum('teh,ehd,te->td', h.astype(jnp.float32), w_down.astype(jnp.float32), combine.astype(jnp.float32))
        sgate = jax.nn.sigmoid(xf @ shgate_w)[:, None]
        sh = jax.nn.silu(xf @ shw_gate) * (xf @ shw_up) @ shw_down
        out = out + (sgate * sh).astype(jnp.float32)
        return out.astype(x.dtype).reshape(b, l, d)
    x = L0_attn_x
    x = x + _L0_attn_ref(_layernorm(x, axis=-1), L0_attn_W_q, L0_attn_W_k, L0_attn_W_v, L0_attn_W_o)
    x = x + _L0_ffn_ref(_layernorm(x, axis=-1), L0_ffn_Wr, L0_ffn_br, L0_ffn_w1, L0_ffn_b1, L0_ffn_w2, L0_ffn_b2, L0_ffn_Wp1, L0_ffn_bp1, L0_ffn_Wp2, L0_ffn_bp2)
    x = x + _L1_attn_ref(_layernorm(x, axis=-1), L1_attn_kv_k, L1_attn_kv_v, L1_attn_Wq, L1_attn_Wo)
    x = x + _L1_ffn_ref(_layernorm(x, axis=-1), L1_ffn_gate_w, L1_ffn_w_gate, L1_ffn_w_up, L1_ffn_w_down, L1_ffn_shgate_w, L1_ffn_shw_gate, L1_ffn_shw_up, L1_ffn_shw_down)
    return x

_drawn_inputs = setup_inputs


def setup_inputs(seed=0):
    import zlib

    import numpy as np

    out = dict(_drawn_inputs(seed))
    spreads = {'L0_ffn_br': (0.0, 0.1),
     'L0_ffn_b1': (0.0, 0.1),
     'L0_ffn_b2': (0.0, 0.1),
     'L0_ffn_bp1': (0.0, 0.1)}
    factors = {'L1_attn_kv_k': 2.772,
     'L1_attn_Wq': 2.836,
     'L1_ffn_gate_w': 7.098,
     'L1_ffn_w_gate': 6.2,
     'L1_ffn_w_up': 6.172,
     'L1_ffn_w_down': 6.139,
     'L1_ffn_shgate_w': 8.0,
     'L1_ffn_shw_gate': 5.917,
     'L1_ffn_shw_up': 5.843,
     'L1_ffn_shw_down': 5.832}
    for name, (base, spread) in spreads.items():
        noise = np.random.default_rng([zlib.crc32(name.encode()), seed]).standard_normal(out[name].shape)
        drawn = base * np.exp(spread * noise) if base else spread * noise
        out[name] = jnp.asarray(drawn.astype(out[name].dtype))
    for name, factor in factors.items():
        out[name] = (out[name] * factor).astype(out[name].dtype)
    return out
```

```python
from contextlib import ExitStack

import concourse.bass as bass
from concourse import mybir

F32 = mybir.dt.float32
BF16 = mybir.dt.bfloat16
U32 = mybir.dt.uint32
I32 = mybir.dt.int32
ACT = mybir.ActivationFunctionType
ALU = mybir.AluOpType
X = mybir.AxisListType.X

P = 128
D = 256
KD = D // P
NB = 4
S = 512
NT = NB * S // P
TB = S // P
EPS = 1e-5

E0, TOP0, I0 = 12, 3, 640
NI = I0 // P

HEADS, DH = 16, 16
KEYS = 4096
NKT = KEYS // P
HG = 4
NG = HEADS // HG
PARTS = 3
SIDE = 6
ROWS = SIDE * DH + PARTS
Q_PART = [0, 1, 2, 0, 1, 0]
K_PART = [0, 0, 0, 1, 1, 2]
VC = DH + 1

E1, TOP1, H1, HS1 = 8, 2, 176, 352
W1C = E1 * H1 + HS1
NSL = W1C // HS1
ND = -(-W1C // P)
DR = W1C - (ND - 1) * P


def build(nc, a, out):
    ctx = ExitStack()
    with ctx:
        def sb(name, shape, dt=F32, stack=ctx):
            return stack.enter_context(nc.sbuf_tensor(name, shape, dt))

        def sem(name):
            return ctx.enter_context(nc.semaphore(name))

        ps = ctx.enter_context(nc.psum_tensor("banks", [P, 8, 512], F32))
        kparts = nc.dram_tensor("key_parts", [PARTS, D, KEYS], BF16, kind="Internal").ap()
        qparts = nc.dram_tensor("query_parts", [PARTS, D, NB * S], BF16, kind="Internal").ap()

        x = sb("x", [P, NT, D])
        ident = sb("ident", [P, P])
        xn = sb("xn", [P, TB, D])
        xnT = sb("xnT", [P, KD, S])
        stats = sb("stats", [P, TB, 6])
        meanvar = sb("meanvar", [P, TB, 2])
        vareps = sb("vareps", [P, TB])
        stdev = sb("stdev", [P, TB])
        rstd = sb("rstd", [P, TB])
        iota_i = sb("iota_i", [P, E0], I32)
        iota = sb("iota", [P, E0])
        z = sb("z", [P, TB, E0])
        ez = sb("ez", [P, TB, E0])
        zmax = sb("zmax", [P, TB])
        zsum = sb("zsum", [P, TB])
        zrec = sb("zrec", [P, TB])
        probs = sb("probs", [P, TB, E0])
        top = sb("top", [P, TB, 8])
        topi = sb("topi", [P, TB, 8], U32)
        topf = sb("topf", [P, TB, 8])
        dtop = sb("dtop", [P, TB, TOP0])
        etop = sb("etop", [P, TB, TOP0])
        tsum = sb("tsum", [P, TB])
        trec = sb("trec", [P, TB])
        wtop = sb("wtop", [P, TB, TOP0])
        hit = sb("hit", [P, TOP0, TB, E0])
        whit = sb("whit", [P, TOP0, TB, E0])
        vaug = sb("vaug", [P, NKT, HEADS, VC])
        wot = sb("wot", [P, KD, D])
        wqt = sb("wqt", [P, KD, D])

        x_loaded, setup_done, load_w = sem("x_loaded"), sem("setup_done"), sem("load_w")
        ln_stats, ln_aggr, ln_var, ln_sd, ln_rstd, ln_xn, ln_T, ln_xnT = map(
            sem, "ln_stats ln_aggr ln_var ln_sd ln_rstd ln_xn ln_T ln_xnT".split())
        mmA, mmB, mmC, mmD, mmE, mmF, mmG = map(sem, "qkv_mm score_mm pT_mm attn_mm proj_mm gate_mm spare_mm".split())
        evA, evB, evC, evD, evE, evF = map(sem, "q_sb k_sb v_sb pT_sb attn_sb pT_sb2".split())
        step, amax, nbias_ready, p_ready, rs_ready, x_upd, z_ready, ez_ready = map(
            sem, "dve_step row_max nbias_ready p_ready rsum_ready x_updated z_ready ez_ready".split())
        dma_in, dma_out, dma_in2, split_done, v_done = map(sem, "dma_in dma_out dma_in2 split_done v_done".split())
        local = [ln_stats, ln_aggr, ln_var, ln_sd, ln_rstd, ln_xn, ln_T, ln_xnT, mmA, mmB, mmC, mmD, mmE,
                 mmF, mmG, evA, evB, evC, evD, evE, evF, step, amax, nbias_ready, p_ready, rs_ready, x_upd,
                 z_ready, ez_ready, dma_in, dma_out, dma_in2, split_done, v_done]

        def clear_local():
            with nc.Block() as block:
                @block.gpsimd
                def _(pool):
                    for s in local:
                        pool.sem_clear(s)

        class Chain:
            def __init__(self, dve):
                self.dve, self.n = dve, 0

            def __call__(self, ins):
                ins.then_inc(step, 1)
                self.n += 1

            def wait(self):
                self.dve.wait_ge(step, self.n)

        def norm_vector(dve, n, rows, transposed_before=True):
            for t in range(TB):
                nc.vector.bn_stats(stats[:, t, :], rows(t)).then_inc(ln_stats, 1)
            dve.wait_ge(ln_stats, TB * (n + 1))
            for t in range(TB):
                nc.vector.bn_aggr(meanvar[:, t, :], stats[:, t, :]).then_inc(ln_aggr, 1)
            dve.wait_ge(ln_aggr, TB * (n + 1))
            nc.vector.tensor_scalar(vareps[:], meanvar[:, :, 1], EPS, None, ALU.add).then_inc(ln_var, 1)
            dve.wait_ge(ln_sd, n + 1)
            nc.vector.reciprocal(rstd[:], stdev[:]).then_inc(ln_rstd, 1)
            dve.wait_ge(ln_rstd, n + 1)
            if n:
                dve.wait_ge(ln_T, n)
            for t in range(TB):
                nc.vector.tensor_scalar(xn[:, t, :], rows(t), meanvar[:, t, 0:1], rstd[:, t:t + 1],
                                        ALU.subtract, ALU.mult).then_inc(ln_xn, 1)

        def norm_scalar(act, n):
            act.wait_ge(ln_var, n + 1)
            nc.scalar.activation(stdev[:], vareps[:], ACT.Sqrt).then_inc(ln_sd, 1)
            act.wait_ge(ln_T, n + 1)
            for k in range(KD):
                nc.scalar.copy(xnT[:, k, :], ps[:, k, :]).then_inc(ln_xnT, 1)

        def norm_tensor(pe, n):
            for t in range(TB):
                pe.wait_ge(ln_xn, TB * n + t + 1)
                for k in range(KD):
                    last = nc.tensor.transpose(ps[:, k, t * P:(t + 1) * P], xn[:, t, k * P:(k + 1) * P], ident[:])
            last.then_inc(ln_T, 1)
            pe.wait_ge(ln_xnT, KD * (n + 1))

        def choose(dve, ch, logits, ne, ntop, bias=None):
            if bias is not None:
                ch(nc.vector.tensor_tensor(z[:, :, 0:ne], logits, bias.unsqueeze(1).to_broadcast([P, TB, ne]), ALU.add))
            else:
                ch(nc.vector.tensor_copy(z[:, :, 0:ne], logits))
            ch.wait()
            ch(nc.vector.tensor_reduce(zmax[:], z[:, :, 0:ne], X, ALU.max))
            ch.wait()
            nc.vector.tensor_tensor(z[:, :, 0:ne], z[:, :, 0:ne], zmax[:].unsqueeze(2).to_broadcast([P, TB, ne]),
                                    ALU.subtract).then_inc(z_ready, 1)
            dve.wait_ge(ez_ready, 1)
            ch(nc.vector.tensor_reduce(zsum[:], ez[:, :, 0:ne], X, ALU.add))
            ch.wait()
            ch(nc.vector.reciprocal(zrec[:], zsum[:]))
            ch.wait()
            ch(nc.vector.tensor_tensor(probs[:, :, 0:ne], ez[:, :, 0:ne],
                                       zrec[:].unsqueeze(2).to_broadcast([P, TB, ne]), ALU.mult))
            ch.wait()
            for i in range(TB):
                ch(nc.vector.max(top[:, i, :], probs[:, i, 0:ne]))
            ch.wait()
            for i in range(TB):
                ch(nc.vector.max_index(topi[:, i, :], top[:, i, :], probs[:, i, 0:ne]))
            ch.wait()
            ch(nc.vector.tensor_copy(topf[:], topi[:]))
            ch.wait()
            for k in range(ntop):
                ch(nc.vector.tensor_tensor(hit[:, k, :, 0:ne], iota[:, 0:ne].unsqueeze(1).to_broadcast([P, TB, ne]),
                                           topf[:, :, k:k + 1].to_broadcast([P, TB, ne]), ALU.is_equal))

        with ExitStack() as l0:
            def s0(name, shape, dt=F32):
                return sb(name, shape, dt, l0)

            ones = s0("ones", [P, P])
            wq, wk, wv, wo = (s0(n, [P, KD, D]) for n in ("wq", "wk", "wv", "wo"))
            wr = s0("wr", [P, KD, E0])
            br = s0("br", [P, E0])
            b1 = s0("b1", [P, E0 * NI])
            b2 = s0("b2", [E0, D])
            wp1 = s0("wp1", [P, KD, P])
            bp1 = s0("bp1", [P, 1])
            wp2 = s0("wp2", [P, 1])
            bp2 = s0("bp2", [P, 1])
            xnT_all = s0("xnT_all", [P, KD, NB * S])
            chosen = s0("chosen", [P, NT, 2 * E0])
            w1 = [s0(f"w1_{i}", [P, KD, I0]) for i in range(2)]
            w2 = [s0(f"w2_{i}", [P, NI, D]) for i in range(2)]

            def load_expert(sp, i, e, done):
                sp.dma_start(w1[i][:], a["L0_ffn_w1"][e].rearrange("(k p) i -> p k i", p=P)).then_inc(done, 16)
                sp.dma_start(w2[i][:], a["L0_ffn_w2"][e].rearrange("(k p) i -> p k i", p=P)).then_inc(done, 16)

            with nc.Block() as block:
                @block.sync
                def _(sp):
                    sp.dma_start(x[:], a["x"].rearrange("(t p) d -> p t d", p=P)).then_inc(x_loaded, 16)
                    for w, n in ((wq, "L0_attn_W_q"), (wk, "L0_attn_W_k"), (wv, "L0_attn_W_v"), (wo, "L0_attn_W_o"),
                                 (wr, "L0_ffn_Wr"), (wp1, "L0_ffn_Wp1"), (wqt, "wqT"), (wot, "woT")):
                        sp.dma_start(w[:], a[n].rearrange("(k p) e -> p k e", p=P)).then_inc(load_w, 16)
                    sp.dma_start(b1[:], a["b1T"]).then_inc(load_w, 16)
                    sp.dma_start(b2[:], a["L0_ffn_b2"]).then_inc(load_w, 16)
                    sp.dma_start(br[:], a["L0_ffn_br"].partition_broadcast(P)).then_inc(load_w, 16)
                    sp.dma_start(bp1[:], a["L0_ffn_bp1"].rearrange("(p o) -> p o", o=1)).then_inc(load_w, 16)
                    sp.dma_start(wp2[:], a["L0_ffn_Wp2"]).then_inc(load_w, 16)
                    sp.dma_start(bp2[:], a["L0_ffn_bp2"].partition_broadcast(P)).then_inc(load_w, 16)
                    load_expert(sp, 0, 0, load_w)
                    sp.wait_ge(x_loaded, 16)
                    sp.wait_ge(load_w, 16 * 16)

                @block.gpsimd
                def _(pool):
                    nc.gpsimd.memset(ident[:], 0.0).then_inc(setup_done, 1)
                    pool.wait_ge(setup_done, 1)
                    nc.gpsimd.affine_select(out=ident[:], in_=ident[:], compare_op=ALU.not_equal, fill=1.0, base=0,
                                            pattern=[[-1, P]], channel_multiplier=1).then_inc(setup_done, 1)
                    nc.gpsimd.iota(iota_i[:], pattern=[[1, E0]], base=0, channel_multiplier=0).then_inc(setup_done, 1)
                    nc.gpsimd.memset(vaug[:], 1.0).then_inc(setup_done, 1)

                @block.vector
                def _(dve):
                    nc.vector.memset(ones[:], 1.0)
                    dve.wait_ge(setup_done, 3)
                    nc.vector.tensor_copy(iota[:], iota_i[:])

            with ExitStack() as at:
                qT, kT, oT = (sb(n, [P, KD, S], F32, at) for n in ("qT", "kT", "oT"))
                v = sb("v", [P, TB, D], F32, at)
                pm = sb("pm", [P, TB, S], F32, at)
                pT = sb("pT", [P, TB, S], F32, at)
                rmax, nbias, rsum, rrec = (sb(n, [P, TB], F32, at) for n in ("rmax", "nbias", "rsum", "rrec"))
                NPC = KEYS // NB
                kf = sb("kf", [P, KD, NPC], F32, at)
                ksp = sb("ksp", [P, PARTS, KD, NPC], BF16, at)
                VT = NKT // NB
                vst = sb("vst", [P, VT, D], F32, at)
                scale = float(D) ** -0.5

                with nc.Fori(0, NB) as b:
                    rows = lambda t: x[:, bass.ds(TB * b + t, 1), :].rearrange("p o d -> p (o d)")
                    with nc.Block() as block:
                        @block.sync
                        def _(sp):
                            sp.dma_start(kf[:], a["kT"].rearrange("(k p) c -> p k c", p=P)[:, :, bass.ds(b * NPC, NPC)]
                                         ).then_inc(dma_in, 16)
                            sp.dma_start(vst[:], a["v"].rearrange("(t p) d -> p t d", p=P)[:, bass.ds(b * VT, VT), :]
                                         ).then_inc(dma_in2, 16)
                            sp.wait_ge(split_done, 5)
                            for s in range(PARTS):
                                sp.dma_start(kparts[s].rearrange("(k p) c -> p k c", p=P)[:, :, bass.ds(b * NPC, NPC)],
                                             ksp[:, s]).then_inc(dma_out, 16)
                            sp.wait_ge(dma_out, 16 * PARTS)

                        @block.gpsimd
                        def _(pool):
                            pool.wait_ge(dma_in, 16)
                            for s in range(PARTS):
                                nc.gpsimd.tensor_copy(ksp[:, s], kf[:]).then_inc(split_done, 1)
                                if s < PARTS - 1:
                                    pool.wait_ge(split_done, 2 * s + 1)
                                    nc.gpsimd.tensor_tensor(kf[:], kf[:], ksp[:, s], ALU.subtract).then_inc(split_done, 1)
                                    pool.wait_ge(split_done, 2 * s + 2)
                            pool.wait_ge(dma_in2, 16)
                            for h2 in range(2):
                                nc.gpsimd.tensor_copy(
                                    vaug[:, bass.ds(b * VT + h2 * (VT // 2), VT // 2), :, 0:DH],
                                    vst[:, h2 * (VT // 2):(h2 + 1) * (VT // 2), :].rearrange("p t (h d) -> p t h d", h=HEADS)
                                ).then_inc(v_done, 1)

                        @block.tensor
                        def _(pe):
                            norm_tensor(pe, 0)
                            for m in range(KD):
                                for k in range(KD):
                                    mm = nc.tensor.matmul(ps[:, 2 + m, :], wq[:, k, m * P:(m + 1) * P], xnT[:, k, :],
                                                          start=(k == 0), stop=(k == KD - 1))
                                mm.then_inc(mmA, 1)
                            for m in range(KD):
                                for k in range(KD):
                                    mm = nc.tensor.matmul(ps[:, 4 + m, :], wk[:, k, m * P:(m + 1) * P], xnT[:, k, :],
                                                          start=(k == 0), stop=(k == KD - 1))
                                mm.then_inc(mmA, 1)
                            for i in range(TB):
                                for k in range(KD):
                                    mm = nc.tensor.matmul(ps[:, 6 + i // 2, (i % 2) * D:(i % 2 + 1) * D],
                                                          xnT[:, k, i * P:(i + 1) * P], wv[:, k, :],
                                                          start=(k == 0), stop=(k == KD - 1))
                                if i % 2:
                                    mm.then_inc(mmA, 1)
                            pe.wait_ge(evA, KD)
                            pe.wait_ge(evB, KD)
                            for i in range(TB):
                                for m in range(KD):
                                    mm = nc.tensor.matmul(ps[:, i, :], qT[:, m, i * P:(i + 1) * P], kT[:, m, :],
                                                          start=(m == 0), stop=(m == KD - 1))
                                mm.then_inc(mmB, 1)
                            pe.wait_ge(evC, 2)
                            pe.wait_ge(p_ready, TB)
                            for kb in range(TB):
                                for i in range(TB):
                                    mm = nc.tensor.transpose(ps[:, 4 + kb, i * P:(i + 1) * P],
                                                             pm[:, i, kb * P:(kb + 1) * P], ident[:])
                                mm.then_inc(mmC, 1)
                            pe.wait_ge(evD, 2)
                            pe.wait_ge(evF, 2)
                            for m in range(KD):
                                for kb in range(TB):
                                    mm = nc.tensor.matmul(ps[:, m, :], v[:, kb, m * P:(m + 1) * P], pT[:, kb, :],
                                                          start=(kb == 0), stop=(kb == TB - 1))
                                mm.then_inc(mmD, 1)
                            pe.wait_ge(evE, KD)
                            for i in range(TB):
                                for m in range(KD):
                                    mm = nc.tensor.matmul(ps[:, 2 + i // 2, (i % 2) * D:(i % 2 + 1) * D],
                                                          oT[:, m, i * P:(i + 1) * P], wo[:, m, :],
                                                          start=(m == 0), stop=(m == KD - 1))
                                if i % 2:
                                    mm.then_inc(mmE, 1)
                            norm_tensor(pe, 1)
                            for i in range(TB):
                                for k in range(KD):
                                    mm = nc.tensor.matmul(ps[:, 4, i * E0:(i + 1) * E0], xnT[:, k, i * P:(i + 1) * P],
                                                          wr[:, k, :], start=(k == 0), stop=(k == KD - 1))
                            mm.then_inc(mmF, 1)

                        @block.scalar
                        def _(act):
                            norm_scalar(act, 0)
                            for m in range(KD):
                                act.wait_ge(mmA, m + 1)
                                nc.scalar.copy(qT[:, m, :], ps[:, 2 + m, :]).then_inc(evA, 1)
                            for j in range(2):
                                act.wait_ge(mmA, 5 + j)
                                nc.scalar.copy(v[:, 2 * j:2 * j + 2, :], ps[:, 6 + j, :]).then_inc(evC, 1)
                            act.wait_ge(nbias_ready, 1)
                            for i in range(TB):
                                nc.scalar.activation(pm[:, i, :], ps[:, i, :], ACT.Exp, bias=nbias[:, i:i + 1],
                                                     scale=scale, accum_out=rsum[:, i:i + 1]).then_inc(p_ready, 1)
                            for kb in range(2, 4):
                                act.wait_ge(mmC, kb + 1)
                                nc.scalar.copy(pT[:, kb, :], ps[:, 4 + kb, :]).then_inc(evF, 1)
                            for m in range(KD):
                                act.wait_ge(mmD, m + 1)
                                nc.scalar.copy(oT[:, m, :], ps[:, m, :]).then_inc(evE, 1)
                            norm_scalar(act, 1)
                            act.wait_ge(z_ready, 1)
                            nc.scalar.activation(ez[:], z[:], ACT.Exp).then_inc(ez_ready, 1)
                            act.wait_ge(z_ready, 2)
                            nc.scalar.activation(etop[:], dtop[:], ACT.Exp).then_inc(ez_ready, 1)

                        @block.vector
                        def _(dve):
                            ch = Chain(dve)
                            norm_vector(dve, 0, rows)
                            for m in range(KD):
                                dve.wait_ge(mmA, 3 + m)
                                nc.vector.tensor_copy(kT[:, m, :], ps[:, 4 + m, :]).then_inc(evB, 1)
                            dve.wait_ge(mmB, TB)
                            nc.vector.tensor_reduce(rmax[:], ps[:, 0:TB, :], X, ALU.max).then_inc(amax, 1)
                            dve.wait_ge(amax, 1)
                            nc.vector.tensor_scalar(nbias[:], rmax[:], -scale, None, ALU.mult).then_inc(nbias_ready, 1)
                            for kb in range(2):
                                dve.wait_ge(mmC, kb + 1)
                                nc.vector.tensor_copy(pT[:, kb, :], ps[:, 4 + kb, :]).then_inc(evD, 1)
                            dve.wait_ge(p_ready, TB)
                            nc.vector.reciprocal(rrec[:], rsum[:]).then_inc(rs_ready, 1)
                            dve.wait_ge(rs_ready, 1)
                            for i in range(TB):
                                dve.wait_ge(mmE, i // 2 + 1)
                                nc.vector.scalar_tensor_tensor(out=rows(i), in0=ps[:, 2 + i // 2, (i % 2) * D:(i % 2 + 1) * D],
                                                               scalar=rrec[:, i:i + 1], in1=rows(i),
                                                               op0=ALU.mult, op1=ALU.add).then_inc(x_upd, 1)
                            dve.wait_ge(x_upd, TB)
                            norm_vector(dve, 1, rows)
                            dve.wait_ge(ln_xnT, 2 * KD)
                            ch(nc.vector.tensor_copy(xnT_all[:, :, bass.ds(b * S, S)], xnT[:]))
                            dve.wait_ge(mmF, 1)
                            choose(dve, ch, ps[:, 4, 0:TB * E0].rearrange("p (i e) -> p i e", e=E0), E0, TOP0, br[:])
                            nc.vector.tensor_tensor(dtop[:], top[:, :, 0:TOP0], top[:, :, 0:1].to_broadcast([P, TB, TOP0]),
                                                    ALU.subtract).then_inc(z_ready, 1)
                            dve.wait_ge(ez_ready, 2)
                            ch(nc.vector.tensor_reduce(tsum[:], etop[:], X, ALU.add))
                            ch.wait()
                            ch(nc.vector.reciprocal(trec[:], tsum[:]))
                            ch.wait()
                            ch(nc.vector.tensor_tensor(wtop[:], etop[:], trec[:].unsqueeze(2).to_broadcast([P, TB, TOP0]), ALU.mult))
                            ch.wait()
                            for k in range(TOP0):
                                ch(nc.vector.tensor_tensor(whit[:, k], hit[:, k], wtop[:, :, k:k + 1].to_broadcast([P, TB, E0]), ALU.mult))
                            ch.wait()
                            cur = bass.ds(TB * b, TB)
                            for c0, src in ((0, whit), (E0, hit)):
                                ch(nc.vector.tensor_tensor(src[:, 0], src[:, 0], src[:, 1], ALU.add))
                                ch.wait()
                                ch(nc.vector.tensor_tensor(chosen[:, cur, c0:c0 + E0], src[:, 0], src[:, 2], ALU.add))
                    clear_local()

            with ExitStack() as ex:
                hT = [sb(f"hT{i}", [P, NI, S], F32, ex) for i in range(2)]
                acc = sb("acc", [P, NT, D], F32, ex)
                cw = sb("cw", [P, NT, E0], F32, ex)
                cwT = sb("cwT", [E0, NB * S], F32, ex)
                cnt = sb("cnt", [P, E0], F32, ex)
                crec = sb("crec", [P, E0], F32, ex)
                we = sb("we", [P, E0], F32, ex)

                with nc.Block() as block:
                    @block.tensor
                    def _(pe):
                        for t in range(NT):
                            mm = nc.tensor.matmul(ps[:, 0, 0:2 * E0], ones[:], chosen[:, t, :], start=(t == 0), stop=(t == NT - 1))
                        mm.then_inc(mmA, 1)
                        pe.wait_ge(x_upd, 1)
                        for t in range(NT):
                            mm = nc.tensor.transpose(ps[0:E0, 1 + t // 4, (t % 4) * P:(t % 4 + 1) * P], cw[:, t, :], ident[:])
                            if t % 4 == 3:
                                mm.then_inc(mmB, 1)
                        pe.wait_ge(evA, 4)
                        for t in range(NT):
                            mm = nc.tensor.matmul(ps[:, t // 2, (t % 2) * D:(t % 2 + 1) * D], cwT[:, t * P:(t + 1) * P], b2[:],
                                                  start=True, stop=True)
                            if t % 2:
                                mm.then_inc(mmC, 1)

                    @block.vector
                    def _(dve):
                        ch = Chain(dve)
                        dve.wait_ge(mmA, 1)
                        ch(nc.vector.tensor_scalar(cnt[:], ps[:, 0, E0:2 * E0], 1.0, None, ALU.max))
                        ch.wait()
                        ch(nc.vector.reciprocal(crec[:], cnt[:]))
                        ch.wait()
                        ch(nc.vector.tensor_tensor(we[:], crec[:], ps[:, 0, 0:E0], ALU.mult))
                        ch.wait()
                        nc.vector.tensor_tensor(cw[:], chosen[:, :, E0:2 * E0], we[:].unsqueeze(1).to_broadcast([P, NT, E0]),
                                                ALU.mult).then_inc(x_upd, 1)
                        for j in range(0, NT // 2, 2):
                            dve.wait_ge(mmC, j + 1)
                            nc.vector.tensor_copy(acc[:, 2 * j:2 * j + 2, :], ps[:, j, :])

                    @block.scalar
                    def _(act):
                        for c in range(4):
                            act.wait_ge(mmB, c + 1)
                            nc.scalar.copy(cwT[:, c * S:(c + 1) * S], ps[0:E0, 1 + c, :]).then_inc(evA, 1)
                        for j in range(1, NT // 2, 2):
                            act.wait_ge(mmC, j + 1)
                            nc.scalar.copy(acc[:, 2 * j:2 * j + 2, :], ps[:, j, :])
                clear_local()

                STEPS = 2 * NB

                def expert_pair(e0, more):
                    with nc.Block() as block:
                        @block.sync
                        def _(sp):
                            load_expert(sp, 1, e0 + 1, dma_in)
                            if more:
                                sp.wait_ge(mmB, 2 * NB)
                                load_expert(sp, 0, e0 + 2, dma_in2)
                                sp.wait_ge(dma_in2, 32)

                        @block.tensor
                        def _(pe):
                            def hidden(s):
                                q, c = divmod(s, NB)
                                if s == NB:
                                    pe.wait_ge(dma_in, 32)
                                for i in range(NI):
                                    n = NI * s + i
                                    if n >= 4:
                                        pe.wait_ge(evA, n - 3)
                                    for k in range(KD):
                                        mm = nc.tensor.matmul(ps[:, n % 4, :], w1[q][:, k, i * P:(i + 1) * P],
                                                              xnT_all[:, k, c * S:(c + 1) * S],
                                                              start=(k == 0), stop=(k == KD - 1))
                                    mm.then_inc(mmA, 1)

                            def output(s):
                                q = s // NB
                                pe.wait_ge(evA, NI * (s + 1))
                                for t in range(TB):
                                    u = 2 * s + t // 2
                                    if u >= 4 and t % 2 == 0:
                                        pe.wait_ge(x_upd, 2 * (u - 3))
                                    for i in range(NI):
                                        mm = nc.tensor.matmul(ps[:, 4 + u % 4, (t % 2) * D:(t % 2 + 1) * D],
                                                              hT[s % 2][:, i, t * P:(t + 1) * P], w2[q][:, i, :],
                                                              start=(i == 0), stop=(i == NI - 1))
                                    if t % 2:
                                        mm.then_inc(mmB, 1)

                            hidden(0)
                            for s in range(STEPS):
                                if s + 1 < STEPS:
                                    hidden(s + 1)
                                output(s)

                        @block.scalar
                        def _(act):
                            for s in range(STEPS):
                                if s >= 2:
                                    act.wait_ge(mmB, 2 * (s - 1))
                                for i in range(NI):
                                    n = NI * s + i
                                    act.wait_ge(mmA, n + 1)
                                    bias = b1[:, bass.ds((e0 + s // NB) * NI + i, 1)]
                                    nc.scalar.activation(hT[s % 2][:, i, :], ps[:, n % 4, :], ACT.Relu,
                                                         bias=bias).then_inc(evA, 1)

                        @block.vector
                        def _(dve):
                            for s in range(STEPS):
                                q, c = divmod(s, NB)
                                for t in range(TB):
                                    n = TB * s + t
                                    u = 2 * s + t // 2
                                    dve.wait_ge(mmB, u + 1)
                                    if n >= NT:
                                        dve.wait_ge(x_upd, n - NT + 1)
                                    tile = TB * c + t
                                    nc.vector.scalar_tensor_tensor(
                                        out=acc[:, tile, :], in0=ps[:, 4 + u % 4, (t % 2) * D:(t % 2 + 1) * D],
                                        scalar=cw[:, tile, bass.ds(e0 + q, 1)], in1=acc[:, tile, :],
                                        op0=ALU.mult, op1=ALU.add).then_inc(x_upd, 1)
                    clear_local()

                with nc.Fori(0, E0 - 2, 2) as e0:
                    expert_pair(e0, True)
                expert_pair(E0 - 2, False)

                pooled = sb("pooled", [P, KD * NB], F32, ex)
                hp = sb("hp", [P, NB], F32, ex)
                gp = sb("gp", [P, NB], F32, ex)
                ephi = sb("ephi", [P, NB], F32, ex)
                phi = sb("phi", [P, NB], F32, ex)
                fac = sb("fac", [P, NB], F32, ex)
                with nc.Block() as block:
                    @block.tensor
                    def _(pe):
                        for m in range(KD):
                            for b in range(NB):
                                for i in range(TB):
                                    mm = nc.tensor.matmul(ps[:, 0, m * NB + b:m * NB + b + 1], acc[:, TB * b + i, m * P:(m + 1) * P],
                                                          ones[:, 0:1], start=(i == 0), stop=(i == TB - 1))
                        mm.then_inc(mmA, 1)
                        pe.wait_ge(step, 1)
                        for m in range(KD):
                            mm = nc.tensor.matmul(ps[:, 1, 0:NB], wp1[:, m, :], pooled[:, m * NB:(m + 1) * NB],
                                                  start=(m == 0), stop=(m == KD - 1))
                        mm.then_inc(mmA, 1)
                        pe.wait_ge(step, 3)
                        nc.tensor.matmul(ps[:, 2, 0:NB], ones[:], gp[:], start=True, stop=True).then_inc(mmA, 1)

                    @block.scalar
                    def _(act):
                        act.wait_ge(step, 4)
                        nc.scalar.activation(ephi[:], phi[:], ACT.Exp, scale=-1.0).then_inc(evA, 1)

                    @block.vector
                    def _(dve):
                        ch = Chain(dve)
                        dve.wait_ge(mmA, 1)
                        ch(nc.vector.tensor_scalar(pooled[:], ps[:, 0, 0:KD * NB], 1.0 / S, None, ALU.mult))
                        dve.wait_ge(mmA, 2)
                        ch(nc.vector.tensor_scalar(hp[:], ps[:, 1, 0:NB], bp1[:, 0:1], 0.0, ALU.add, ALU.max))
                        ch.wait()
                        ch(nc.vector.tensor_scalar(gp[:], hp[:], wp2[:, 0:1], None, ALU.mult))
                        dve.wait_ge(mmA, 3)
                        ch(nc.vector.tensor_scalar(phi[:], ps[:, 2, 0:NB], bp2[:, 0:1], None, ALU.add))
                        dve.wait_ge(evA, 1)
                        ch(nc.vector.tensor_scalar(ephi[:], ephi[:], 1.0, None, ALU.add))
                        ch.wait()
                        ch(nc.vector.reciprocal(phi[:], ephi[:]))
                        ch.wait()
                        ch(nc.vector.tensor_scalar(fac[:], phi[:], 0.7, -0.8, ALU.is_gt, ALU.mult))
                        ch.wait()
                        ch(nc.vector.tensor_scalar(fac[:], fac[:], 1.0, None, ALU.add))
                        ch.wait()
                        for t in range(NT):
                            nc.vector.scalar_tensor_tensor(out=x[:, t, :], in0=acc[:, t, :], scalar=fac[:, t // TB:t // TB + 1],
                                                           in1=x[:, t, :], op0=ALU.mult, op1=ALU.add)
                clear_local()

        with ExitStack() as l1:
            attn = sb("attn", [P, NT, D], F32, l1)
            kst = [sb(f"kst{i}", [ROWS, HG, KEYS], BF16, l1) for i in range(2)]
            qst = [sb(f"qst{i}", [ROWS, HG, S], BF16, l1) for i in range(NB)]
            pring = sb("pring", [P, 2 * HG, S], F32, l1)
            osb = sb("osb", [P, S], F32, l1)
            orec = sb("orec", [P, TB, HG], F32, l1)
            maxp = sb("maxp", [P, HG, TB, KEYS // 512], F32, l1)
            mneg = sb("mneg", [P, HG * TB], F32, l1)
            mres = sb("mres", [HG * TB, P], F32, l1)
            mrow = sb("mrow", [HG * TB, PARTS, P], BF16, l1)
            q_loaded = [sem(f"q_loaded{i}") for i in range(NB)]
            local.extend(q_loaded)

            def load_keys(sp, i, g, done):
                for s in range(SIDE):
                    src = kparts[K_PART[s]].rearrange("(h r) c -> r h c", r=DH)[:, bass.ds(g * HG, HG), :]
                    sp.dma_start(kst[i][s * DH:(s + 1) * DH], src).then_inc(done, 16)

            def load_queries(sp, i, g, done):
                for s in range(SIDE):
                    src = qparts[Q_PART[s]].rearrange("(h r) c -> r h c", r=DH)[:, bass.ds(g * HG, HG), i * S:(i + 1) * S]
                    sp.dma_start(qst[i][s * DH:(s + 1) * DH], src).then_inc(done, 16)

            def load_maxima(sp, i):
                for s in range(PARTS):
                    sp.dma_start(qst[i][SIDE * DH + s:SIDE * DH + s + 1].rearrange("o h s -> o (h s)"),
                                 mrow[:, s, :]).then_inc(dma_out, 16)

            qres = sb("qres", [P, KD, S], F32, l1)
            qsp = sb("qsp", [P, PARTS, KD, S], BF16, l1)
            with nc.Fori(0, NB) as b:
                rows = lambda t: x[:, bass.ds(TB * b + t, 1), :].rearrange("p o d -> p (o d)")
                with nc.Block() as block:
                    @block.tensor
                    def _(pe):
                        norm_tensor(pe, 0)
                        for m in range(KD):
                            for k in range(KD):
                                mm = nc.tensor.matmul(ps[:, 2 + m, :], wqt[:, k, m * P:(m + 1) * P], xnT[:, k, :],
                                                      start=(k == 0), stop=(k == KD - 1))
                        mm.then_inc(mmA, 1)

                    @block.scalar
                    def _(act):
                        norm_scalar(act, 0)

                    @block.vector
                    def _(dve):
                        ch = Chain(dve)
                        norm_vector(dve, 0, rows)
                        dve.wait_ge(mmA, 1)
                        src = ps[:, 2:2 + KD, :]
                        for s in range(PARTS):
                            ch(nc.vector.tensor_copy(qsp[:, s], src))
                            ch.wait()
                            if s < PARTS - 1:
                                ch(nc.vector.tensor_tensor(qres[:], src, qsp[:, s], ALU.subtract))
                                ch.wait()
                                src = qres[:]

                    @block.sync
                    def _(sp):
                        sp.wait_ge(step, 2 * PARTS - 1)
                        for s in range(PARTS):
                            sp.dma_start(qparts[s].rearrange("(k p) c -> p k c", p=P)[:, :, bass.ds(b * S, S)],
                                         qsp[:, s]).then_inc(dma_out, 16)
                        sp.wait_ge(dma_out, 16 * PARTS)
                clear_local()

            NU = TB * (KEYS // 512) * (HG // 2)
            SOON = NKT - 4

            def schedule(its, maxes):
                plan = []
                for n, i in enumerate(its):
                    nxt = maxes[n]
                    done = 0
                    for kt in range(NKT):
                        ev = []
                        if n and kt == 2:
                            ev.append(("turn_out", its[n - 1], 0))
                        if nxt is not None:
                            upto = min(NU, -(-NU * (kt + 1) // SOON))
                            ev += [("max", nxt, u) for u in range(done, upto)]
                            done = upto
                            if kt == NKT - 2:
                                ev.append(("turn_max", nxt, 0))
                        plan.append(ev)
                return plan

            def run_scores(g, last):
                its = list(range(NB))
                nexts = [(i + 1) % NB if (i + 1 < NB or not last) else None for i in its]
                plan = schedule(its, nexts)
                tail = [("turn_out", its[-1], 0)]
                key_buf = lambda i: 1 if i == 0 else 0
                nth = lambda i: nexts.index(i) + 1

                with nc.Block() as block:
                    @block.sync
                    def _(sp):
                        if not last:
                            sp.wait_ge(evF, 1)
                            load_keys(sp, 1, g + 1, dma_in)
                        for i in its:
                            if nexts[i] is not None:
                                sp.wait_ge(nbias_ready, i + 1)
                                load_maxima(sp, nexts[i])
                                sp.wait_ge(dma_out, 16 * PARTS * (i + 1))
                            if not last:
                                sp.wait_ge(mmB, NKT * HG * (i + 1))
                                load_queries(sp, i, g + 1, q_loaded[i])
                        if not last:
                            for i in its:
                                sp.wait_ge(q_loaded[i], 16 * SIDE)
                            sp.wait_ge(dma_in, 16 * SIDE)

                    @block.tensor
                    def _(pe):
                        units = 0

                        def scores(i, kt, j):
                            n = (i * NKT + kt) * HG + j
                            if n >= 3:
                                pe.wait_ge(p_ready, n - 2)
                            mm = nc.tensor.matmul(ps[:, n % 3, :], kst[0][:, j, kt * P:(kt + 1) * P], qst[i][:, j, :],
                                                  start=True, stop=True)
                            mm.then_inc(mmB, 1)
                            return mm

                        def values(i, kt):
                            G = i * NKT + kt
                            pe.wait_ge(p_ready, HG * (G + 1))
                            if kt == 0 and i:
                                pe.wait_ge(evA, i)
                            for j in range(HG):
                                mm = nc.tensor.matmul(ps[32 * j:32 * j + VC, 7, :], vcur[:, kt, j, :], pring[:, (G % 2) * HG + j, :],
                                                      start=(kt == 0), stop=(kt == NKT - 1))
                            mm.then_inc(mmC, 1)

                        def unit(kind, i, u):
                            nonlocal units
                            base = 3 + 2 * (units % 2)
                            if units >= 2:
                                pe.wait_ge(x_upd, units - 1)
                            if kind == "max":
                                if u == 0 and i == 0:
                                    pe.wait_ge(dma_in, 16 * SIDE)
                                    pe.wait_ge(q_loaded[0], 16 * SIDE)
                                qt, kb, hp2 = u // 16, (u % 16) // 2, u % 2
                                for jj in range(2):
                                    j = 2 * hp2 + jj
                                    mm = nc.tensor.matmul(ps[:, base + jj, :], qst[i][0:SIDE * DH, j, qt * P:(qt + 1) * P],
                                                          kst[key_buf(i)][0:SIDE * DH, j, kb * 512:(kb + 1) * 512],
                                                          start=True, stop=True)
                            elif kind == "turn_max":
                                pe.wait_ge(amax, nth(i))
                                mm = nc.tensor.transpose(ps[0:HG * TB, base, 0:P], mneg[:], ident[:])
                            else:
                                pe.wait_ge(evA, i + 1)
                                for t in range(TB):
                                    mm = nc.tensor.transpose(ps[:, base, t * P:(t + 1) * P], osb[:, t * P:(t + 1) * P], ident[:])
                            mm.then_inc(mmD, 1)
                            units += 1

                        pe.wait_ge(evE, 1)
                        pe.wait_ge(evF, 1)
                        for i in its:
                            if i:
                                pe.wait_ge(dma_out, 16 * PARTS * i)
                            for kt in range(NKT):
                                ev = plan[i * NKT + kt]
                                half = (len(ev) + 1) // 2
                                scores(i, kt, 0)
                                scores(i, kt, 1)
                                for e in ev[:half]:
                                    unit(*e)
                                scores(i, kt, 2)
                                mm = scores(i, kt, 3)
                                for e in ev[half:]:
                                    unit(*e)
                                if kt:
                                    values(i, kt - 1)
                                elif i:
                                    values(i - 1, NKT - 1)
                        values(NB - 1, NKT - 1)
                        unit(*tail[0])

                    @block.scalar
                    def _(act):
                        for n in range(NB * NKT * HG):
                            G = n // HG
                            act.wait_ge(mmB, n + 1)
                            if G >= 2 and n % HG == 0:
                                act.wait_ge(mmC, G - 1)
                            nc.scalar.activation(pring[:, n % (2 * HG), :], ps[:, n % 3, :], ACT.Exp,
                                                 scale=float(DH) ** -0.5).then_inc(p_ready, 1)

                    @block.vector
                    def _(dve):
                        ch = Chain(dve)
                        units = 0
                        nc.vector.tensor_copy(vcur[:], vaug[:, :, bass.ds(g * HG, HG), :]).then_inc(evE, 1)
                        nc.vector.tensor_copy(kst[0][:], kst[1][:]).then_inc(evF, 1)

                        def unit(kind, i, u):
                            nonlocal units
                            base = 3 + 2 * (units % 2)
                            dve.wait_ge(mmD, units + 1)
                            if kind == "max":
                                qt, kb, hp2 = u // 16, (u % 16) // 2, u % 2
                                nc.vector.tensor_reduce(maxp[:, 2 * hp2:2 * hp2 + 2, qt, kb], ps[:, base:base + 2, :], X,
                                                        ALU.max).then_inc(x_upd, 1)
                                if u == NU - 1:
                                    dve.wait_ge(x_upd, units + 1)
                                    nc.vector.tensor_reduce(mneg[:], maxp[:].rearrange("p h t k -> p (h t) k"), X, ALU.max,
                                                            negate=True).then_inc(amax, 1)
                            elif kind == "turn_max":
                                src = ps[0:HG * TB, base, 0:P]
                                if nth(i) > 1:
                                    dve.wait_ge(dma_out, 16 * PARTS * (nth(i) - 1))
                                for s in range(PARTS):
                                    last_part = nc.vector.tensor_copy(mrow[:, s, :], src)
                                    if s < PARTS - 1:
                                        ch(last_part)
                                        ch.wait()
                                        w = nc.vector.tensor_tensor(mres[:], src, mrow[:, s, :], ALU.subtract)
                                        if s == 0:
                                            w.then_inc(x_upd, 1)
                                            dve.wait_ge(x_upd, units + 1)
                                        else:
                                            ch(w)
                                            ch.wait()
                                        src = mres[:]
                                last_part.then_inc(nbias_ready, 1)
                            else:
                                view = ps[:, base, :].rearrange("p (t h c) -> p t h c", t=TB, h=HG)
                                ch(nc.vector.reciprocal(orec[:], view[:, :, :, DH]))
                                ch.wait()
                                dst = attn[:, TB * i:TB * (i + 1), bass.ds(g * HG * DH, HG * DH)].rearrange(
                                    "p t (h d) -> p t h d", h=HG)
                                for t in range(TB):
                                    w = nc.vector.tensor_tensor(dst[:, t], view[:, t, :, 0:DH],
                                                                orec[:, t, :].unsqueeze(2).to_broadcast([P, HG, DH]), ALU.mult)
                                w.then_inc(x_upd, 1)
                            units += 1

                        def take_sums(i):
                            dve.wait_ge(mmC, NKT * (i + 1))
                            if i:
                                dve.wait_ge(x_upd, out_units[i - 1] + 1)
                            nc.vector.tensor_copy(osb[:], ps[:, 7, :]).then_inc(evA, 1)

                        flat = [e for ev in plan for e in ev] + tail
                        out_units = {e[1]: n for n, e in enumerate(flat) if e[0] == "turn_out"}
                        for i in its:
                            for kt in range(NKT):
                                if i and kt == 1:
                                    take_sums(i - 1)
                                for e in plan[i * NKT + kt]:
                                    unit(*e)
                        take_sums(NB - 1)
                        unit(*tail[0])

            vcur = sb("vcur", [P, NKT, HG, VC], F32, l1)
            with nc.Block() as block:
                @block.sync
                def _(sp):
                    load_keys(sp, 1, 0, dma_in)
                    for i in range(NB):
                        load_queries(sp, i, 0, q_loaded[i])
                    sp.wait_ge(nbias_ready, 1)
                    load_maxima(sp, 0)
                    sp.wait_ge(dma_out, 16 * PARTS)
                    for i in range(NB):
                        sp.wait_ge(q_loaded[i], 16 * SIDE)

                @block.gpsimd
                def _(pool):
                    nc.gpsimd.memset(kst[1][SIDE * DH:ROWS], 1.0).then_inc(evD, 1)
                    pool.wait_ge(evD, 1)
                    nc.gpsimd.memset(osb[:], 0.0).then_inc(evB, 1)

                @block.tensor
                def _(pe):
                    pe.wait_ge(evB, 1)
                    nc.tensor.matmul(ps[:, 7, :], ident[:], osb[:], start=True, stop=True).then_inc(evC, 1)
                    pe.wait_ge(dma_in, 16 * SIDE)
                    pe.wait_ge(q_loaded[0], 16 * SIDE)
                    for u in range(NU):
                        base = 2 * (u % 3)
                        if u >= 3:
                            pe.wait_ge(x_upd, u - 2)
                        qt, kb, hp2 = u // 16, (u % 16) // 2, u % 2
                        for jj in range(2):
                            j = 2 * hp2 + jj
                            mm = nc.tensor.matmul(ps[:, base + jj, :], qst[0][0:SIDE * DH, j, qt * P:(qt + 1) * P],
                                                  kst[1][0:SIDE * DH, j, kb * 512:(kb + 1) * 512], start=True, stop=True)
                        mm.then_inc(mmD, 1)
                    pe.wait_ge(amax, 1)
                    nc.tensor.transpose(ps[0:HG * TB, 6, 0:P], mneg[:], ident[:]).then_inc(mmE, 1)

                @block.vector
                def _(dve):
                    ch = Chain(dve)
                    for u in range(NU):
                        base = 2 * (u % 3)
                        qt, kb, hp2 = u // 16, (u % 16) // 2, u % 2
                        dve.wait_ge(mmD, u + 1)
                        nc.vector.tensor_reduce(maxp[:, 2 * hp2:2 * hp2 + 2, qt, kb], ps[:, base:base + 2, :], X,
                                                ALU.max).then_inc(x_upd, 1)
                    dve.wait_ge(x_upd, NU)
                    nc.vector.tensor_reduce(mneg[:], maxp[:].rearrange("p h t k -> p (h t) k"), X, ALU.max,
                                            negate=True).then_inc(amax, 1)
                    dve.wait_ge(mmE, 1)
                    src = ps[0:HG * TB, 6, 0:P]
                    for s in range(PARTS):
                        w = nc.vector.tensor_copy(mrow[:, s, :], src)
                        if s < PARTS - 1:
                            ch(w)
                            ch.wait()
                            ch(nc.vector.tensor_tensor(mres[:], src, mrow[:, s, :], ALU.subtract))
                            ch.wait()
                            src = mres[:]
                    w.then_inc(nbias_ready, 1)
            clear_local()

            with nc.Fori(0, NG - 1) as g:
                run_scores(g, False)
                clear_local()
            run_scores(NG - 1, True)
            clear_local()

            ab = qres
            with nc.Fori(0, NB) as b:
                rows = lambda t: x[:, bass.ds(TB * b + t, 1), :].rearrange("p o d -> p (o d)")
                abv = ab[:].rearrange("p k (u d) -> p (k u) d", d=D)
                with nc.Block() as block:
                    @block.gpsimd
                    def _(pool):
                        nc.gpsimd.tensor_copy(abv, attn[:, bass.ds(TB * b, TB), :]).then_inc(evA, 1)

                    @block.tensor
                    def _(pe):
                        pe.wait_ge(evA, 1)
                        for t in range(TB):
                            for k in range(KD):
                                mm = nc.tensor.transpose(ps[:, k, t * P:(t + 1) * P], abv[:, t, k * P:(k + 1) * P], ident[:])
                        mm.then_inc(mmA, 1)
                        pe.wait_ge(evB, KD)
                        for t in range(TB):
                            for k in range(KD):
                                mm = nc.tensor.matmul(ps[:, 2 + t // 2, (t % 2) * D:(t % 2 + 1) * D], xnT[:, k, t * P:(t + 1) * P],
                                                      wot[:, k, :], start=(k == 0), stop=(k == KD - 1))
                        mm.then_inc(mmB, 1)

                    @block.scalar
                    def _(act):
                        act.wait_ge(mmA, 1)
                        for k in range(KD):
                            nc.scalar.copy(xnT[:, k, :], ps[:, k, :]).then_inc(evB, 1)

                    @block.vector
                    def _(dve):
                        dve.wait_ge(mmB, 1)
                        for t in range(TB):
                            nc.vector.tensor_tensor(rows(t), rows(t), ps[:, 2 + t // 2, (t % 2) * D:(t % 2 + 1) * D], ALU.add)
                clear_local()
            for s in q_loaded:
                local.remove(s)

        with ExitStack() as l2:
            wg, wu = (sb(n, [P, KD, W1C], F32, l2) for n in ("wg", "wu"))
            wd = sb("wd", [P, ND, D], F32, l2)
            wgate = sb("wgate", [P, KD, E1 + 1], F32, l2)
            sg = sb("sg", [P, 2, HS1], F32, l2)
            h = sb("h", [P, 2, W1C], F32, l2)
            hT2 = sb("hT2", [P, 2, ND, P], F32, l2)
            comb = sb("comb", [P, TB, E1 + 1], F32, l2)
            zs = sb("zs", [P, TB], F32, l2)
            ezs = sb("ezs", [P, TB], F32, l2)
            yout = sb("yout", [P, TB, D], F32, l2)
            with nc.Block() as block:
                @block.sync
                def _(sp):
                    sp.dma_start(wgate[:], a["gateT"].rearrange("(k p) e -> p k e", p=P)).then_inc(dma_in, 16)
                    sp.dma_start(wg[:], a["wg"].rearrange("(k p) e -> p k e", p=P)).then_inc(dma_in, 16)
                    sp.dma_start(wu[:], a["wu"].rearrange("(k p) e -> p k e", p=P)).then_inc(dma_in, 16)
                    sp.dma_start(wd[:, 0:ND - 1, :], a["wd"][0:(ND - 1) * P].rearrange("(k p) e -> p k e", p=P)).then_inc(dma_in, 16)
                    sp.dma_start(wd[0:DR, ND - 1, :], a["wd"][(ND - 1) * P:W1C]).then_inc(dma_in, 16)
                    sp.wait_ge(dma_in, 16 * 5)
            clear_local()

            NTB = -(-ND // 4)
            with nc.Fori(0, NB) as b:
                rows = lambda t: x[:, bass.ds(TB * b + t, 1), :].rearrange("p o d -> p (o d)")
                with nc.Block() as block:
                    @block.tensor
                    def _(pe):
                        norm_tensor(pe, 0)
                        for i in range(TB):
                            for k in range(KD):
                                mm = nc.tensor.matmul(ps[:, 6, i * 16:i * 16 + E1 + 1], xnT[:, k, i * P:(i + 1) * P],
                                                      wgate[:, k, :], start=(k == 0), stop=(k == KD - 1))
                        mm.then_inc(mmF, 1)

                        def gate_up(i):
                            for s in range(NSL):
                                n = NSL * i + s
                                if n >= 2:
                                    pe.wait_ge(evB, n - 1)
                                for w, bank in ((wg, 0), (wu, 1)):
                                    for k in range(KD):
                                        mm = nc.tensor.matmul(ps[:, 2 * (n % 2) + bank, 0:HS1], xnT[:, k, i * P:(i + 1) * P],
                                                              w[:, k, s * HS1:(s + 1) * HS1], start=(k == 0), stop=(k == KD - 1))
                                mm.then_inc(mmA, 1)

                        def turn(i):
                            pe.wait_ge(evB, NSL * (i + 1))
                            for q in range(NTB):
                                n = NTB * i + q
                                if n >= 2:
                                    pe.wait_ge(evC, n - 1)
                                for c in range(4 * q, min(ND, 4 * q + 4)):
                                    r = P if c < ND - 1 else DR
                                    mm = nc.tensor.transpose(ps[0:r, 4 + n % 2, (c % 4) * P:(c % 4 + 1) * P],
                                                             h[:, i % 2, c * P:c * P + r], ident[:])
                                mm.then_inc(mmC, 1)

                        def down(i):
                            pe.wait_ge(evC, NTB * (i + 1))
                            if i == 0:
                                pe.wait_ge(z_ready, 1)
                            if i >= 2:
                                pe.wait_ge(x_upd, i - 1)
                            for c in range(ND):
                                r = P if c < ND - 1 else DR
                                mm = nc.tensor.matmul(ps[:, 6 + i % 2, 0:D], hT2[0:r, i % 2, c, :], wd[0:r, c, :],
                                                      start=(c == 0), stop=(c == ND - 1))
                            mm.then_inc(mmD, 1)

                        gate_up(0)
                        for i in range(TB):
                            if i + 1 < TB:
                                gate_up(i + 1)
                            turn(i)
                            down(i)

                    @block.scalar
                    def _(act):
                        norm_scalar(act, 0)
                        act.wait_ge(z_ready, 1)
                        nc.scalar.activation(ez[:, :, 0:E1], z[:, :, 0:E1], ACT.Exp).then_inc(ez_ready, 1)
                        nc.scalar.activation(ezs[:], zs[:], ACT.Exp, scale=-1.0).then_inc(ez_ready, 1)

                        def silu(i):
                            for s in range(NSL):
                                n = NSL * i + s
                                act.wait_ge(mmA, n + 1)
                                if n >= 2:
                                    act.wait_ge(evB, n - 1)
                                nc.scalar.activation(sg[:, n % 2, :], ps[:, 2 * (n % 2), 0:HS1], ACT.Silu).then_inc(evA, 1)

                        def take(i):
                            for q in range(NTB):
                                n = NTB * i + q
                                act.wait_ge(mmC, n + 1)
                                if i >= 2 and q == 0:
                                    act.wait_ge(mmD, i - 1)
                                full = min(ND - 1, 4 * q + 4) - 4 * q
                                cp = nc.scalar.copy(hT2[:, i % 2, 4 * q:4 * q + full, :], ps[:, 4 + n % 2, 0:full * P])
                                if 4 * q + 4 >= ND:
                                    cp = nc.scalar.copy(hT2[0:DR, i % 2, ND - 1, :], ps[0:DR, 4 + n % 2, full * P:(full + 1) * P])
                                cp.then_inc(evC, 1)

                        silu(0)
                        for i in range(TB):
                            if i + 1 < TB:
                                silu(i + 1)
                            take(i)

                    @block.vector
                    def _(dve):
                        ch = Chain(dve)
                        norm_vector(dve, 0, rows)
                        dve.wait_ge(mmF, 1)
                        lg = ps[:, 6, 0:TB * 16].rearrange("p (i e) -> p i e", e=16)
                        ch(nc.vector.tensor_copy(zs[:], lg[:, :, E1]))
                        choose(dve, ch, lg[:, :, 0:E1], E1, TOP1)
                        ch(nc.vector.tensor_tensor(tsum[:], top[:, :, 0], top[:, :, 1], ALU.add))
                        ch.wait()
                        ch(nc.vector.reciprocal(trec[:], tsum[:]))
                        ch.wait()
                        ch(nc.vector.tensor_tensor(wtop[:, :, 0:TOP1], top[:, :, 0:TOP1],
                                                   trec[:].unsqueeze(2).to_broadcast([P, TB, TOP1]), ALU.mult))
                        ch.wait()
                        for k in range(TOP1):
                            ch(nc.vector.tensor_tensor(whit[:, k, :, 0:E1], hit[:, k, :, 0:E1],
                                                       wtop[:, :, k:k + 1].to_broadcast([P, TB, E1]), ALU.mult))
                        ch.wait()
                        ch(nc.vector.tensor_tensor(comb[:, :, 0:E1], whit[:, 0, :, 0:E1], whit[:, 1, :, 0:E1], ALU.add))
                        dve.wait_ge(ez_ready, 2)
                        ch(nc.vector.tensor_scalar(ezs[:], ezs[:], 1.0, None, ALU.add))
                        ch.wait()
                        ch(nc.vector.reciprocal(comb[:, :, E1], ezs[:]))
                        ch.wait()

                        def gated(i):
                            if i >= 2:
                                dve.wait_ge(mmC, NTB * (i - 1))
                            for s in range(NSL):
                                n = NSL * i + s
                                dve.wait_ge(evA, n + 1)
                                parts = 2 if s < NSL - 1 else 1
                                w = HS1 // parts
                                for e in range(parts):
                                    ins = nc.vector.scalar_tensor_tensor(
                                        out=h[:, i % 2, s * HS1 + e * w:s * HS1 + (e + 1) * w],
                                        in0=sg[:, n % 2, e * w:(e + 1) * w], scalar=comb[:, i, 2 * s + e:2 * s + e + 1],
                                        in1=ps[:, 2 * (n % 2) + 1, e * w:(e + 1) * w], op0=ALU.mult, op1=ALU.mult)
                                ins.then_inc(evB, 1)

                        def result(i):
                            dve.wait_ge(mmD, i + 1)
                            nc.vector.tensor_tensor(yout[:, i, :], rows(i), ps[:, 6 + i % 2, 0:D], ALU.add).then_inc(x_upd, 1)

                        gated(0)
                        for i in range(TB):
                            if i + 1 < TB:
                                gated(i + 1)
                            result(i)

                    @block.sync
                    def _(sp):
                        sp.wait_ge(x_upd, TB)
                        sp.dma_start(out.rearrange("(t p) d -> p t d", p=P)[:, bass.ds(TB * b, TB), :], yout[:]).then_inc(dma_out, 16)
                        sp.wait_ge(dma_out, 16)
                clear_local()


def kernel(**inputs):
    import numpy as _np
    import concourse.bacc as _bacc
    from concourse import mybir as _mybir
    from concourse.bass_utils import run_bass_kernel_spmd as _run

    n = {k: _np.asarray(v) for k, v in inputs.items()}
    arrays = {k: n[k] for k in ("L0_attn_W_q", "L0_attn_W_k", "L0_attn_W_v", "L0_attn_W_o", "L0_ffn_Wr", "L0_ffn_br",
                                "L0_ffn_w1", "L0_ffn_w2", "L0_ffn_b2", "L0_ffn_Wp1", "L0_ffn_bp1", "L0_ffn_Wp2",
                                "L0_ffn_bp2")}
    arrays["x"] = n["L0_attn_x"].reshape(NB * S, D)
    arrays["b1T"] = n["L0_ffn_b1"].reshape(E0 * NI, P).T
    arrays["kT"] = n["L1_attn_kv_k"].reshape(KEYS, D).T
    arrays["v"] = n["L1_attn_kv_v"].reshape(KEYS, D)
    arrays["wqT"] = n["L1_attn_Wq"].T
    arrays["woT"] = n["L1_attn_Wo"].T
    arrays["gateT"] = _np.concatenate([n["L1_ffn_gate_w"], n["L1_ffn_shgate_w"][None]]).T
    for name, w, sh in (("wg", "w_gate", "shw_gate"), ("wu", "w_up", "shw_up")):
        arrays[name] = _np.concatenate([n["L1_ffn_" + w].transpose(1, 0, 2).reshape(D, E1 * H1), n["L1_ffn_" + sh]], 1)
    arrays["wd"] = _np.concatenate([n["L1_ffn_w_down"].reshape(E1 * H1, D), n["L1_ffn_shw_down"]])

    nc = _bacc.Bacc("TRN2", target_bir_lowering=False, num_devices=1)
    feed, aps = {}, {}
    for k, v in arrays.items():
        v = _np.ascontiguousarray(v)
        feed[f"in_{k}"] = v
        aps[k] = nc.dram_tensor(f"in_{k}", v.shape, _mybir.dt.from_np(v.dtype), kind="ExternalInput").ap()
    out = nc.dram_tensor("out_x", (NB * S, D), _mybir.dt.float32, kind="ExternalOutput").ap()
    build(nc, aps, out)
    r = _run(nc, [feed], core_ids=[0])
    return r.results[0]["out_x"].reshape(NB, S, D)
```

```python
from contextlib import ExitStack

import concourse.bass as bass
from concourse import mybir

F32 = mybir.dt.float32
F32R = mybir.dt.float32r
BF16 = mybir.dt.bfloat16
U32 = mybir.dt.uint32
I32 = mybir.dt.int32
ACT = mybir.ActivationFunctionType
ALU = mybir.AluOpType
X = mybir.AxisListType.X

P = 128
D = 256
KD = D // P
NB = 4
S = 512
NT = NB * S // P
TB = S // P
EPS = 1e-5

E0, TOP0, I0 = 12, 3, 640
NI = I0 // P

HEADS, DH = 16, 16
KEYS = 4096
NKT = KEYS // P
HG = 4
NG = HEADS // HG
PARTS = 3
SIDE = 6
ROWS = SIDE * DH + PARTS
Q_PART = [0, 1, 2, 0, 1, 0]
K_PART = [0, 0, 0, 1, 1, 2]
VC = DH + 1

E1, TOP1, H1, HS1 = 8, 2, 176, 352
W1C = E1 * H1 + HS1
NSL = W1C // HS1
ND = -(-W1C // P)
DR = W1C - (ND - 1) * P


def build(nc, a, out):
    with ExitStack() as ctx:
        l2 = ctx.enter_context(ExitStack())
        def sb(name, shape, dt=F32, stack=ctx, side=None):
            return stack.enter_context(nc.sbuf_tensor(name, shape, dt, side=side))

        def sem(name):
            return ctx.enter_context(nc.semaphore(name))

        ps = ctx.enter_context(nc.psum_tensor("banks", [P, 8, 512], F32))
        kparts = nc.dram_tensor("key_parts", [PARTS, D, KEYS], BF16, kind="Internal").ap()
        qparts = nc.dram_tensor("query_parts", [PARTS, D, NB * S], BF16, kind="Internal").ap()

        x = sb("x", [P, NT, D])
        ident = sb("ident", [P, P])
        xn = sb("xn", [P, TB, D])
        xnT = sb("xnT", [P, KD, S])
        mhalf = sb("mhalf", [P, TB])
        acc = sb("acc", [P, NT, D])
        fac = sb("fac", [P, NB])
        iota_i = sb("iota_i", [P, E0], I32)
        iota = sb("iota", [P, E0])
        ones = sb("ones", [P, P])
        wp1 = sb("wp1", [P, KD, P])
        bp1, wp2, bp2 = (sb(n, [P, 1]) for n in ("bp1", "wp2", "bp2"))
        wot = sb("wot", [P, KD, D])
        wqt = sb("wqt", [P, KD, D])

        x_loaded, setup_done, load_w = sem("x_loaded"), sem("setup_done"), sem("load_w")
        step = sem("vector_step")

        def sems(names):
            return [sem(n) for n in names.split()]

        def clear(*used):
            with nc.Block() as block:
                @block.gpsimd
                def _(pool):
                    for s in used[0::4]:
                        pool.sem_clear(s)

                @block.sync
                def _(sp):
                    for s in used[1::4]:
                        sp.sem_clear(s)

                @block.scalar
                def _(act):
                    for s in used[2::4]:
                        act.sem_clear(s)

                @block.vector
                def _(dve):
                    for s in used[3::4]:
                        dve.sem_clear(s)

        class Chain:
            def __init__(self, dve):
                self.dve, self.n = dve, 0

            def __call__(self, ins):
                ins.then_inc(step, 1)
                self.n += 1

            def wait(self):
                self.dve.wait_ge(step, self.n)

        def f32(t):
            return t.bitcast(F32)

        class Lane:
            def __init__(self, tag, bank, xn, xnT, stack):
                self.bank, self.xn, self.xnT = bank, xn, xnT
                self.stats = sb("stats" + tag, [P, TB, 6], F32, stack)
                self.meanvar = sb("meanvar" + tag, [P, TB, 2], F32, stack)
                self.vareps = sb("vareps" + tag, [P, TB], F32, stack)
                self.rstd = sb("rstd" + tag, [P, TB], F32, stack)
                self.stats_done, self.aggr_done, self.var_done, self.rstd_done, self.norm_done, self.turned, self.taken = self.norm_sems = (
                    [sem(n + tag) for n in ("ln_stats", "ln_aggr", "ln_var", "ln_rstd", "ln_norm", "ln_turned", "ln_taken")])

        def norm_stats(dve, n, rows, L):
            for t in range(TB):
                nc.vector.bn_stats(L.stats[:, t, :], rows(t)).then_inc(L.stats_done, 1)
            dve.wait_ge(L.stats_done, TB * (n + 1))
            for t in range(TB):
                nc.vector.bn_aggr(L.meanvar[:, t, :], L.stats[:, t, :]).then_inc(L.aggr_done, 1)
            dve.wait_ge(L.aggr_done, TB * (n + 1))
            nc.vector.tensor_scalar(L.vareps[:], L.meanvar[:, :, 1], EPS, None, ALU.add).then_inc(L.var_done, 1)

        def norm_apply(dve, n, rows, L):
            dve.wait_ge(L.rstd_done, n + 1)
            if n:
                dve.wait_ge(L.turned, n)
            for t in range(TB):
                nc.vector.tensor_scalar(L.xn[:, t, :], rows(t), L.meanvar[:, t, 0:1], L.rstd[:, t:t + 1],
                                        ALU.subtract, ALU.mult).then_inc(L.norm_done, 1)

        def norm_vector(dve, n, rows, L):
            norm_stats(dve, n, rows, L)
            norm_apply(dve, n, rows, L)

        def norm_pool(pool, n, L):
            pool.wait_ge(L.var_done, n + 1)
            nc.gpsimd.tensor_tensor(L.rstd[:], L.vareps[:], mhalf[:], ALU.pow).then_inc(L.rstd_done, 1)

        def norm_scalar(act, n, L):
            act.wait_ge(L.turned, n + 1)
            for k in range(KD):
                nc.scalar.copy(L.xnT[:, k, :], ps[:, L.bank + k, :]).then_inc(L.taken, 1)

        def turn_tile(pe, n, t, L):
            pe.wait_ge(L.norm_done, TB * n + t + 1)
            for k in range(KD):
                mm = nc.tensor.transpose(ps[:, L.bank + k, t * P:(t + 1) * P], L.xn[:, t, k * P:(k + 1) * P], ident[:])
            if t == TB - 1:
                mm.then_inc(L.turned, 1)

        def norm_tensor(pe, n, L):
            for t in range(TB):
                turn_tile(pe, n, t, L)

        main = Lane("", 0, xn, xnT, ctx)

        def choice_buffers(stack, nt):
            shapes = dict(z=[nt, E0], ez=[nt, E0], zmax=[nt], zsum=[nt], zrec=[nt], probs=[nt, E0], top=[nt, 8], topi=[nt, 8],
                          topf=[nt, 8], dtop=[nt, TOP0], etop=[nt, TOP0], tsum=[nt], trec=[nt], wtop=[nt, TOP0],
                          hit=[TOP0, nt, E0], whit=[TOP0, nt, E0])
            return [sb(f"{n}_{nt}", [P] + sh, U32 if n == "topi" else F32, stack) for n, sh in shapes.items()]

        def spread(t, nt, ne):
            return t[:, 0:nt].unsqueeze(2).to_broadcast([P, nt, ne])

        def choose_start(ch, nt, ne, z_ready):
            if ch.n:
                ch.wait()
            ch(nc.vector.tensor_reduce(zmax[:, 0:nt], z[:, 0:nt, 0:ne], X, ALU.max))
            ch.wait()
            nc.vector.tensor_tensor(z[:, 0:nt, 0:ne], z[:, 0:nt, 0:ne], spread(zmax, nt, ne), ALU.subtract).then_inc(z_ready, 1)

        def choose_top(dve, ch, nt, ne, ez_ready):
            dve.wait_ge(ez_ready, 1)
            ch(nc.vector.tensor_reduce(zsum[:, 0:nt], ez[:, 0:nt, 0:ne], X, ALU.add))
            ch.wait()
            ch(nc.vector.reciprocal(zrec[:, 0:nt], zsum[:, 0:nt]))
            ch.wait()
            ch(nc.vector.tensor_tensor(probs[:, 0:nt, 0:ne], ez[:, 0:nt, 0:ne], spread(zrec, nt, ne), ALU.mult))
            ch.wait()
            for i in range(nt):
                ch(nc.vector.max(top[:, i, :], probs[:, i, 0:ne]))
            ch.wait()

        def choose_hits(ch, nt, ne, ntop):
            for i in range(nt):
                ch(nc.vector.max_index(topi[:, i, :], top[:, i, :], probs[:, i, 0:ne]))
            ch.wait()
            ch(nc.vector.tensor_copy(topf[:, 0:nt], topi[:, 0:nt]))
            ch.wait()
            for k in range(ntop):
                ch(nc.vector.tensor_tensor(hit[:, k, 0:nt, 0:ne], iota[:, 0:ne].unsqueeze(1).to_broadcast([P, nt, ne]),
                                           topf[:, 0:nt, k:k + 1].to_broadcast([P, nt, ne]), ALU.is_equal))

        with ExitStack() as l0:
            def s0(name, shape, dt=F32):
                return sb(name, shape, dt, l0)

            (z, ez, zmax, zsum, zrec, probs, top, topi, topf, dtop, etop, tsum, trec, wtop, hit, whit) = choice_buffers(l0, NT)
            wq, wk, wv, wo = (s0(n, [P, KD, D]) for n in ("wq", "wk", "wv", "wo"))
            wr = s0("wr", [P, KD, E0])
            br = s0("br", [P, E0])
            b1 = s0("b1", [P, E0 * NI])
            b2 = s0("b2", [E0, D])
            xh, xl = (s0(n, [P, KD, NB * S], F32R) for n in ("xh", "xl"))
            chosen = s0("chosen", [P, NT, 2 * E0])
            w1f = s0("w1f", [P, KD, I0])
            w2f = s0("w2f", [P, NI, D])
            w1h, w1l = ([s0(f"w1{n}0", [P, KD, I0], F32R)] for n in "hl")
            w2h, w2l = ([s0(f"w2{n}0", [P, NI, D], F32R)] for n in "hl")

            def load_expert(sp, e, done):
                sp.dma_start(w1f[:], a["L0_ffn_w1"][e].rearrange("(k p) i -> p k i", p=P)).then_inc(done, 16)
                sp.dma_start(w2f[:], a["L0_ffn_w2"][e].rearrange("(k p) i -> p k i", p=P)).then_inc(done, 16)

            def split_expert(eng, ops, i, done, before):
                ops.tensor_copy(w1h[i][:], w1f[:]).then_inc(done, 1)
                ops.tensor_copy(w2h[i][:], w2f[:]).then_inc(done, 1)
                eng.wait_ge(done, before + 2)
                ops.tensor_tensor(w1l[i][:], w1f[:], f32(w1h[i][:]), ALU.subtract).then_inc(done, 1)
                ops.tensor_tensor(w2l[i][:], w2f[:], f32(w2h[i][:]), ALU.subtract).then_inc(done, 1)

            expert0_in, first_split = sems("expert0_in first_split")

            WEIGHTS = 14

            with nc.Block() as block:
                @block.sync
                def _(sp):
                    sp.dma_start(x[:], a["x"].rearrange("(t p) d -> p t d", p=P)).then_inc(x_loaded, 16)
                    for w, n in ((wq, "L0_attn_W_q"), (wk, "L0_attn_W_k"), (wv, "L0_attn_W_v"), (wo, "L0_attn_W_o"),
                                 (wr, "L0_ffn_Wr"), (wp1, "L0_ffn_Wp1"), (wqt, "wqT"), (wot, "woT")):
                        sp.dma_start(w[:], a[n].rearrange("(k p) e -> p k e", p=P)).then_inc(load_w, 16)
                    sp.dma_start(b1[:], a["b1T"]).then_inc(load_w, 16)
                    sp.dma_start(b2[:], a["L0_ffn_b2"]).then_inc(load_w, 16)
                    sp.dma_start(br[:], a["L0_ffn_br"].partition_broadcast(P)).then_inc(load_w, 16)
                    sp.dma_start(bp1[:], a["L0_ffn_bp1"].rearrange("(p o) -> p o", o=1)).then_inc(load_w, 16)
                    sp.dma_start(wp2[:], a["L0_ffn_Wp2"]).then_inc(load_w, 16)
                    sp.dma_start(bp2[:], a["L0_ffn_bp2"].partition_broadcast(P)).then_inc(load_w, 16)
                    load_expert(sp, 0, expert0_in)

                @block.gpsimd
                def _(pool):
                    nc.gpsimd.memset(ident[:], 0.0).then_inc(setup_done, 1)
                    pool.wait_ge(setup_done, 1)
                    nc.gpsimd.affine_select(out=ident[:], in_=ident[:], compare_op=ALU.not_equal, fill=1.0, base=0,
                                            pattern=[[-1, P]], channel_multiplier=1).then_inc(setup_done, 1)
                    nc.gpsimd.iota(iota_i[:], pattern=[[1, E0]], base=0, channel_multiplier=0).then_inc(setup_done, 1)

                @block.vector
                def _(dve):
                    nc.vector.memset(ones[:], 1.0)
                    dve.wait_ge(setup_done, 3)
                    nc.vector.tensor_copy(iota[:], iota_i[:])
                    nc.vector.memset(mhalf[:], -0.5)

            with ExitStack() as at:
                scale = float(D) ** -0.5

                class AttnLane(Lane):
                    def __init__(self, c):
                        tag = str(c)
                        xn_, xnT_ = (xn, xnT) if c == 0 else (sb("xn1", [P, TB, D], F32, at), sb("xnT1", [P, KD, S], F32, at))
                        super().__init__(tag, 4 * c, xn_, xnT_, at)
                        self.qT, self.kT = (sb(n + tag, [P, KD, S], F32, at) for n in ("qT", "kT"))
                        self.oT = self.qT
                        self.v = sb("v" + tag, [P, TB, D], F32, at)
                        self.pm = sb("pm" + tag, [P, TB, S], F32, at)
                        self.pT = sb("pT" + tag, [P, TB, S], F32, at)
                        self.nmax, self.rsum, self.rrec = (sb(n + tag, [P, TB], F32, at) for n in ("nmax", "rsum", "rrec"))
                        (self.q_mm, self.k_mm, self.v_mm, self.score_mm, self.pT_mm, self.pv_mm, self.proj_mm, self.route_mm,
                         self.q_taken, self.k_taken, self.v_taken, self.nmax_done, self.p_done, self.pT_act, self.pT_dve,
                         self.o_taken, self.rrec_done, self.x_done, self.xh_done) = self.attn_sems = sems(" ".join(n + tag for n in (
                             "q_mm k_mm v_mm score_mm pT_mm pv_mm proj_mm route_mm q_taken k_taken v_taken nmax_done "
                             "p_done pT_act pT_dve o_taken rrec_done x_done xh_done").split()))

                lanes = [AttnLane(c) for c in range(2)]
                assert NB % 2 == 0

                with nc.Fori(0, NB // 2) as b2i:
                    def rows_of(c):
                        return lambda t: x[:, bass.ds(2 * TB * b2i + TB * c + t, 1), :].rearrange("p o d -> p (o d)")

                    with nc.Block() as block:
                        @block.gpsimd
                        def _(pool):
                            for L in lanes:
                                norm_pool(pool, 0, L)
                            for c, L in enumerate(lanes):
                                norm_pool(pool, 1, L)
                            for c, L in enumerate(lanes):
                                cur = bass.ds(2 * S * b2i + S * c, S)
                                pool.wait_ge(L.taken, 2 * KD)
                                nc.gpsimd.tensor_copy(xh[:, :, cur], L.xnT[:]).then_inc(L.xh_done, 1)
                                pool.wait_ge(L.xh_done, 1)
                                nc.gpsimd.tensor_tensor(xl[:, :, cur], L.xnT[:], f32(xh[:, :, cur]), ALU.subtract)

                        @block.tensor
                        def _(pe):
                            def project(L, w, bank, done):
                                for m in range(KD):
                                    for k in range(KD):
                                        mm = nc.tensor.matmul(ps[:, bank + m, :], w[:, k, m * P:(m + 1) * P], L.xnT[:, k, :],
                                                              start=(k == 0), stop=(k == KD - 1))
                                    mm.then_inc(done, 1)

                            def qkv(L):
                                B = L.bank
                                pe.wait_ge(L.taken, KD)
                                project(L, wq, B + 2, L.q_mm)
                                project(L, wk, B, L.k_mm)
                                for i in range(TB):
                                    if i % 2 == 0:
                                        pe.wait_ge(L.q_taken, i // 2 + 1)
                                    for k in range(KD):
                                        mm = nc.tensor.matmul(ps[:, B + 2 + i // 2, (i % 2) * D:(i % 2 + 1) * D],
                                                              L.xnT[:, k, i * P:(i + 1) * P], wv[:, k, :],
                                                              start=(k == 0), stop=(k == KD - 1))
                                    if i % 2:
                                        mm.then_inc(L.v_mm, 1)

                            def scores(L):
                                pe.wait_ge(L.k_taken, KD)
                                for i in range(TB):
                                    if i >= 2:
                                        pe.wait_ge(L.v_taken, i - 1)
                                    for m in range(KD):
                                        mm = nc.tensor.matmul(ps[:, L.bank + i, :], L.qT[:, m, i * P:(i + 1) * P], L.kT[:, m, :],
                                                              start=(m == 0), stop=(m == KD - 1))
                                    mm.then_inc(L.score_mm, 1)

                            def turn_probs(L):
                                pe.wait_ge(L.p_done, TB)
                                for kb in range(TB):
                                    for i in range(TB):
                                        mm = nc.tensor.transpose(ps[:, L.bank + kb, i * P:(i + 1) * P],
                                                                 L.pm[:, i, kb * P:(kb + 1) * P], ident[:])
                                    mm.then_inc(L.pT_mm, 1)

                            def weigh(L, m):
                                pe.wait_ge(L.pT_dve, 2)
                                pe.wait_ge(L.pT_act, 2)
                                for kb in range(TB):
                                    mm = nc.tensor.matmul(ps[:, L.bank + m, :], L.v[:, kb, m * P:(m + 1) * P], L.pT[:, kb, :],
                                                          start=(kb == 0), stop=(kb == TB - 1))
                                mm.then_inc(L.pv_mm, 1)

                            def output(L):
                                pe.wait_ge(L.o_taken, KD)
                                for i in range(TB):
                                    for m in range(KD):
                                        mm = nc.tensor.matmul(ps[:, L.bank + 2 + i // 2, (i % 2) * D:(i % 2 + 1) * D],
                                                              L.oT[:, m, i * P:(i + 1) * P], wo[:, m, :],
                                                              start=(m == 0), stop=(m == KD - 1))
                                    if i % 2:
                                        mm.then_inc(L.proj_mm, 1)

                            def router(L):
                                pe.wait_ge(L.taken, 2 * KD)
                                for i in range(TB):
                                    for k in range(KD):
                                        mm = nc.tensor.matmul(ps[:, L.bank + 2, i * E0:(i + 1) * E0],
                                                              L.xnT[:, k, i * P:(i + 1) * P], wr[:, k, :],
                                                              start=(k == 0), stop=(k == KD - 1))
                                mm.then_inc(L.route_mm, 1)

                            pe.wait_ge(load_w, 16 * WEIGHTS)
                            one, two = lanes
                            norm_tensor(pe, 0, one)
                            norm_tensor(pe, 0, two)
                            qkv(one)
                            qkv(two)
                            scores(one)
                            scores(two)
                            turn_probs(one)
                            turn_probs(two)
                            weigh(one, 0)
                            weigh(one, 1)
                            weigh(two, 0)
                            output(one)
                            weigh(two, 1)
                            output(two)
                            norm_tensor(pe, 1, one)
                            norm_tensor(pe, 1, two)
                            router(one)
                            router(two)

                        @block.scalar
                        def _(act):
                            for L in lanes:
                                norm_scalar(act, 0, L)
                            for L in lanes:
                                for m in range(KD):
                                    act.wait_ge(L.q_mm, m + 1)
                                    nc.scalar.activation(L.qT[:, m, :], ps[:, L.bank + 2 + m, :], ACT.Copy,
                                                         scale=scale).then_inc(L.q_taken, 1)
                            for L in lanes:
                                for i in range(TB):
                                    act.wait_ge(L.nmax_done, i + 1)
                                    nc.scalar.activation(L.pm[:, i, :], ps[:, L.bank + i, :], ACT.Exp, bias=L.nmax[:, i:i + 1],
                                                         accum_out=L.rsum[:, i:i + 1]).then_inc(L.p_done, 1)
                            for L in lanes:
                                for kb in (1, 3):
                                    act.wait_ge(L.pT_mm, kb + 1)
                                    nc.scalar.copy(L.pT[:, kb, :], ps[:, L.bank + kb, :]).then_inc(L.pT_act, 1)
                            for L in lanes:
                                for m in range(KD):
                                    act.wait_ge(L.pv_mm, m + 1)
                                    nc.scalar.copy(L.oT[:, m, :], ps[:, L.bank + m, :]).then_inc(L.o_taken, 1)
                            for L in lanes:
                                norm_scalar(act, 1, L)

                        @block.vector
                        def _(dve):
                            dve.wait_ge(x_loaded, 16)
                            dve.wait_ge(load_w, 16 * WEIGHTS)
                            for c, L in enumerate(lanes):
                                norm_vector(dve, 0, rows_of(c), L)
                            for L in lanes:
                                for m in range(KD):
                                    dve.wait_ge(L.k_mm, m + 1)
                                    nc.vector.tensor_copy(L.kT[:, m, :], ps[:, L.bank + m, :]).then_inc(L.k_taken, 1)
                                for j in range(2):
                                    dve.wait_ge(L.v_mm, j + 1)
                                    nc.vector.tensor_copy(L.v[:, 2 * j:2 * j + 2, :], ps[:, L.bank + 2 + j, :]).then_inc(L.v_taken, 1)
                            for L in lanes:
                                for i in range(TB):
                                    dve.wait_ge(L.score_mm, i + 1)
                                    nc.vector.tensor_reduce(L.nmax[:, i:i + 1], ps[:, L.bank + i, :], X, ALU.max,
                                                            negate=True).then_inc(L.nmax_done, 1)
                            for L in lanes:
                                for kb in (0, 2):
                                    dve.wait_ge(L.pT_mm, kb + 1)
                                    nc.vector.tensor_copy(L.pT[:, kb, :], ps[:, L.bank + kb, :]).then_inc(L.pT_dve, 1)
                                nc.vector.reciprocal(L.rrec[:], L.rsum[:]).then_inc(L.rrec_done, 1)
                            for c, L in enumerate(lanes):
                                rows = rows_of(c)
                                dve.wait_ge(L.rrec_done, 1)
                                for i in range(TB):
                                    dve.wait_ge(L.proj_mm, i // 2 + 1)
                                    nc.vector.scalar_tensor_tensor(out=rows(i), in0=ps[:, L.bank + 2 + i // 2, (i % 2) * D:(i % 2 + 1) * D],
                                                                   scalar=L.rrec[:, i:i + 1], in1=rows(i),
                                                                   op0=ALU.mult, op1=ALU.add).then_inc(L.x_done, 1)
                                dve.wait_ge(L.x_done, TB)
                                norm_vector(dve, 1, rows, L)
                            for c, L in enumerate(lanes):
                                dve.wait_ge(L.route_mm, 1)
                                logits = ps[:, L.bank + 2, 0:TB * E0].rearrange("p (i e) -> p i e", e=E0)
                                nc.vector.tensor_tensor(z[:, bass.ds(2 * TB * b2i + TB * c, TB), :], logits,
                                                        br[:].unsqueeze(1).to_broadcast([P, TB, E0]), ALU.add)
                    clear(*[s for L in lanes for s in L.norm_sems + L.attn_sems])

            with ExitStack() as ex:
                hf = sb("hf", [P, 2, S], F32, ex)
                hh, hl = ([sb(f"h{n}{i}", [P, NI, S], F32R, ex) for i in range(2)] for n in "hl")
                cw = sb("cw", [P, NT, E0], F32, ex)
                cwT = sb("cwT", [E0, NB * S], F32, ex)
                cnt = sb("cnt", [P, E0], F32, ex)
                crec = sb("crec", [P, E0], F32, ex)
                we = sb("we", [P, E0], F32, ex)

                for t, n, sh in ((w1h, "w1h1", [P, KD, I0]), (w1l, "w1l1", [P, KD, I0]),
                                 (w2h, "w2h1", [P, NI, D]), (w2l, "w2l1", [P, NI, D])):
                    t.append(sb(n, sh, F32R, ex))
                KC = 256
                KPAIR = 3
                kf = sb("kf", [P, KD, KC], F32, ex)
                ksp = sb("ksp", [P, PARTS, KD, KC], BF16, ex)

                second_in, chosen_ready, z_ready, ez_ready, count_mm, cw_done, cw_turned, cw_taken, bias_mm = sems(
                    "second_in chosen_ready z_ready ez_ready count_mm cw_done cw_turned cw_taken bias_mm")

                with nc.Block() as block:
                    @block.sync
                    def _(sp):
                        sp.wait_ge(first_split, 4)
                        load_expert(sp, 1, second_in)
                        sp.wait_ge(second_in, 32)

                    @block.gpsimd
                    def _(pool):
                        pool.wait_ge(expert0_in, 32)
                        split_expert(pool, nc.gpsimd, 0, first_split, 0)

                    @block.tensor
                    def _(pe):
                        pe.wait_ge(chosen_ready, 2)
                        for t in range(NT):
                            mm = nc.tensor.matmul(ps[:, 0, 0:2 * E0], ones[:], chosen[:, t, :], start=(t == 0), stop=(t == NT - 1))
                        mm.then_inc(count_mm, 1)
                        pe.wait_ge(cw_done, 1)
                        for t in range(NT):
                            mm = nc.tensor.transpose(ps[0:E0, 1 + t // 4, (t % 4) * P:(t % 4 + 1) * P], cw[:, t, :], ident[:])
                            if t % 4 == 3:
                                mm.then_inc(cw_turned, 1)
                        pe.wait_ge(cw_taken, 4)
                        for t in range(NT):
                            mm = nc.tensor.matmul(ps[:, t // 2, (t % 2) * D:(t % 2 + 1) * D], cwT[:, t * P:(t + 1) * P], b2[:],
                                                  start=True, stop=True)
                            if t % 2:
                                mm.then_inc(bias_mm, 1)

                    @block.vector
                    def _(dve):
                        ch = Chain(dve)
                        choose_start(ch, NT, E0, z_ready)
                        choose_top(dve, ch, NT, E0, ez_ready)
                        choose_hits(ch, NT, E0, TOP0)
                        nc.vector.tensor_tensor(dtop[:], top[:, :, 0:TOP0], top[:, :, 0:1].to_broadcast([P, NT, TOP0]),
                                                ALU.subtract).then_inc(z_ready, 1)
                        dve.wait_ge(ez_ready, 2)
                        ch(nc.vector.tensor_reduce(tsum[:], etop[:], X, ALU.add))
                        ch.wait()
                        ch(nc.vector.reciprocal(trec[:], tsum[:]))
                        ch.wait()
                        ch(nc.vector.tensor_tensor(wtop[:], etop[:], trec[:].unsqueeze(2).to_broadcast([P, NT, TOP0]), ALU.mult))
                        ch.wait()
                        for k in range(TOP0):
                            ch(nc.vector.tensor_tensor(whit[:, k], hit[:, k], wtop[:, :, k:k + 1].to_broadcast([P, NT, E0]), ALU.mult))
                        ch.wait()
                        for c0, src in ((0, whit), (E0, hit)):
                            ch(nc.vector.tensor_tensor(src[:, 0], src[:, 0], src[:, 1], ALU.add))
                            ch.wait()
                            nc.vector.tensor_tensor(chosen[:, :, c0:c0 + E0], src[:, 0], src[:, 2], ALU.add).then_inc(chosen_ready, 1)
                        dve.wait_ge(count_mm, 1)
                        ch(nc.vector.tensor_scalar(cnt[:], ps[:, 0, E0:2 * E0], 1.0, None, ALU.max))
                        ch.wait()
                        ch(nc.vector.reciprocal(crec[:], cnt[:]))
                        ch.wait()
                        ch(nc.vector.tensor_tensor(we[:], crec[:], ps[:, 0, 0:E0], ALU.mult))
                        ch.wait()
                        nc.vector.tensor_tensor(cw[:], chosen[:, :, E0:2 * E0], we[:].unsqueeze(1).to_broadcast([P, NT, E0]),
                                                ALU.mult).then_inc(cw_done, 1)
                        for j in range(0, NT // 2, 2):
                            dve.wait_ge(bias_mm, j + 1)
                            nc.vector.tensor_copy(acc[:, 2 * j:2 * j + 2, :], ps[:, j, :])

                    @block.scalar
                    def _(act):
                        act.wait_ge(z_ready, 1)
                        nc.scalar.activation(ez[:], z[:], ACT.Exp).then_inc(ez_ready, 1)
                        act.wait_ge(z_ready, 2)
                        nc.scalar.activation(etop[:], dtop[:], ACT.Exp).then_inc(ez_ready, 1)
                        for c in range(4):
                            act.wait_ge(cw_turned, c + 1)
                            nc.scalar.copy(cwT[:, c * S:(c + 1) * S], ps[0:E0, 1 + c, :]).then_inc(cw_taken, 1)
                        for j in range(1, NT // 2, 2):
                            act.wait_ge(bias_mm, j + 1)
                            nc.scalar.copy(acc[:, 2 * j:2 * j + 2, :], ps[:, j, :])
                clear(step)

                weights_in, weights_split, hidden_mm, out_mm, relu_done, parts_done, high_done, sum_done, keys_in, keys_out, key_parts = \
                    pair_sems = sems("weights_in weights_split hidden_mm out_mm relu_done parts_done high_done sum_done "
                                     "keys_in keys_out key_parts")
                STEPS = 2 * NB

                def three(out, ah, al, bh, bl, first, last):
                    nc.tensor.matmul(out, ah, bh, start=first, stop=False)
                    nc.tensor.matmul(out, ah, bl, start=False, stop=False)
                    return nc.tensor.matmul(out, al, bh, start=False, stop=last)

                def expert_pair(e0, more, k0):
                    with nc.Block() as block:
                        @block.sync
                        def _(sp):
                            times = KPAIR if more else KEYS // KC - KPAIR * (E0 // 2 - 1)
                            chunk = lambda n: bass.ds(k0 + n * KC, KC)

                            def load_key_chunk(n):
                                sp.dma_start(kf[:], a["kT"].rearrange("(k p) c -> p k c", p=P)[:, :, chunk(n)]).then_inc(keys_in, 16)

                            load_key_chunk(0)
                            for n in range(times):
                                sp.wait_ge(key_parts, 5 * (n + 1))
                                if n + 1 < times:
                                    load_key_chunk(n + 1)
                                for s in range(PARTS):
                                    sp.dma_start(kparts[s].rearrange("(k p) c -> p k c", p=P)[:, :, chunk(n)],
                                                 ksp[:, s]).then_inc(keys_out, 16)
                                if n == 0 and more:
                                    load_expert(sp, e0 + 2, weights_in)
                            sp.wait_ge(keys_out, 16 * PARTS * times)
                            if more:
                                sp.wait_ge(weights_split, 8)
                                load_expert(sp, e0 + 3, weights_in)
                                sp.wait_ge(weights_in, 64)

                        @block.gpsimd
                        def _(pool):
                            split_expert(pool, nc.gpsimd, 1, weights_split, 0)
                            for n in range(KPAIR if more else KEYS // KC - KPAIR * (E0 // 2 - 1)):
                                pool.wait_ge(keys_in, 16 * (n + 1))
                                if n:
                                    pool.wait_ge(keys_out, 16 * PARTS * n)
                                for s in range(PARTS):
                                    nc.gpsimd.tensor_copy(ksp[:, s], kf[:]).then_inc(key_parts, 1)
                                    if s < PARTS - 1:
                                        pool.wait_ge(key_parts, 5 * n + 2 * s + 1)
                                        nc.gpsimd.tensor_tensor(kf[:], kf[:], ksp[:, s], ALU.subtract).then_inc(key_parts, 1)
                                        pool.wait_ge(key_parts, 5 * n + 2 * s + 2)
                            if more:
                                pool.wait_ge(weights_in, 32)
                                pool.wait_ge(out_mm, 2 * NB)
                                split_expert(pool, nc.gpsimd, 0, weights_split, 4)

                        @block.tensor
                        def _(pe):
                            def hidden(s):
                                q, c = divmod(s, NB)
                                if s == NB:
                                    pe.wait_ge(weights_split, 4)
                                for i in range(NI):
                                    n = NI * s + i
                                    if n >= 4:
                                        pe.wait_ge(relu_done, n - 3)
                                    for k in range(KD):
                                        mm = three(ps[:, n % 4, :], w1h[q][:, k, i * P:(i + 1) * P],
                                                   w1l[q][:, k, i * P:(i + 1) * P], xh[:, k, c * S:(c + 1) * S],
                                                   xl[:, k, c * S:(c + 1) * S], k == 0, k == KD - 1)
                                    mm.then_inc(hidden_mm, 1)

                            def output(s):
                                q = s // NB
                                pe.wait_ge(parts_done, NI * (s + 1))
                                for t in range(TB):
                                    u = 2 * s + t // 2
                                    if u >= 4 and t % 2 == 0:
                                        pe.wait_ge(sum_done, 2 * (u - 3))
                                    for i in range(NI):
                                        mm = three(ps[:, 4 + u % 4, (t % 2) * D:(t % 2 + 1) * D],
                                                   hh[s % 2][:, i, t * P:(t + 1) * P], hl[s % 2][:, i, t * P:(t + 1) * P],
                                                   w2h[q][:, i, :], w2l[q][:, i, :], i == 0, i == NI - 1)
                                    if t % 2:
                                        mm.then_inc(out_mm, 1)

                            hidden(0)
                            for s in range(STEPS):
                                if s + 1 < STEPS:
                                    hidden(s + 1)
                                output(s)

                        @block.scalar
                        def _(act):
                            for n in range(NI * STEPS):
                                act.wait_ge(hidden_mm, n + 1)
                                if n >= 2:
                                    act.wait_ge(parts_done, n - 1)
                                bias = b1[:, bass.ds((e0 + n // (NI * NB)) * NI + n % NI, 1)]
                                nc.scalar.activation(hf[:, n % 2, :], ps[:, n % 4, :], ACT.Relu, bias=bias).then_inc(relu_done, 1)

                        @block.vector
                        def _(dve):
                            def parts(s):
                                if s >= 2:
                                    dve.wait_ge(out_mm, 2 * (s - 1))
                                for i in range(NI):
                                    n = NI * s + i
                                    dve.wait_ge(relu_done, n + 1)
                                    nc.vector.tensor_copy(hh[s % 2][:, i, :], hf[:, n % 2, :]).then_inc(high_done, 1)
                                    dve.wait_ge(high_done, n + 1)
                                    nc.vector.tensor_tensor(hl[s % 2][:, i, :], hf[:, n % 2, :], f32(hh[s % 2][:, i, :]),
                                                            ALU.subtract).then_inc(parts_done, 1)

                            def sums(s):
                                q, c = divmod(s, NB)
                                for t in range(TB):
                                    n = TB * s + t
                                    u = 2 * s + t // 2
                                    dve.wait_ge(out_mm, u + 1)
                                    if n >= NT:
                                        dve.wait_ge(sum_done, n - NT + 1)
                                    tile = TB * c + t
                                    nc.vector.scalar_tensor_tensor(
                                        out=acc[:, tile, :], in0=ps[:, 4 + u % 4, (t % 2) * D:(t % 2 + 1) * D],
                                        scalar=cw[:, tile, bass.ds(e0 + q, 1)], in1=acc[:, tile, :],
                                        op0=ALU.mult, op1=ALU.add).then_inc(sum_done, 1)
                                if q and not more:
                                    dve.wait_ge(sum_done, TB * (s + 1))
                                    nc.vector.tensor_reduce(xn[:, c, :], acc[:, TB * c:TB * (c + 1), :].rearrange("p t d -> p d t"),
                                                            X, ALU.add)

                            parts(0)
                            for s in range(STEPS):
                                if s + 1 < STEPS:
                                    parts(s + 1)
                                sums(s)
                    clear(*pair_sems)

                with nc.Fori(0, E0 // 2 - 1) as pair:
                    expert_pair(2 * pair, True, KPAIR * KC * pair)
                expert_pair(E0 - 2, False, KPAIR * KC * (E0 // 2 - 1))


        with ExitStack() as l1:
            kst = [sb(f"kst{i}", [ROWS, HG, KEYS], BF16, l1) for i in range(2)]
            qst = [sb(f"qst{i}", [ROWS, HG, S], BF16, l1) for i in range(NB)]
            vnext = sb("vnext", [P, NKT, HG * DH], F32, l1)
            vcur = sb("vcur", [P, NKT, HG, VC], F32, l1)
            pring = sb("pring", [P, 2 * HG, S], F32, l1)
            osb = sb("osb", [P, S], F32, l1)
            orec = sb("orec", [P, TB, HG], F32, l1)
            maxp = sb("maxp", [P, HG, TB, KEYS // 512], F32, l1)
            mneg = sb("mneg", [P, HG * TB], F32, l1)
            mres = sb("mres", [HG * TB, P], F32, l1)
            mrow = sb("mrow", [HG * TB, PARTS, P], BF16, l1)
            q_loaded = [sem(f"q_loaded{i}") for i in range(NB)]
            v_loaded = sem("v_loaded")
            keys_in0, ones_set, max_mm, max_taken, max_turned = sems("keys_in0 ones_set max_mm max_taken max_turned")
            rows_in, max_done, rows_ready = maxima_sems = sems("rows_in max_done rows_ready")
            q_mm, q_taken, q_split, q_stored, x_done = query_sems = sems("q_mm q_taken q_split q_stored x_done")

            def load_keys(sp, i, g, done):
                for s in range(SIDE):
                    src = kparts[K_PART[s]].rearrange("(h r) c -> r h c", r=DH)[:, bass.ds(g * HG, HG), :]
                    sp.dma_start(kst[i][s * DH:(s + 1) * DH], src).then_inc(done, 16)

            def load_values(sp, g):
                sp.dma_start(vnext[:], a["v"].rearrange("(t p) d -> p t d", p=P)[:, :, bass.ds(g * HG * DH, HG * DH)]
                             ).then_inc(v_loaded, 16)

            def load_queries(sp, i, g):
                for s in range(SIDE):
                    src = qparts[Q_PART[s]].rearrange("(h r) c -> r h c", r=DH)[:, bass.ds(g * HG, HG), i * S:(i + 1) * S]
                    sp.dma_start(qst[i][s * DH:(s + 1) * DH], src).then_inc(q_loaded[i], 16)

            def load_maxima(sp, i):
                for s in range(PARTS):
                    sp.dma_start(qst[i][SIDE * DH + s:SIDE * DH + s + 1].rearrange("o h s -> o (h s)"),
                                 mrow[:, s, :]).then_inc(rows_in, 16)

            NU = TB * (KEYS // 512) * (HG // 2)

            def max_unit(u, i, keys, base):
                qt, kb, hp = u // 16, (u % 16) // 2, u % 2
                for jj in range(2):
                    j = 2 * hp + jj
                    mm = nc.tensor.matmul(ps[:, base + jj, :], qst[i][0:SIDE * DH, j, qt * P:(qt + 1) * P],
                                          keys[0:SIDE * DH, j, kb * 512:(kb + 1) * 512], start=True, stop=True)
                return mm

            def max_reduce(u, base):
                qt, kb, hp = u // 16, (u % 16) // 2, u % 2
                return nc.vector.tensor_reduce(maxp[:, 2 * hp:2 * hp + 2, qt, kb], ps[:, base:base + 2, :], X, ALU.max)

            def max_total():
                return nc.vector.tensor_reduce(mneg[:], maxp[:].rearrange("p h t k -> p (h t) k"), X, ALU.max, negate=True)

            with ExitStack() as qs:
                qf = sb("qf", [P, KD, S], F32, qs)
                qsp = sb("qsp", [P, PARTS, KD, S], BF16, qs)

                def residual(dve, b):
                    for t in range(TB * b, TB * b + TB):
                        nc.vector.scalar_tensor_tensor(out=x[:, t, :], in0=acc[:, t, :], scalar=fac[:, b:b + 1],
                                                       in1=x[:, t, :], op0=ALU.mult, op1=ALU.add).then_inc(x_done, 1)

                def half_queries(m):
                    for k in range(KD):
                        mm = nc.tensor.matmul(ps[:, 2 + m, :], wqt[:, k, m * P:(m + 1) * P], xnT[:, k, :],
                                              start=(k == 0), stop=(k == KD - 1))
                    mm.then_inc(q_mm, 1)

                def take_queries(act, n):
                    if n:
                        act.wait_ge(q_split, 5 * n)
                    for m in range(KD):
                        act.wait_ge(q_mm, KD * n + m + 1)
                        nc.scalar.copy(qf[:, m, :], ps[:, 2 + m, :]).then_inc(q_taken, 1)

                def split_queries(eng, ops, n):
                    eng.wait_ge(q_taken, KD * (n + 1))
                    if n:
                        eng.wait_ge(q_stored, 16 * PARTS * n)
                    for s in range(PARTS):
                        ops.tensor_copy(qsp[:, s], qf[:]).then_inc(q_split, 1)
                        if s < PARTS - 1:
                            eng.wait_ge(q_split, 5 * n + 2 * s + 1)
                            ops.tensor_tensor(qf[:], qf[:], qsp[:, s], ALU.subtract).then_inc(q_split, 1)
                            eng.wait_ge(q_split, 5 * n + 2 * s + 2)

                def store_queries(sp, n, b):
                    sp.wait_ge(q_split, 5 * (n + 1))
                    for s in range(PARTS):
                        sp.dma_start(qparts[s].rearrange("(k p) c -> p k c", p=P)[:, :, b * S:(b + 1) * S],
                                     qsp[:, s]).then_inc(q_stored, 16)
                    sp.wait_ge(q_stored, 16 * PARTS * (n + 1))

                pooled = sb("pooled", [P, KD * NB], F32, qs)
                hp, gp, ephi, phi = (sb(n, [P, NB], F32, qs) for n in ("hp", "gp", "ephi", "phi"))
                phi_mm, ephi_done = sems("phi_mm ephi_done")

                with nc.Block() as block:
                    @block.sync
                    def _(sp):
                        load_keys(sp, 1, 0, keys_in0)
                        store_queries(sp, 0, 0)
                        load_queries(sp, 0, 0)
                        load_values(sp, 0)
                        sp.wait_ge(q_loaded[0], 16 * SIDE)
                        sp.wait_ge(keys_in0, 16 * SIDE)

                    @block.gpsimd
                    def _(pool):
                        norm_pool(pool, 0, main)
                        pool.wait_ge(main.rstd_done, 1)
                        nc.gpsimd.memset(kst[1][SIDE * DH:ROWS], 1.0).then_inc(ones_set, 1)
                        pool.wait_ge(ones_set, 1)
                        nc.gpsimd.memset(vcur[:, :, :, DH], 1.0)

                    @block.tensor
                    def _(pe):
                        for m in range(KD):
                            for b in range(NB):
                                mm = nc.tensor.matmul(ps[:, 0, m * NB + b:m * NB + b + 1], xn[:, b, m * P:(m + 1) * P],
                                                      ones[:, 0:1], start=True, stop=True)
                        mm.then_inc(phi_mm, 1)
                        pe.wait_ge(step, 1)
                        for m in range(KD):
                            mm = nc.tensor.matmul(ps[:, 1, 0:NB], wp1[:, m, :], pooled[:, m * NB:(m + 1) * NB],
                                                  start=(m == 0), stop=(m == KD - 1))
                        mm.then_inc(phi_mm, 1)
                        pe.wait_ge(step, 3)
                        nc.tensor.matmul(ps[:, 2, 0:NB], ones[:], gp[:], start=True, stop=True).then_inc(phi_mm, 1)
                        norm_tensor(pe, 0, main)
                        pe.wait_ge(main.taken, KD)
                        half_queries(0)
                        half_queries(1)

                    @block.scalar
                    def _(act):
                        act.wait_ge(step, 4)
                        nc.scalar.activation(ephi[:], phi[:], ACT.Exp, scale=-1.0).then_inc(ephi_done, 1)
                        norm_scalar(act, 0, main)
                        take_queries(act, 0)

                    @block.vector
                    def _(dve):
                        ch = Chain(dve)
                        dve.wait_ge(phi_mm, 1)
                        ch(nc.vector.tensor_scalar(pooled[:], ps[:, 0, 0:KD * NB], 1.0 / S, None, ALU.mult))
                        dve.wait_ge(phi_mm, 2)
                        ch(nc.vector.tensor_scalar(hp[:], ps[:, 1, 0:NB], bp1[:, 0:1], 0.0, ALU.add, ALU.max))
                        ch.wait()
                        ch(nc.vector.tensor_scalar(gp[:], hp[:], wp2[:, 0:1], None, ALU.mult))
                        dve.wait_ge(phi_mm, 3)
                        ch(nc.vector.tensor_scalar(phi[:], ps[:, 2, 0:NB], bp2[:, 0:1], None, ALU.add))
                        dve.wait_ge(ephi_done, 1)
                        ch(nc.vector.tensor_scalar(ephi[:], ephi[:], 1.0, None, ALU.add))
                        ch.wait()
                        ch(nc.vector.reciprocal(phi[:], ephi[:]))
                        ch.wait()
                        ch(nc.vector.tensor_scalar(fac[:], phi[:], 0.7, -0.8, ALU.is_gt, ALU.mult))
                        ch.wait()
                        ch(nc.vector.tensor_scalar(fac[:], fac[:], 1.0, None, ALU.add))
                        ch.wait()
                        residual(dve, 0)
                        dve.wait_ge(x_done, TB)
                        norm_vector(dve, 0, lambda t: x[:, t, :], main)
                        split_queries(dve, nc.vector, 0)
                clear(step, *query_sems, *main.norm_sems)

                STATS = {1 + 20 * n: n for n in range(NB - 1)}
                APPLY = {3 + 20 * n: n for n in range(NB - 1)}
                PIECE = {5 + 20 * n + (i if i < TB else 5 + 2 * (i - TB)): (n, i) for n in range(NB - 1) for i in range(TB + KD)}
                with nc.Block() as block:
                    @block.sync
                    def _(sp):
                        for n in range(NB - 1):
                            store_queries(sp, n, n + 1)
                            if n + 1 < NB - 1:
                                load_queries(sp, n + 1, 0)
                        sp.wait_ge(rows_ready, 1)
                        load_maxima(sp, 0)
                        sp.wait_ge(rows_in, 16 * PARTS)
                        for n in range(1, NB - 1):
                            sp.wait_ge(q_loaded[n], 16 * SIDE)
                        sp.wait_ge(v_loaded, 16)

                    @block.gpsimd
                    def _(pool):
                        for n in range(NB - 1):
                            norm_pool(pool, n, main)
                            split_queries(pool, nc.gpsimd, n)

                    @block.tensor
                    def _(pe):
                        for u in range(NU):
                            if u in PIECE:
                                n, i = PIECE[u]
                                if i < TB:
                                    turn_tile(pe, n, i, main)
                                elif i == TB:
                                    pe.wait_ge(main.taken, KD * (n + 1))
                                    if n:
                                        pe.wait_ge(q_taken, KD * n)
                                    half_queries(0)
                                else:
                                    half_queries(1)
                            if u >= 2:
                                pe.wait_ge(max_taken, u - 1)
                            max_unit(u, 0, kst[1], 4 + 2 * (u % 2)).then_inc(max_mm, 1)
                        pe.wait_ge(max_done, 1)
                        nc.tensor.transpose(ps[0:HG * TB, 0, 0:P], mneg[:], ident[:]).then_inc(max_turned, 1)

                    @block.scalar
                    def _(act):
                        for n in range(NB - 1):
                            norm_scalar(act, n, main)
                            take_queries(act, n)

                    @block.vector
                    def _(dve):
                        ch = Chain(dve)
                        for u in range(NU):
                            if u in STATS:
                                n = STATS[u]
                                residual(dve, n + 1)
                                dve.wait_ge(x_done, TB * (n + 1))
                                norm_stats(dve, n, lambda t: x[:, TB * (n + 1) + t, :], main)
                            if u in APPLY:
                                n = APPLY[u]
                                norm_apply(dve, n, lambda t: x[:, TB * (n + 1) + t, :], main)
                            dve.wait_ge(max_mm, u + 1)
                            max_reduce(u, 4 + 2 * (u % 2)).then_inc(max_taken, 1)
                        dve.wait_ge(max_taken, NU)
                        max_total().then_inc(max_done, 1)
                        dve.wait_ge(max_turned, 1)
                        src = ps[0:HG * TB, 0, 0:P]
                        for s in range(PARTS):
                            w = nc.vector.tensor_copy(mrow[:, s, :], src)
                            if s < PARTS - 1:
                                ch(w)
                                ch.wait()
                                ch(nc.vector.tensor_tensor(mres[:], src, mrow[:, s, :], ALU.subtract))
                                ch.wait()
                                src = mres[:]
                        w.then_inc(rows_ready, 1)
                clear(step, v_loaded, *q_loaded, *maxima_sems, *main.norm_sems)

            wgf, wuf = (sb(n, [P, KD, W1C], F32, l2, "right") for n in ("wgf", "wuf"))
            wdf = sb("wdf", [P, ND, D], F32, l2, "right")

            PIECES = 4
            AHEAD = 3

            def schedule(nexts):
                plan = [[] for _ in range(NB * NKT)]
                for i, nxt in enumerate(nexts):
                    end = (i + 1) * NKT - AHEAD
                    begin = i * NKT - (AHEAD if i else 0)
                    if nxt is not None:
                        for u in range(NU):
                            plan[begin + u * (end - begin) // NU].append(("max", nxt, u))
                        plan[end].append(("turn_max", nxt, 0))
                    if i:
                        plan[i * NKT + 2].append(("turn_out", i - 1, 0))
                return plan

            stage_in, score_mm, exp_done, keys_moved, values_moved, value_mm, sums_taken, unit_mm, unit_taken = group_sems = sems(
                "stage_in score_mm exp_done keys_moved values_moved value_mm sums_taken unit_mm unit_taken")

            def run_scores(g, last):
                nexts = [(i + 1) % NB if (i + 1 < NB or not last) else None for i in range(NB)]
                nth = lambda i: nexts.index(i) + 1
                plan = schedule(nexts)
                tail = ("turn_out", NB - 1, 0)

                with nc.Block() as block:
                    @block.sync
                    def _(sp):
                        load_queries(sp, NB - 1, g)
                        if last:
                            sp.dma_start(wgf[:], a["wg"].rearrange("(k p) e -> p k e", p=P)).then_inc(stage_in, 16)
                            sp.dma_start(wuf[:], a["wu"].rearrange("(k p) e -> p k e", p=P)).then_inc(stage_in, 16)
                            sp.dma_start(wdf[:, 0:ND - 1, :], a["wd"][0:(ND - 1) * P].rearrange("(k p) e -> p k e", p=P)
                                         ).then_inc(stage_in, 16)
                            sp.dma_start(wdf[0:DR, ND - 1, :], a["wd"][(ND - 1) * P:W1C]).then_inc(stage_in, 16)
                        if not last:
                            sp.wait_ge(keys_moved, PIECES)
                            load_keys(sp, 1, g + 1, stage_in)
                            sp.wait_ge(values_moved, PIECES)
                            load_values(sp, g + 1)
                        for i in range(NB):
                            if nexts[i] is not None:
                                sp.wait_ge(rows_ready, i + 1)
                                load_maxima(sp, nexts[i])
                                sp.wait_ge(rows_in, 16 * PARTS * (i + 1))
                            if not last and i < NB - 1:
                                sp.wait_ge(score_mm, NKT * HG * (i + 1))
                                load_queries(sp, i, g + 1)
                        if last:
                            sp.wait_ge(stage_in, 16 * 4)
                        else:
                            for i in range(NB - 1):
                                sp.wait_ge(q_loaded[i], 16 * SIDE)
                            sp.wait_ge(stage_in, 16 * SIDE)
                            sp.wait_ge(v_loaded, 16)

                    @block.gpsimd
                    def _(pool):
                        for n in range(PIECES):
                            tiles = slice(n * NKT // PIECES, (n + 1) * NKT // PIECES)
                            nc.gpsimd.tensor_copy(vcur[:, tiles, :, 0:DH], vnext[:, tiles, :].rearrange("p t (h d) -> p t h d", h=HG)
                                                  ).then_inc(values_moved, 1)

                    @block.tensor
                    def _(pe):
                        units = 0

                        def scores(i, kt, j):
                            n = (i * NKT + kt) * HG + j
                            if n >= 3:
                                pe.wait_ge(exp_done, n - 2)
                            if i == 0 and j == 0 and kt % (NKT // PIECES) == 0:
                                pe.wait_ge(keys_moved, kt // (NKT // PIECES) + 1)
                            nc.tensor.matmul(ps[:, n % 3, :], kst[0][:, j, kt * P:(kt + 1) * P], qst[i][:, j, :],
                                             start=True, stop=True).then_inc(score_mm, 1)

                        def values(i, kt):
                            G = i * NKT + kt
                            if i == 0 and kt % (NKT // PIECES) == 0:
                                pe.wait_ge(values_moved, kt // (NKT // PIECES) + 1)
                            pe.wait_ge(exp_done, HG * (G + 1))
                            if kt == 0 and i:
                                pe.wait_ge(sums_taken, i)
                            for j in range(HG):
                                mm = nc.tensor.matmul(ps[32 * j:32 * j + VC, 7, :], vcur[:, kt, j, :],
                                                      pring[:, (G % 2) * HG + j, :], start=(kt == 0), stop=(kt == NKT - 1))
                            mm.then_inc(value_mm, 1)

                        def unit(kind, i, u):
                            nonlocal units
                            base = 3 + 2 * (units % 2)
                            if units >= 2:
                                pe.wait_ge(unit_taken, units - 1)
                            if kind == "max":
                                if u == 0 and i == 0:
                                    pe.wait_ge(stage_in, 16 * SIDE)
                                    pe.wait_ge(q_loaded[0], 16 * SIDE)
                                if units < 16 and u % 2 == 0:
                                    pe.wait_ge(keys_moved, u // 2 * 512 // (KEYS // PIECES) + 1)
                                if u == 0 and i == NB - 1:
                                    pe.wait_ge(q_loaded[i], 16 * SIDE)
                                mm = max_unit(u, i, kst[1 if i == 0 else 0], base)
                            elif kind == "turn_max":
                                pe.wait_ge(max_done, nth(i))
                                mm = nc.tensor.transpose(ps[0:HG * TB, base, 0:P], mneg[:], ident[:])
                            else:
                                pe.wait_ge(sums_taken, i + 1)
                                for t in range(TB):
                                    mm = nc.tensor.transpose(ps[:, base, t * P:(t + 1) * P], osb[:, t * P:(t + 1) * P], ident[:])
                            mm.then_inc(unit_mm, 1)
                            units += 1

                        for i in range(NB):
                            if i:
                                pe.wait_ge(rows_in, 16 * PARTS * i)
                            for kt in range(NKT):
                                ev = plan[i * NKT + kt]
                                half = (len(ev) + 1) // 2
                                scores(i, kt, 0)
                                scores(i, kt, 1)
                                for e in ev[:half]:
                                    unit(*e)
                                scores(i, kt, 2)
                                scores(i, kt, 3)
                                for e in ev[half:]:
                                    unit(*e)
                                if kt:
                                    values(i, kt - 1)
                                elif i:
                                    values(i - 1, NKT - 1)
                        values(NB - 1, NKT - 1)
                        unit(*tail)

                    @block.scalar
                    def _(act):
                        for n in range(NB * NKT * HG):
                            G = n // HG
                            act.wait_ge(score_mm, n + 1)
                            if G >= 2 and n % HG == 0:
                                act.wait_ge(value_mm, G - 1)
                            nc.scalar.activation(pring[:, n % (2 * HG), :], ps[:, n % 3, :], ACT.Exp,
                                                 scale=float(DH) ** -0.5).then_inc(exp_done, 1)

                    @block.vector
                    def _(dve):
                        ch = Chain(dve)
                        units = 0
                        for n in range(PIECES):
                            cols = slice(n * KEYS // PIECES, (n + 1) * KEYS // PIECES)
                            nc.vector.tensor_copy(kst[0][:, :, cols], kst[1][:, :, cols]).then_inc(keys_moved, 1)

                        def unit(kind, i, u):
                            nonlocal units
                            base = 3 + 2 * (units % 2)
                            dve.wait_ge(unit_mm, units + 1)
                            if kind == "max":
                                max_reduce(u, base).then_inc(unit_taken, 1)
                                if u == NU - 1:
                                    dve.wait_ge(unit_taken, units + 1)
                                    max_total().then_inc(max_done, 1)
                            elif kind == "turn_max":
                                src = ps[0:HG * TB, base, 0:P]
                                if nth(i) > 1:
                                    dve.wait_ge(rows_in, 16 * PARTS * (nth(i) - 1))
                                for s in range(PARTS):
                                    part = nc.vector.tensor_copy(mrow[:, s, :], src)
                                    if s < PARTS - 1:
                                        ch(part)
                                        ch.wait()
                                        w = nc.vector.tensor_tensor(mres[:], src, mrow[:, s, :], ALU.subtract)
                                        if s == 0:
                                            w.then_inc(unit_taken, 1)
                                            dve.wait_ge(unit_taken, units + 1)
                                        else:
                                            ch(w)
                                            ch.wait()
                                        src = mres[:]
                                part.then_inc(rows_ready, 1)
                            else:
                                view = ps[:, base, :].rearrange("p (t h c) -> p t h c", t=TB, h=HG)
                                ch(nc.vector.reciprocal(orec[:], view[:, :, :, DH]))
                                ch.wait()
                                dst = acc[:, TB * i:TB * (i + 1), bass.ds(g * HG * DH, HG * DH)].rearrange(
                                    "p t (h d) -> p t h d", h=HG)
                                for t in range(TB):
                                    w = nc.vector.tensor_tensor(dst[:, t], view[:, t, :, 0:DH],
                                                                orec[:, t, :].unsqueeze(2).to_broadcast([P, HG, DH]), ALU.mult)
                                w.then_inc(unit_taken, 1)
                            units += 1

                        def take_sums(i):
                            dve.wait_ge(value_mm, NKT * (i + 1))
                            if i:
                                dve.wait_ge(unit_taken, out_units[i - 1] + 1)
                            nc.vector.tensor_copy(osb[:], ps[:, 7, :]).then_inc(sums_taken, 1)

                        flat = [e for ev in plan for e in ev] + [tail]
                        out_units = {e[1]: n for n, e in enumerate(flat) if e[0] == "turn_out"}
                        for i in range(NB):
                            for kt in range(NKT):
                                if i and kt == 1:
                                    take_sums(i - 1)
                                for e in plan[i * NKT + kt]:
                                    unit(*e)
                        take_sums(NB - 1)
                        unit(*tail)

            with nc.Fori(0, NG - 1) as g:
                run_scores(g, False)
                clear(step, v_loaded, *q_loaded, *maxima_sems, *group_sems)
            run_scores(NG - 1, True)
            clear(step)

        with ExitStack() as l3:
            CR = PARTS * (E1 + 1)
            wgate = sb("wgate", [P, KD, E1 + 1], F32, l3)
            (z, ez, zmax, zsum, zrec, probs, top, topi, topf, dtop, etop, tsum, trec, wtop, hit, whit) = choice_buffers(l3, TB)
            wgh, wgl, wuh, wul = (sb(n, [P, KD, W1C], F32R, l3) for n in ("wgh", "wgl", "wuh", "wul"))
            wdh, wdl = (sb(n, [P, ND, D], F32R, l3) for n in ("wdh", "wdl"))
            xh2, xl2 = ([sb(f"x{n}2{i}", [P, KD, S], F32R, l3) for i in range(2)] for n in "hl")
            combT = [sb(f"combT{i}", [CR, S], BF16, l3) for i in range(2)]
            owner = sb("owner", [CR, W1C], BF16, l3)
            comb = sb("comb", [P, TB, E1 + 1], F32, l3)
            cparts = sb("cparts", [P, TB, E1 + 1, PARTS], BF16, l3)
            cpartsf = sb("cpartsf", [P, TB, CR], F32, l3)
            ab = sb("ab", [P, TB, D], F32, l3)
            aT = sb("aT", [P, KD, S], F32, l3)
            zs = sb("zs", [P, TB], F32, l3)
            ezs = sb("ezs", [P, TB], F32, l3)
            gate_in, wd_split, high_split, owner_set = sems("gate_in wd_split high_split owner_set")
            (front_mm, front_taken, front_x, ab_done, z_ready1, ez_ready1, combT_done, gate_mm, bcast_mm, silu_done, m1_done, m2_done,
             high_done, low_done, down_mm, y_done, stored, cparts_done, yT_done, y_mm) = trip_sems = sems(
                "front_mm front_taken front_x ab_done z_ready1 ez_ready1 combT_done gate_mm bcast_mm silu_done m1_done m2_done "
                "high_taken low_taken down_mm y_done stored cparts_done yT_done y_mm")
            RING = 3
            BACK = {0: 0, 1: 1}
            FRONT = {2: 0, 3: 1, 4: 2, 5: 3, 7: 4, 8: 5, 9: 6, 13: 7}

            def trip(b, ffn, front, first, back):
                nb = b + 1
                nxt = 0 if first else 1
                rows_n = lambda t: x[:, bass.ds(TB * nb + t, 1), :].rearrange("p o d -> p (o d)")
                if first:
                    rows_n = lambda t: x[:, t, :]
                height = lambda c: P if c < ND - 1 else DR

                with nc.Block() as block:
                    @block.sync
                    def _(sp):
                        if first:
                            sp.dma_start(wgate[:], a["gateT"].rearrange("(k p) e -> p k e", p=P)).then_inc(gate_in, 16)
                            sp.wait_ge(gate_in, 16)
                        outputs = ([b - 1] if back else []) + ([b] if ffn and not front else [])
                        for n, batch in enumerate(outputs):
                            sp.wait_ge(y_done, 2 * (n + 1))
                            sp.dma_start(out.rearrange("(t p) d -> p t d", p=P)[:, bass.ds(TB * batch, TB), :], yout[:]
                                         ).then_inc(stored, 16)
                            sp.wait_ge(stored, 16 * (n + 1))

                    @block.gpsimd
                    def _(pool):
                        if front:
                            if not first:
                                nc.gpsimd.tensor_copy(ab[:], acc[:, bass.ds(TB * nb, TB), :]).then_inc(ab_done, 1)
                            norm_pool(pool, 0, main)
                        if first:
                            routed = owner[:, 0:E1 * H1].rearrange("r (e h) -> r e h", e=E1)
                            nc.gpsimd.memset(owner[:], 1.0).then_inc(owner_set, 1)
                            pool.wait_ge(owner_set, 1)
                            nc.gpsimd.affine_select(out=routed, in_=routed, compare_op=ALU.is_ge, fill=0.0, base=0,
                                                    pattern=[[-PARTS, E1], [0, H1]], channel_multiplier=1).then_inc(owner_set, 1)
                            nc.gpsimd.affine_select(out=owner[:, E1 * H1:W1C], in_=owner[:, E1 * H1:W1C], compare_op=ALU.is_ge,
                                                    fill=0.0, base=-PARTS * E1, pattern=[[0, HS1]],
                                                    channel_multiplier=1).then_inc(owner_set, 1)
                            pool.wait_ge(owner_set, 3)
                            nc.gpsimd.affine_select(out=routed, in_=routed, compare_op=ALU.is_ge, fill=0.0, base=PARTS - 1,
                                                    pattern=[[PARTS, E1], [0, H1]], channel_multiplier=-1).then_inc(owner_set, 1)
                            pool.wait_ge(wd_split, 2)
                            nc.gpsimd.tensor_tensor(wdl[:, 0:ND - 1], wdf[:, 0:ND - 1], f32(wdh[:, 0:ND - 1]), ALU.subtract)
                            nc.gpsimd.tensor_tensor(wdl[0:DR, ND - 1], wdf[0:DR, ND - 1], f32(wdh[0:DR, ND - 1]), ALU.subtract)

                    @block.tensor
                    def _(pe):
                        def three(out_, ah, al, bh, bl, begin, end):
                            nc.tensor.matmul(out_, ah, bh, start=begin, stop=False)
                            nc.tensor.matmul(out_, ah, bl, start=False, stop=False)
                            return nc.tensor.matmul(out_, al, bh, start=False, stop=end)

                        def gate_up(c):
                            r = height(c)
                            if c >= 2:
                                pe.wait_ge(m1_done, c - 1)
                            for wh, wl, bank in ((wgh, wgl, 0), (wuh, wul, 2)):
                                for k in range(KD):
                                    col = slice(c * P, c * P + r)
                                    mm = three(ps[0:r, bank + c % 2, :], wh[:, k, col], wl[:, k, col], xh2[0][:, k, :],
                                               xl2[0][:, k, :], k == 0, k == KD - 1)
                                mm.then_inc(gate_mm, 1)

                        def weights(c):
                            if c:
                                pe.wait_ge(m2_done, c)
                            nc.tensor.matmul(ps[0:height(c), 4, :], owner[:, c * P:c * P + height(c)], combT[0][:],
                                             start=True, stop=True).then_inc(bcast_mm, 1)

                        def down(c):
                            r = height(c)
                            pe.wait_ge(low_done, c + 1)
                            for m in range(KD):
                                mm = three(ps[:, 5 + m, :], wdh[0:r, c, m * P:(m + 1) * P], wdl[0:r, c, m * P:(m + 1) * P],
                                           hh[0:r, c % RING, :], hl[0:r, c % RING, :], c == 0, c == ND - 1)
                            mm.then_inc(down_mm, 1)

                        def turn_back(m, bank):
                            for t in range(TB):
                                mm = nc.tensor.transpose(ps[:, bank, t * P:(t + 1) * P], yT[:, m, t * P:(t + 1) * P], ident[:])
                            mm.then_inc(y_mm, 1)

                        def front_step(n):
                            attn = acc if first else ab
                            if n == 0:
                                if not first:
                                    pe.wait_ge(ab_done, 1)
                                if back:
                                    pe.wait_ge(y_done, KD)
                            elif n == 7:
                                pe.wait_ge(cparts_done, 1)
                            else:
                                pe.wait_ge(front_taken, n)
                            if n in (0, 1):
                                for t in range(TB):
                                    mm = nc.tensor.transpose(ps[:, 7, t * P:(t + 1) * P], attn[:, t, n * P:(n + 1) * P], ident[:])
                            elif n in (2, 3):
                                for t in range(2 * (n - 2), 2 * (n - 2) + 2):
                                    for k in range(KD):
                                        mm = nc.tensor.matmul(ps[:, 7, (t % 2) * D:(t % 2 + 1) * D], aT[:, k, t * P:(t + 1) * P],
                                                              wot[:, k, :], start=(k == 0), stop=(k == KD - 1))
                            elif n in (4, 5):
                                pe.wait_ge(main.norm_done, TB)
                                for t in range(TB):
                                    mm = nc.tensor.transpose(ps[:, 7, t * P:(t + 1) * P], xn[:, t, (n - 4) * P:(n - 3) * P], ident[:])
                            elif n == 6:
                                if first:
                                    pe.wait_ge(gate_in, 16)
                                for t in range(TB):
                                    for k in range(KD):
                                        mm = nc.tensor.matmul(ps[:, 7, t * 16:t * 16 + E1 + 1], xnT[:, k, t * P:(t + 1) * P],
                                                              wgate[:, k, :], start=(k == 0), stop=(k == KD - 1))
                            else:
                                for t in range(TB):
                                    mm = nc.tensor.transpose(ps[0:CR, 7, t * P:(t + 1) * P], cpartsf[:, t, :], ident[:])
                            mm.then_inc(front_mm, 1)

                        if not ffn:
                            for n in range(8):
                                front_step(n)
                            return
                        for c in range(ND):
                            gate_up(c)
                            weights(c)
                            if back and c in BACK:
                                if BACK[c]:
                                    pe.wait_ge(y_done, BACK[c])
                                turn_back(BACK[c], 7)
                            if front and c in FRONT:
                                front_step(FRONT[c])
                            if c >= 2:
                                down(c - 2)
                        down(ND - 2)
                        down(ND - 1)
                        if not front:
                            pe.wait_ge(yT_done, KD)
                            pe.wait_ge(m1_done, ND)
                            turn_back(0, 0)
                            turn_back(1, 1)

                    @block.scalar
                    def _(act):
                        def silu(c):
                            act.wait_ge(gate_mm, 2 * c + 1)
                            if c >= 2:
                                act.wait_ge(m2_done, c - 1)
                            r = height(c)
                            nc.scalar.activation(sg[0:r, c % 2, :], ps[0:r, c % 2, :], ACT.Silu).then_inc(silu_done, 1)

                        def high(c):
                            act.wait_ge(m2_done, c + 1)
                            if c >= RING:
                                act.wait_ge(down_mm, c - RING + 1)
                            r = height(c)
                            nc.scalar.copy(hh[0:r, c % RING, :], hf[0:r, c % 2, :]).then_inc(high_done, 1)

                        def take(n):
                            act.wait_ge(front_mm, n + 1)
                            dst = {0: aT, 1: aT, 4: xnT, 5: xnT}.get(n)
                            if n == 7:
                                nc.scalar.copy(combT[nxt][:], ps[0:CR, 7, :]).then_inc(combT_done, 1)
                            else:
                                nc.scalar.copy(dst[:, n % 2, :], ps[:, 7, :]).then_inc(front_taken, 1)

                        def exps():
                            act.wait_ge(z_ready1, 1)
                            nc.scalar.activation(ez[:, 0:TB, 0:E1], z[:, 0:TB, 0:E1], ACT.Exp).then_inc(ez_ready1, 1)
                            nc.scalar.activation(ezs[:], zs[:], ACT.Exp, scale=-1.0).then_inc(ez_ready1, 1)

                        if not ffn:
                            take(0)
                            take(1)
                            nc.scalar.copy(wgh[:], wgf[:]).then_inc(high_split, 1)
                            nc.scalar.copy(wdh[:, 0:ND - 1], wdf[:, 0:ND - 1]).then_inc(wd_split, 1)
                            nc.scalar.copy(wdh[0:DR, ND - 1], wdf[0:DR, ND - 1]).then_inc(wd_split, 1)
                            nc.scalar.copy(wuh[:], wuf[:]).then_inc(high_split, 1)
                            take(4)
                            take(5)
                            exps()
                            take(7)
                            return
                        for c in range(ND):
                            silu(c)
                            if c:
                                high(c - 1)
                            n = FRONT.get(c)
                            if front and n in (0, 1, 4, 5, 7):
                                take(n)
                            if front and n == 6:
                                exps()
                        high(ND - 1)
                        act.wait_ge(down_mm, ND)
                        nc.scalar.copy(yT[:, 0, :], ps[:, 5, :]).then_inc(yT_done, 1)

                    @block.vector
                    def _(dve):
                        ch = Chain(dve)

                        def gated(c):
                            r = height(c)
                            dve.wait_ge(silu_done, c + 1)
                            dve.wait_ge(gate_mm, 2 * c + 2)
                            nc.vector.tensor_tensor(sg[0:r, c % 2, :], sg[0:r, c % 2, :], ps[0:r, 2 + c % 2, :], ALU.mult).then_inc(m1_done, 1)
                            dve.wait_ge(m1_done, c + 1)
                            dve.wait_ge(bcast_mm, c + 1)
                            if c >= 2:
                                dve.wait_ge(low_done, c - 1)
                            nc.vector.tensor_tensor(hf[0:r, c % 2, :], sg[0:r, c % 2, :], ps[0:r, 4, :], ALU.mult).then_inc(m2_done, 1)

                        def low(c):
                            r = height(c)
                            dve.wait_ge(high_done, c + 1)
                            nc.vector.tensor_tensor(hl[0:r, c % RING, :], hf[0:r, c % 2, :], f32(hh[0:r, c % RING, :]),
                                                    ALU.subtract).then_inc(low_done, 1)

                        def add_projection(n):
                            dve.wait_ge(front_mm, n + 1)
                            for t in range(2 * (n - 2), 2 * (n - 2) + 2):
                                w = nc.vector.tensor_tensor(rows_n(t), rows_n(t), ps[:, 7, (t % 2) * D:(t % 2 + 1) * D], ALU.add)
                                if t % 2 == 0:
                                    w.then_inc(front_x, 1)
                            w.then_inc(front_taken, 1)

                        def next_stats():
                            dve.wait_ge(front_x, 2)
                            dve.wait_ge(front_taken, 4)
                            norm_stats(dve, 0, rows_n, main)

                        def next_parts():
                            dve.wait_ge(front_taken, 6)
                            ch(nc.vector.tensor_copy(xh2[nxt][:], xnT[:]))
                            ch.wait()
                            ch(nc.vector.tensor_tensor(xl2[nxt][:], xnT[:], f32(xh2[nxt][:]), ALU.subtract))

                        def route_start():
                            dve.wait_ge(front_mm, 7)
                            lg = ps[:, 7, 0:TB * 16].rearrange("p (i e) -> p i e", e=16)
                            ch(nc.vector.tensor_copy(zs[:], lg[:, :, E1]))
                            nc.vector.tensor_copy(z[:, 0:TB, 0:E1], lg[:, :, 0:E1]).then_inc(front_taken, 1)
                            dve.wait_ge(front_taken, 7)
                            choose_start(ch, TB, E1, z_ready1)

                        def combine():
                            ch(nc.vector.tensor_tensor(tsum[:], top[:, :, 0], top[:, :, 1], ALU.add))
                            ch.wait()
                            ch(nc.vector.reciprocal(trec[:], tsum[:]))
                            ch.wait()
                            ch(nc.vector.tensor_tensor(wtop[:, :, 0:TOP1], top[:, :, 0:TOP1], spread(trec, TB, TOP1), ALU.mult))
                            ch.wait()
                            for k in range(TOP1):
                                ch(nc.vector.tensor_tensor(whit[:, k, :, 0:E1], hit[:, k, :, 0:E1],
                                                           wtop[:, :, k:k + 1].to_broadcast([P, TB, E1]), ALU.mult))
                            ch.wait()
                            ch(nc.vector.tensor_tensor(comb[:, :, 0:E1], whit[:, 0, :, 0:E1], whit[:, 1, :, 0:E1], ALU.add))
                            dve.wait_ge(ez_ready1, 2)
                            ch(nc.vector.tensor_scalar(ezs[:], ezs[:], 1.0, None, ALU.add))
                            ch.wait()
                            ch(nc.vector.reciprocal(comb[:, :, E1], ezs[:]))

                        def combine_parts():
                            for s in range(PARTS):
                                ch.wait()
                                ch(nc.vector.tensor_copy(cparts[:, :, :, s], comb[:]))
                                ch.wait()
                                if s < PARTS - 1:
                                    ch(nc.vector.tensor_tensor(comb[:], comb[:], cparts[:, :, :, s], ALU.subtract))
                            nc.vector.tensor_copy(cpartsf[:], cparts[:].rearrange("p t e s -> p t (e s)")).then_inc(cparts_done, 1)

                        if not ffn:
                            def low_parts(n, k, hi, lo, src):
                                dve.wait_ge(high_split, n)
                                nc.vector.tensor_tensor(lo[:, k, :], src[:, k, :], f32(hi[:, k, :]), ALU.subtract)

                            add_projection(2)
                            add_projection(3)
                            next_stats()
                            norm_apply(dve, 0, rows_n, main)
                            low_parts(1, 0, wgh, wgl, wgf)
                            next_parts()
                            route_start()
                            low_parts(1, 1, wgh, wgl, wgf)
                            choose_top(dve, ch, TB, E1, ez_ready1)
                            choose_hits(ch, TB, E1, TOP1)
                            combine()
                            combine_parts()
                            low_parts(2, 0, wuh, wul, wuf)
                            low_parts(2, 1, wuh, wul, wuf)
                            return
                        def result(n, m, bank):
                            batch = b if n is None else n
                            dve.wait_ge(y_mm, results.pop(0))
                            nc.vector.tensor_tensor(yout[:, :, m * P:(m + 1) * P], x[:, bass.ds(TB * batch, TB), m * P:(m + 1) * P],
                                                    ps[:, bank, :].rearrange("p (t d) -> p t d", t=TB), ALU.add).then_inc(y_done, 1)

                        results = list(range(1, 5))
                        for c in range(ND):
                            gated(c)
                            if c:
                                low(c - 1)
                            if back and c in BACK:
                                result(b - 1, BACK[c], 7)
                            if front:
                                if c == 4:
                                    add_projection(2)
                                elif c == 5:
                                    add_projection(3)
                                    next_stats()
                                elif c == 6:
                                    norm_apply(dve, 0, rows_n, main)
                                elif c == 8:
                                    next_parts()
                                elif c == 9:
                                    route_start()
                                elif c == 10:
                                    choose_top(dve, ch, TB, E1, ez_ready1)
                                elif c == 11:
                                    choose_hits(ch, TB, E1, TOP1)
                                    combine()
                                elif c == 12:
                                    combine_parts()
                        low(ND - 1)
                        if front:
                            dve.wait_ge(gate_mm, 2 * ND)
                            nc.vector.tensor_copy(xh2[0][:], f32(xh2[1][:]))
                            nc.vector.tensor_copy(xl2[0][:], f32(xl2[1][:]))
                            dve.wait_ge(bcast_mm, ND)
                            dve.wait_ge(combT_done, 1)
                            nc.vector.tensor_copy(combT[0][:], combT[1][:])
                        dve.wait_ge(down_mm, ND)
                        nc.vector.tensor_copy(yT[:, 1, :], ps[:, 6, :]).then_inc(yT_done, 1)
                        if not front:
                            if back:
                                dve.wait_ge(stored, 16)
                            result(None, 0, 0)
                            result(None, 1, 1)

            trip(-1, False, True, True, False)
            clear(step, *trip_sems, *main.norm_sems)
            l2.close()
            sg = sb("sg", [P, 2, S], F32, l3)
            hf = sb("hf1", [P, 2, S], F32, l3)
            hh, hl = (sb(n, [P, RING, S], F32R, l3) for n in ("hh", "hl"))
            yT = sb("yT", [P, KD, S], F32, l3)
            yout = sb("yout", [P, TB, D], F32, l3)
            trip(0, True, True, False, False)
            clear(step, *trip_sems, *main.norm_sems)
            with nc.Fori(0, NB - 2) as b:
                trip(b + 1, True, True, False, True)
                clear(step, *trip_sems, *main.norm_sems)
            trip(NB - 1, True, False, False, True)


def kernel(**inputs):
    import numpy as _np
    import concourse.bacc as _bacc
    from concourse import mybir as _mybir
    from concourse.bass_utils import run_bass_kernel_spmd as _run

    n = {k: _np.asarray(v) for k, v in inputs.items()}
    arrays = {k: n[k] for k in ("L0_attn_W_q", "L0_attn_W_k", "L0_attn_W_v", "L0_attn_W_o", "L0_ffn_Wr", "L0_ffn_br",
                                "L0_ffn_w1", "L0_ffn_w2", "L0_ffn_b2", "L0_ffn_Wp1", "L0_ffn_bp1", "L0_ffn_Wp2",
                                "L0_ffn_bp2")}
    arrays["x"] = n["L0_attn_x"].reshape(NB * S, D)
    arrays["b1T"] = n["L0_ffn_b1"].reshape(E0 * NI, P).T
    arrays["kT"] = n["L1_attn_kv_k"].reshape(KEYS, D).T
    arrays["v"] = n["L1_attn_kv_v"].reshape(KEYS, D)
    arrays["wqT"] = n["L1_attn_Wq"].T
    arrays["woT"] = n["L1_attn_Wo"].T
    arrays["gateT"] = _np.concatenate([n["L1_ffn_gate_w"], n["L1_ffn_shgate_w"][None]]).T
    for name, w, sh in (("wg", "w_gate", "shw_gate"), ("wu", "w_up", "shw_up")):
        arrays[name] = _np.concatenate([n["L1_ffn_" + w].transpose(1, 0, 2).reshape(D, E1 * H1), n["L1_ffn_" + sh]], 1)
    arrays["wd"] = _np.concatenate([n["L1_ffn_w_down"].reshape(E1 * H1, D), n["L1_ffn_shw_down"]])

    nc = _bacc.Bacc("TRN2", target_bir_lowering=False, num_devices=1)
    feed, aps = {}, {}
    for k, v in arrays.items():
        v = _np.ascontiguousarray(v)
        feed[f"in_{k}"] = v
        aps[k] = nc.dram_tensor(f"in_{k}", v.shape, _mybir.dt.from_np(v.dtype), kind="ExternalInput").ap()
    out = nc.dram_tensor("out_x", (NB * S, D), _mybir.dt.float32, kind="ExternalOutput").ap()
    build(nc, aps, out)
    r = _run(nc, [feed], core_ids=[0])
    return r.results[0]["out_x"].reshape(NB, S, D)
```

```python
from contextlib import ExitStack

import concourse.bass as bass
from concourse import mybir

F32 = mybir.dt.float32
F32R = mybir.dt.float32r
BF16 = mybir.dt.bfloat16
U32 = mybir.dt.uint32
I32 = mybir.dt.int32
ACT = mybir.ActivationFunctionType
ALU = mybir.AluOpType
X = mybir.AxisListType.X

P = 128
D = 256
KD = D // P
NB = 4
S = 512
NT = NB * S // P
TB = S // P
EPS = 1e-5

E0, TOP0, I0 = 12, 3, 640
NI = I0 // P

HEADS, DH = 16, 16
KEYS = 4096
NKT = KEYS // P
HG = 4
NG = HEADS // HG
PARTS = 3
SIDE = 6
ROWS = SIDE * DH + PARTS
Q_PART = [0, 1, 2, 0, 1, 0]
K_PART = [0, 0, 0, 1, 1, 2]
VC = DH + 1

E1, TOP1, H1, HS1 = 8, 2, 176, 352
W1C = E1 * H1 + HS1
NSL = W1C // HS1
ND = -(-W1C // P)
DR = W1C - (ND - 1) * P


def build(nc, a, out):
    with ExitStack() as ctx:
        arrivals = ctx.enter_context(ExitStack())

        def sb(name, shape, dt=F32, stack=ctx, side=None):
            return stack.enter_context(nc.sbuf_tensor(name, shape, dt, side=side))

        def sem(name):
            return ctx.enter_context(nc.semaphore(name))

        ps = ctx.enter_context(nc.psum_tensor("banks", [P, 8, 512], F32))
        kparts = nc.dram_tensor("key_parts", [PARTS, D, KEYS], BF16, kind="Internal").ap()
        qparts = nc.dram_tensor("query_parts", [PARTS, D, NB * S], BF16, kind="Internal").ap()

        x = sb("x", [P, NT, D])
        ident = sb("ident", [P, P])
        xn = sb("xn", [P, TB, D])
        xnT = sb("xnT", [P, KD, S])
        mhalf = sb("mhalf", [P, TB])
        acc = sb("acc", [P, NT, D])
        fac = sb("fac", [P, NB])
        iota_i = sb("iota_i", [P, E0], I32)
        iota = sb("iota", [P, E0])
        ones = sb("ones", [P, P])
        wp1 = sb("wp1", [P, KD, P])
        bp1, wp2, bp2 = (sb(n, [P, 1]) for n in ("bp1", "wp2", "bp2"))
        wot = sb("wot", [P, KD, D])
        wqt = sb("wqt", [P, KD, D])

        x_loaded = [sem(f"x_loaded{h}") for h in range(2)]
        setup_done, qkv_in, load_w = sem("setup_done"), sem("qkv_in"), sem("load_w")
        step = sem("vector_step")

        def sems(names):
            return [sem(n) for n in names.split()]

        def clear(*used):
            with nc.Block() as block:
                @block.gpsimd
                def _(pool):
                    for s in used[0::4]:
                        pool.sem_clear(s)

                @block.sync
                def _(sp):
                    for s in used[1::4]:
                        sp.sem_clear(s)

                @block.scalar
                def _(act):
                    for s in used[2::4]:
                        act.sem_clear(s)

                @block.vector
                def _(dve):
                    for s in used[3::4]:
                        dve.sem_clear(s)

        class Chain:
            def __init__(self, dve):
                self.dve, self.n = dve, 0

            def __call__(self, ins):
                ins.then_inc(step, 1)
                self.n += 1

            def wait(self):
                self.dve.wait_ge(step, self.n)

        def f32(t):
            return t.bitcast(F32)

        class Lane:
            def __init__(self, tag, bank, xn, xnT, stack):
                self.bank, self.xn, self.xnT = bank, xn, xnT
                self.stats = sb("stats" + tag, [P, TB, 6], F32, stack)
                self.meanvar = sb("meanvar" + tag, [P, TB, 2], F32, stack)
                self.vareps = sb("vareps" + tag, [P, TB], F32, stack)
                self.rstd = sb("rstd" + tag, [P, TB], F32, stack)
                self.stats_done, self.aggr_done, self.var_done, self.rstd_done, self.norm_done, self.turned, self.taken = self.norm_sems = (
                    [sem(n + tag) for n in ("ln_stats", "ln_aggr", "ln_var", "ln_rstd", "ln_norm", "ln_turned", "ln_taken")])

        def norm_stats(dve, n, rows, L):
            for t in range(TB):
                nc.vector.bn_stats(L.stats[:, t, :], rows(t)).then_inc(L.stats_done, 1)
            dve.wait_ge(L.stats_done, TB * (n + 1))
            for t in range(TB):
                nc.vector.bn_aggr(L.meanvar[:, t, :], L.stats[:, t, :]).then_inc(L.aggr_done, 1)
            dve.wait_ge(L.aggr_done, TB * (n + 1))
            nc.vector.tensor_scalar(L.vareps[:], L.meanvar[:, :, 1], EPS, None, ALU.add).then_inc(L.var_done, 1)

        def norm_apply(dve, n, rows, L):
            dve.wait_ge(L.rstd_done, n + 1)
            if n:
                dve.wait_ge(L.turned, n)
            for t in range(TB):
                nc.vector.tensor_scalar(L.xn[:, t, :], rows(t), L.meanvar[:, t, 0:1], L.rstd[:, t:t + 1],
                                        ALU.subtract, ALU.mult).then_inc(L.norm_done, 1)

        def norm_vector(dve, n, rows, L):
            norm_stats(dve, n, rows, L)
            norm_apply(dve, n, rows, L)

        def norm_pool(pool, n, L):
            pool.wait_ge(L.var_done, n + 1)
            nc.gpsimd.tensor_tensor(L.rstd[:], L.vareps[:], mhalf[:], ALU.pow).then_inc(L.rstd_done, 1)

        def norm_scalar(act, n, L):
            act.wait_ge(L.turned, n + 1)
            for k in range(KD):
                nc.scalar.copy(L.xnT[:, k, :], ps[:, L.bank + k, :]).then_inc(L.taken, 1)

        def turn_tile(pe, n, t, L):
            pe.wait_ge(L.norm_done, TB * n + t + 1)
            for k in range(KD):
                mm = nc.tensor.transpose(ps[:, L.bank + k, t * P:(t + 1) * P], L.xn[:, t, k * P:(k + 1) * P], ident[:])
            if t == TB - 1:
                mm.then_inc(L.turned, 1)

        def norm_tensor(pe, n, L):
            for t in range(TB):
                turn_tile(pe, n, t, L)

        main = Lane("", 0, xn, xnT, ctx)

        def choice_buffers(stack, nt):
            shapes = dict(z=[nt, E0], ez=[nt, E0], zmax=[nt], zsum=[nt], zrec=[nt], probs=[nt, E0], top=[nt, 8], topi=[nt, 8],
                          topf=[nt, 8], dtop=[nt, TOP0], etop=[nt, TOP0], tsum=[nt], trec=[nt], wtop=[nt, TOP0],
                          hit=[TOP0, nt, E0], whit=[TOP0, nt, E0])
            return [sb(f"{n}_{nt}", [P] + sh, U32 if n == "topi" else F32, stack) for n, sh in shapes.items()]

        def spread(t, nt, ne):
            return t[:, 0:nt].unsqueeze(2).to_broadcast([P, nt, ne])

        def choose_start(ch, nt, ne, z_ready):
            if ch.n:
                ch.wait()
            ch(nc.vector.tensor_reduce(zmax[:, 0:nt], z[:, 0:nt, 0:ne], X, ALU.max))
            ch.wait()
            nc.vector.tensor_tensor(z[:, 0:nt, 0:ne], z[:, 0:nt, 0:ne], spread(zmax, nt, ne), ALU.subtract).then_inc(z_ready, 1)

        def choose_top(dve, ch, nt, ne, ez_ready):
            dve.wait_ge(ez_ready, 1)
            ch(nc.vector.tensor_reduce(zsum[:, 0:nt], ez[:, 0:nt, 0:ne], X, ALU.add))
            ch.wait()
            ch(nc.vector.reciprocal(zrec[:, 0:nt], zsum[:, 0:nt]))
            ch.wait()
            ch(nc.vector.tensor_tensor(probs[:, 0:nt, 0:ne], ez[:, 0:nt, 0:ne], spread(zrec, nt, ne), ALU.mult))
            ch.wait()
            for i in range(nt):
                ch(nc.vector.max(top[:, i, :], probs[:, i, 0:ne]))
            ch.wait()

        def choose_hits(ch, nt, ne, ntop):
            for i in range(nt):
                ch(nc.vector.max_index(topi[:, i, :], top[:, i, :], probs[:, i, 0:ne]))
            ch.wait()
            ch(nc.vector.tensor_copy(topf[:, 0:nt], topi[:, 0:nt]))
            ch.wait()
            for k in range(ntop):
                ch(nc.vector.tensor_tensor(hit[:, k, 0:nt, 0:ne], iota[:, 0:ne].unsqueeze(1).to_broadcast([P, nt, ne]),
                                           topf[:, 0:nt, k:k + 1].to_broadcast([P, nt, ne]), ALU.is_equal))

        with ExitStack() as l0:
            def s0(name, shape, dt=F32):
                return sb(name, shape, dt, l0)

            (z, ez, zmax, zsum, zrec, probs, top, topi, topf, dtop, etop, tsum, trec, wtop, hit, whit) = choice_buffers(l0, NT)
            wq, wk, wv, wo = (s0(n, [P, KD, D]) for n in ("wq", "wk", "wv", "wo"))
            wr = s0("wr", [P, KD, E0])
            br = s0("br", [P, E0])
            b1 = s0("b1", [P, E0 * NI])
            b2 = s0("b2", [E0, D])
            xh, xl = (s0(n, [P, KD, NB * S], F32R) for n in ("xh", "xl"))
            chosen = s0("chosen", [P, NT, 2 * E0])
            w1f = s0("w1f", [P, KD, I0])
            w2f = s0("w2f", [P, NI, D])
            w1h, w1l = ([s0(f"w1{n}0", [P, KD, I0], F32R)] for n in "hl")
            w2h, w2l = ([s0(f"w2{n}0", [P, NI, D], F32R)] for n in "hl")

            def load_expert(sp, e, done):
                sp.dma_start(w1f[:], a["L0_ffn_w1"][e].rearrange("(k p) i -> p k i", p=P)).then_inc(done, 16)
                sp.dma_start(w2f[:], a["L0_ffn_w2"][e].rearrange("(k p) i -> p k i", p=P)).then_inc(done, 16)

            def split_expert(eng, ops, i, done, before):
                ops.tensor_copy(w1h[i][:], w1f[:]).then_inc(done, 1)
                ops.tensor_copy(w2h[i][:], w2f[:]).then_inc(done, 1)
                eng.wait_ge(done, before + 2)
                ops.tensor_tensor(w1l[i][:], w1f[:], f32(w1h[i][:]), ALU.subtract).then_inc(done, 1)
                ops.tensor_tensor(w2l[i][:], w2f[:], f32(w2h[i][:]), ALU.subtract).then_inc(done, 1)

            expert0_in, first_split = sems("expert0_in first_split")
            WEIGHTS = 11

            def load_x(sp, h):
                tiles = slice(h * NT // 2, (h + 1) * NT // 2)
                sp.dma_start(x[:, tiles, :], a["x"].rearrange("(t p) d -> p t d", p=P)[:, tiles, :]).then_inc(x_loaded[h], 16)

            with nc.Block() as block:
                @block.sync
                def _(sp):
                    load_x(sp, 0)
                    for w, n in ((wq, "L0_attn_W_q"), (wk, "L0_attn_W_k"), (wv, "L0_attn_W_v")):
                        sp.dma_start(w[:], a[n].rearrange("(k p) e -> p k e", p=P)).then_inc(qkv_in, 16)
                    load_x(sp, 1)
                    for w, n in ((wo, "L0_attn_W_o"), (wr, "L0_ffn_Wr"), (wp1, "L0_ffn_Wp1"), (wqt, "wqT"), (wot, "woT")):
                        sp.dma_start(w[:], a[n].rearrange("(k p) e -> p k e", p=P)).then_inc(load_w, 16)
                    sp.dma_start(b1[:], a["b1T"]).then_inc(load_w, 16)
                    sp.dma_start(b2[:], a["L0_ffn_b2"]).then_inc(load_w, 16)
                    sp.dma_start(br[:], a["L0_ffn_br"].partition_broadcast(P)).then_inc(load_w, 16)
                    sp.dma_start(bp1[:], a["L0_ffn_bp1"].rearrange("(p o) -> p o", o=1)).then_inc(load_w, 16)
                    sp.dma_start(wp2[:], a["L0_ffn_Wp2"]).then_inc(load_w, 16)
                    sp.dma_start(bp2[:], a["L0_ffn_bp2"].partition_broadcast(P)).then_inc(load_w, 16)
                    load_expert(sp, 0, expert0_in)

                @block.gpsimd
                def _(pool):
                    nc.gpsimd.memset(ident[:], 0.0).then_inc(setup_done, 1)
                    pool.wait_ge(setup_done, 1)
                    nc.gpsimd.affine_select(out=ident[:], in_=ident[:], compare_op=ALU.not_equal, fill=1.0, base=0,
                                            pattern=[[-1, P]], channel_multiplier=1).then_inc(setup_done, 1)
                    nc.gpsimd.iota(iota_i[:], pattern=[[1, E0]], base=0, channel_multiplier=0).then_inc(setup_done, 1)

                @block.vector
                def _(dve):
                    nc.vector.memset(ones[:], 1.0)
                    dve.wait_ge(setup_done, 3)
                    nc.vector.tensor_copy(iota[:], iota_i[:])
                    nc.vector.memset(mhalf[:], -0.5)

            with ExitStack() as at:
                scale = float(D) ** -0.5

                class AttnLane(Lane):
                    def __init__(self, c):
                        tag = str(c)
                        xn_, xnT_ = (xn, xnT) if c == 0 else (sb("xn1", [P, TB, D], F32, at), sb("xnT1", [P, KD, S], F32, at))
                        super().__init__(tag, 4 * c, xn_, xnT_, at)
                        self.qT, self.kT = (sb(n + tag, [P, KD, S], F32, at) for n in ("qT", "kT"))
                        self.oT = self.qT
                        self.v = sb("v" + tag, [P, TB, D], F32, at)
                        self.pm = sb("pm" + tag, [P, TB, S], F32, at)
                        self.pT = sb("pT" + tag, [P, TB, S], F32, at)
                        self.nmax, self.rsum, self.rrec = (sb(n + tag, [P, TB], F32, at) for n in ("nmax", "rsum", "rrec"))
                        (self.q_mm, self.k_mm, self.v_mm, self.score_mm, self.pT_mm, self.pv_mm, self.proj_mm, self.route_mm,
                         self.q_taken, self.k_taken, self.v_taken, self.nmax_done, self.p_done, self.pT_act, self.pT_dve,
                         self.o_taken, self.rrec_done, self.x_done, self.xh_done) = self.attn_sems = sems(" ".join(n + tag for n in (
                             "q_mm k_mm v_mm score_mm pT_mm pv_mm proj_mm route_mm q_taken k_taken v_taken nmax_done "
                             "p_done pT_act pT_dve o_taken rrec_done x_done xh_done").split()))

                lanes = [AttnLane(c) for c in range(2)]
                assert NB % 2 == 0

                with nc.Fori(0, NB // 2) as b2i:
                    def rows_of(c):
                        return lambda t: x[:, bass.ds(2 * TB * b2i + TB * c + t, 1), :].rearrange("p o d -> p (o d)")

                    with nc.Block() as block:
                        @block.gpsimd
                        def _(pool):
                            for L in lanes:
                                norm_pool(pool, 0, L)
                            for L in lanes:
                                norm_pool(pool, 1, L)
                        @block.tensor
                        def _(pe):
                            def project(L, w, bank, done):
                                for m in range(KD):
                                    for k in range(KD):
                                        mm = nc.tensor.matmul(ps[:, bank + m, :], w[:, k, m * P:(m + 1) * P], L.xnT[:, k, :],
                                                              start=(k == 0), stop=(k == KD - 1))
                                    mm.then_inc(done, 1)

                            def qkv(L):
                                B = L.bank
                                pe.wait_ge(L.taken, KD)
                                pe.wait_ge(qkv_in, 16 * 3)
                                project(L, wq, B + 2, L.q_mm)
                                project(L, wk, B, L.k_mm)
                                for i in range(TB):
                                    if i % 2 == 0:
                                        pe.wait_ge(L.q_taken, i // 2 + 1)
                                    for k in range(KD):
                                        mm = nc.tensor.matmul(ps[:, B + 2 + i // 2, (i % 2) * D:(i % 2 + 1) * D],
                                                              L.xnT[:, k, i * P:(i + 1) * P], wv[:, k, :],
                                                              start=(k == 0), stop=(k == KD - 1))
                                    if i % 2:
                                        mm.then_inc(L.v_mm, 1)

                            def scores(L):
                                pe.wait_ge(L.k_taken, KD)
                                for i in range(TB):
                                    if i >= 2:
                                        pe.wait_ge(L.v_taken, i - 1)
                                    for m in range(KD):
                                        mm = nc.tensor.matmul(ps[:, L.bank + i, :], L.qT[:, m, i * P:(i + 1) * P], L.kT[:, m, :],
                                                              start=(m == 0), stop=(m == KD - 1))
                                    mm.then_inc(L.score_mm, 1)

                            def turn_probs(L):
                                pe.wait_ge(L.p_done, TB)
                                for kb in range(TB):
                                    for i in range(TB):
                                        mm = nc.tensor.transpose(ps[:, L.bank + kb, i * P:(i + 1) * P],
                                                                 L.pm[:, i, kb * P:(kb + 1) * P], ident[:])
                                    mm.then_inc(L.pT_mm, 1)

                            def weigh(L, m):
                                pe.wait_ge(L.pT_dve, 2)
                                pe.wait_ge(L.pT_act, 2)
                                for kb in range(TB):
                                    mm = nc.tensor.matmul(ps[:, L.bank + m, :], L.v[:, kb, m * P:(m + 1) * P], L.pT[:, kb, :],
                                                          start=(kb == 0), stop=(kb == TB - 1))
                                mm.then_inc(L.pv_mm, 1)

                            def output(L):
                                pe.wait_ge(L.o_taken, KD)
                                pe.wait_ge(load_w, 16 * WEIGHTS)
                                for i in range(TB):
                                    for m in range(KD):
                                        mm = nc.tensor.matmul(ps[:, L.bank + 2 + i // 2, (i % 2) * D:(i % 2 + 1) * D],
                                                              L.oT[:, m, i * P:(i + 1) * P], wo[:, m, :],
                                                              start=(m == 0), stop=(m == KD - 1))
                                    if i % 2:
                                        mm.then_inc(L.proj_mm, 1)

                            def router(L):
                                pe.wait_ge(L.taken, 2 * KD)
                                for i in range(TB):
                                    for k in range(KD):
                                        mm = nc.tensor.matmul(ps[:, L.bank + 2, i * E0:(i + 1) * E0],
                                                              L.xnT[:, k, i * P:(i + 1) * P], wr[:, k, :],
                                                              start=(k == 0), stop=(k == KD - 1))
                                mm.then_inc(L.route_mm, 1)

                            one, two = lanes
                            norm_tensor(pe, 0, one)
                            norm_tensor(pe, 0, two)
                            qkv(one)
                            qkv(two)
                            scores(one)
                            scores(two)
                            turn_probs(one)
                            turn_probs(two)
                            weigh(one, 0)
                            weigh(one, 1)
                            weigh(two, 0)
                            output(one)
                            weigh(two, 1)
                            output(two)
                            norm_tensor(pe, 1, one)
                            norm_tensor(pe, 1, two)
                            router(one)
                            router(two)

                        @block.scalar
                        def _(act):
                            for L in lanes:
                                norm_scalar(act, 0, L)
                            for L in lanes:
                                for m in range(KD):
                                    act.wait_ge(L.q_mm, m + 1)
                                    nc.scalar.activation(L.qT[:, m, :], ps[:, L.bank + 2 + m, :], ACT.Copy,
                                                         scale=scale).then_inc(L.q_taken, 1)
                            for L in lanes:
                                for i in range(TB):
                                    act.wait_ge(L.nmax_done, i + 1)
                                    nc.scalar.activation(L.pm[:, i, :], ps[:, L.bank + i, :], ACT.Exp, bias=L.nmax[:, i:i + 1],
                                                         accum_out=L.rsum[:, i:i + 1]).then_inc(L.p_done, 1)
                            for L in lanes:
                                for kb in (1, 3):
                                    act.wait_ge(L.pT_mm, kb + 1)
                                    nc.scalar.copy(L.pT[:, kb, :], ps[:, L.bank + kb, :]).then_inc(L.pT_act, 1)
                            for L in lanes:
                                for m in range(KD):
                                    act.wait_ge(L.pv_mm, m + 1)
                                    nc.scalar.copy(L.oT[:, m, :], ps[:, L.bank + m, :]).then_inc(L.o_taken, 1)
                            for c, L in enumerate(lanes):
                                norm_scalar(act, 1, L)
                                for k in range(KD):
                                    nc.scalar.copy(xh[:, k, bass.ds(2 * S * b2i + S * c, S)], ps[:, L.bank + k, :]).then_inc(L.xh_done, 1)

                        @block.vector
                        def _(dve):
                            dve.wait_ge(x_loaded[0], 16)
                            for c, L in enumerate(lanes):
                                norm_vector(dve, 0, rows_of(c), L)
                            for L in lanes:
                                for m in range(KD):
                                    dve.wait_ge(L.k_mm, m + 1)
                                    nc.vector.tensor_copy(L.kT[:, m, :], ps[:, L.bank + m, :]).then_inc(L.k_taken, 1)
                                for j in range(2):
                                    dve.wait_ge(L.v_mm, j + 1)
                                    nc.vector.tensor_copy(L.v[:, 2 * j:2 * j + 2, :], ps[:, L.bank + 2 + j, :]).then_inc(L.v_taken, 1)
                            for L in lanes:
                                for i in range(TB):
                                    dve.wait_ge(L.score_mm, i + 1)
                                    nc.vector.tensor_reduce(L.nmax[:, i:i + 1], ps[:, L.bank + i, :], X, ALU.max,
                                                            negate=True).then_inc(L.nmax_done, 1)
                            for L in lanes:
                                for kb in (0, 2):
                                    dve.wait_ge(L.pT_mm, kb + 1)
                                    nc.vector.tensor_copy(L.pT[:, kb, :], ps[:, L.bank + kb, :]).then_inc(L.pT_dve, 1)
                                nc.vector.reciprocal(L.rrec[:], L.rsum[:]).then_inc(L.rrec_done, 1)
                            for c, L in enumerate(lanes):
                                rows = rows_of(c)
                                dve.wait_ge(L.rrec_done, 1)
                                for i in range(TB):
                                    dve.wait_ge(L.proj_mm, i // 2 + 1)
                                    nc.vector.scalar_tensor_tensor(out=rows(i), in0=ps[:, L.bank + 2 + i // 2, (i % 2) * D:(i % 2 + 1) * D],
                                                                   scalar=L.rrec[:, i:i + 1], in1=rows(i),
                                                                   op0=ALU.mult, op1=ALU.add).then_inc(L.x_done, 1)
                                dve.wait_ge(L.x_done, TB)
                                norm_vector(dve, 1, rows, L)
                            dve.wait_ge(x_loaded[1], 16)
                            dve.wait_ge(load_w, 16 * WEIGHTS)
                            for c, L in enumerate(lanes):
                                for k in range(KD):
                                    cur = bass.ds(2 * S * b2i + S * c, S)
                                    dve.wait_ge(L.xh_done, k + 1)
                                    nc.vector.tensor_tensor(xl[:, k, cur], ps[:, L.bank + k, :], f32(xh[:, k, cur]), ALU.subtract)
                                dve.wait_ge(L.route_mm, 1)
                                logits = ps[:, L.bank + 2, 0:TB * E0].rearrange("p (i e) -> p i e", e=E0)
                                nc.vector.tensor_tensor(z[:, bass.ds(2 * TB * b2i + TB * c, TB), :], logits,
                                                        br[:].unsqueeze(1).to_broadcast([P, TB, E0]), ALU.add)
                    clear(*[s for L in lanes for s in L.norm_sems + L.attn_sems])

            with ExitStack() as ex:
                hf = sb("hf", [P, 2, S], F32, ex)
                hh, hl = ([sb(f"h{n}{i}", [P, NI, S], F32R, ex) for i in range(2)] for n in "hl")
                cw = sb("cw", [P, NT, E0], F32, ex)
                cwT = sb("cwT", [E0, NB * S], F32, ex)
                total = sb("total", [P, 2 * E0], F32, ex)
                cnt = sb("cnt", [P, E0], F32, ex)
                crec = sb("crec", [P, E0], F32, ex)
                we = sb("we", [P, E0], F32, ex)

                for t, n, sh in ((w1h, "w1h1", [P, KD, I0]), (w1l, "w1l1", [P, KD, I0]),
                                 (w2h, "w2h1", [P, NI, D]), (w2l, "w2l1", [P, NI, D])):
                    t.append(sb(n, sh, F32R, ex))
                KC = 256
                KPAIR = 3
                kf = sb("kf", [P, KD, KC], F32, ex)
                ksp = sb("ksp", [P, PARTS, KD, KC], BF16, ex)

                second_in, total_ready, chosen_ready, z_ready, ez_ready, count_mm, cw_done, cw_turned, cw_taken, bias_mm = sems(
                    "second_in total_ready chosen_ready z_ready ez_ready count_mm cw_done cw_turned cw_taken bias_mm")

                with nc.Block() as block:
                    @block.sync
                    def _(sp):
                        sp.wait_ge(first_split, 4)
                        load_expert(sp, 1, second_in)

                    @block.gpsimd
                    def _(pool):
                        pool.wait_ge(expert0_in, 32)
                        split_expert(pool, nc.gpsimd, 0, first_split, 0)

                    @block.tensor
                    def _(pe):
                        pe.wait_ge(total_ready, 1)
                        nc.tensor.matmul(ps[:, 0, 0:2 * E0], ones[:], total[:], start=True, stop=True).then_inc(count_mm, 1)
                        pe.wait_ge(cw_done, 1)
                        for t in range(NT):
                            mm = nc.tensor.transpose(ps[0:E0, 1 + t // 4, (t % 4) * P:(t % 4 + 1) * P], cw[:, t, :], ident[:])
                            if t % 4 == 3:
                                mm.then_inc(cw_turned, 1)
                        pe.wait_ge(cw_taken, 4)
                        for t in range(NT):
                            mm = nc.tensor.matmul(ps[:, t // 2, (t % 2) * D:(t % 2 + 1) * D], cwT[:, t * P:(t + 1) * P], b2[:],
                                                  start=True, stop=True)
                            if t % 2:
                                mm.then_inc(bias_mm, 1)

                    @block.vector
                    def _(dve):
                        ch = Chain(dve)
                        choose_start(ch, NT, E0, z_ready)
                        choose_top(dve, ch, NT, E0, ez_ready)
                        choose_hits(ch, NT, E0, TOP0)
                        nc.vector.tensor_tensor(dtop[:], top[:, :, 0:TOP0], top[:, :, 0:1].to_broadcast([P, NT, TOP0]),
                                                ALU.subtract).then_inc(z_ready, 1)
                        dve.wait_ge(ez_ready, 2)
                        ch(nc.vector.tensor_reduce(tsum[:], etop[:], X, ALU.add))
                        ch.wait()
                        ch(nc.vector.reciprocal(trec[:], tsum[:]))
                        ch.wait()
                        ch(nc.vector.tensor_tensor(wtop[:], etop[:], trec[:].unsqueeze(2).to_broadcast([P, NT, TOP0]), ALU.mult))
                        ch.wait()
                        for k in range(TOP0):
                            ch(nc.vector.tensor_tensor(whit[:, k], hit[:, k], wtop[:, :, k:k + 1].to_broadcast([P, NT, E0]), ALU.mult))
                        ch.wait()
                        for c0, src in ((0, whit), (E0, hit)):
                            ch(nc.vector.tensor_tensor(src[:, 0], src[:, 0], src[:, 1], ALU.add))
                            ch.wait()
                            nc.vector.tensor_tensor(chosen[:, :, c0:c0 + E0], src[:, 0], src[:, 2], ALU.add).then_inc(chosen_ready, 1)
                        dve.wait_ge(chosen_ready, 2)
                        nc.vector.tensor_reduce(total[:], chosen[:].rearrange("p t e -> p e t"), X, ALU.add).then_inc(total_ready, 1)
                        dve.wait_ge(count_mm, 1)
                        ch(nc.vector.tensor_scalar(cnt[:], ps[:, 0, E0:2 * E0], 1.0, None, ALU.max))
                        ch.wait()
                        ch(nc.vector.reciprocal(crec[:], cnt[:]))
                        ch.wait()
                        ch(nc.vector.tensor_tensor(we[:], crec[:], ps[:, 0, 0:E0], ALU.mult))
                        ch.wait()
                        nc.vector.tensor_tensor(cw[:], chosen[:, :, E0:2 * E0], we[:].unsqueeze(1).to_broadcast([P, NT, E0]),
                                                ALU.mult).then_inc(cw_done, 1)
                        for j in range(0, NT // 2, 2):
                            dve.wait_ge(bias_mm, j + 1)
                            nc.vector.tensor_copy(acc[:, 2 * j:2 * j + 2, :], ps[:, j, :])

                    @block.scalar
                    def _(act):
                        act.wait_ge(z_ready, 1)
                        nc.scalar.activation(ez[:], z[:], ACT.Exp).then_inc(ez_ready, 1)
                        act.wait_ge(z_ready, 2)
                        nc.scalar.activation(etop[:], dtop[:], ACT.Exp).then_inc(ez_ready, 1)
                        for c in range(4):
                            act.wait_ge(cw_turned, c + 1)
                            nc.scalar.copy(cwT[:, c * S:(c + 1) * S], ps[0:E0, 1 + c, :]).then_inc(cw_taken, 1)
                        for j in range(1, NT // 2, 2):
                            act.wait_ge(bias_mm, j + 1)
                            nc.scalar.copy(acc[:, 2 * j:2 * j + 2, :], ps[:, j, :])
                clear(step)

                weights_in, weights_split, hidden_mm, out_mm, relu_done, parts_done, high_done, sum_done, keys_in, keys_out, key_parts = \
                    pair_sems = sems("weights_in weights_split hidden_mm out_mm relu_done parts_done high_done sum_done "
                                     "keys_in keys_out key_parts")
                STEPS = 2 * NB

                def three(out, ah, al, bh, bl, first, last):
                    nc.tensor.matmul(out, ah, bh, start=first, stop=False)
                    nc.tensor.matmul(out, ah, bl, start=False, stop=False)
                    return nc.tensor.matmul(out, al, bh, start=False, stop=last)

                def expert_pair(e0, more, k0):
                    times = KPAIR if more else KEYS // KC - KPAIR * (E0 // 2 - 1)
                    with nc.Block() as block:
                        @block.sync
                        def _(sp):
                            chunk = lambda n: bass.ds(k0 + n * KC, KC)

                            def load_key_chunk(n):
                                sp.dma_start(kf[:], a["kT"].rearrange("(k p) c -> p k c", p=P)[:, :, chunk(n)]).then_inc(keys_in, 16)

                            load_key_chunk(0)
                            for n in range(times):
                                sp.wait_ge(key_parts, 5 * (n + 1))
                                if n + 1 < times:
                                    load_key_chunk(n + 1)
                                for s in range(PARTS):
                                    sp.dma_start(kparts[s].rearrange("(k p) c -> p k c", p=P)[:, :, chunk(n)],
                                                 ksp[:, s]).then_inc(keys_out, 16)
                                if n == 0 and more:
                                    load_expert(sp, e0 + 2, weights_in)
                            sp.wait_ge(keys_out, 16 * PARTS * times)
                            if more:
                                sp.wait_ge(weights_split, 8)
                                load_expert(sp, e0 + 3, weights_in)
                                sp.wait_ge(weights_in, 64)

                        @block.gpsimd
                        def _(pool):
                            pool.wait_ge(second_in, 32)
                            split_expert(pool, nc.gpsimd, 1, weights_split, 0)
                            for n in range(times):
                                pool.wait_ge(keys_in, 16 * (n + 1))
                                if n:
                                    pool.wait_ge(keys_out, 16 * PARTS * n)
                                for s in range(PARTS):
                                    nc.gpsimd.tensor_copy(ksp[:, s], kf[:]).then_inc(key_parts, 1)
                                    if s < PARTS - 1:
                                        pool.wait_ge(key_parts, 5 * n + 2 * s + 1)
                                        nc.gpsimd.tensor_tensor(kf[:], kf[:], ksp[:, s], ALU.subtract).then_inc(key_parts, 1)
                                        pool.wait_ge(key_parts, 5 * n + 2 * s + 2)
                            if more:
                                pool.wait_ge(weights_in, 32)
                                pool.wait_ge(out_mm, 2 * NB)
                                split_expert(pool, nc.gpsimd, 0, weights_split, 4)

                        @block.tensor
                        def _(pe):
                            def hidden(s):
                                q, c = divmod(s, NB)
                                if s == NB:
                                    pe.wait_ge(weights_split, 4)
                                for i in range(NI):
                                    n = NI * s + i
                                    if n >= 4:
                                        pe.wait_ge(relu_done, n - 3)
                                    for k in range(KD):
                                        mm = three(ps[:, n % 4, :], w1h[q][:, k, i * P:(i + 1) * P],
                                                   w1l[q][:, k, i * P:(i + 1) * P], xh[:, k, c * S:(c + 1) * S],
                                                   xl[:, k, c * S:(c + 1) * S], k == 0, k == KD - 1)
                                    mm.then_inc(hidden_mm, 1)

                            def output(s):
                                q = s // NB
                                pe.wait_ge(parts_done, NI * (s + 1))
                                for t in range(TB):
                                    u = 2 * s + t // 2
                                    if u >= 4 and t % 2 == 0:
                                        pe.wait_ge(sum_done, 2 * (u - 3))
                                    for i in range(NI):
                                        mm = three(ps[:, 4 + u % 4, (t % 2) * D:(t % 2 + 1) * D],
                                                   hh[s % 2][:, i, t * P:(t + 1) * P], hl[s % 2][:, i, t * P:(t + 1) * P],
                                                   w2h[q][:, i, :], w2l[q][:, i, :], i == 0, i == NI - 1)
                                    if t % 2:
                                        mm.then_inc(out_mm, 1)

                            hidden(0)
                            for s in range(STEPS):
                                if s + 1 < STEPS:
                                    hidden(s + 1)
                                output(s)

                        @block.scalar
                        def _(act):
                            for n in range(NI * STEPS):
                                act.wait_ge(hidden_mm, n + 1)
                                if n >= 2:
                                    act.wait_ge(parts_done, n - 1)
                                bias = b1[:, bass.ds((e0 + n // (NI * NB)) * NI + n % NI, 1)]
                                nc.scalar.activation(hf[:, n % 2, :], ps[:, n % 4, :], ACT.Relu, bias=bias).then_inc(relu_done, 1)

                        @block.vector
                        def _(dve):
                            def parts(s):
                                if s >= 2:
                                    dve.wait_ge(out_mm, 2 * (s - 1))
                                for i in range(NI):
                                    n = NI * s + i
                                    dve.wait_ge(relu_done, n + 1)
                                    nc.vector.tensor_copy(hh[s % 2][:, i, :], hf[:, n % 2, :]).then_inc(high_done, 1)
                                    dve.wait_ge(high_done, n + 1)
                                    nc.vector.tensor_tensor(hl[s % 2][:, i, :], hf[:, n % 2, :], f32(hh[s % 2][:, i, :]),
                                                            ALU.subtract).then_inc(parts_done, 1)

                            def sums(s):
                                q, c = divmod(s, NB)
                                for t in range(TB):
                                    n = TB * s + t
                                    u = 2 * s + t // 2
                                    dve.wait_ge(out_mm, u + 1)
                                    if n >= NT:
                                        dve.wait_ge(sum_done, n - NT + 1)
                                    tile = TB * c + t
                                    nc.vector.scalar_tensor_tensor(
                                        out=acc[:, tile, :], in0=ps[:, 4 + u % 4, (t % 2) * D:(t % 2 + 1) * D],
                                        scalar=cw[:, tile, bass.ds(e0 + q, 1)], in1=acc[:, tile, :],
                                        op0=ALU.mult, op1=ALU.add).then_inc(sum_done, 1)
                                if q and not more:
                                    dve.wait_ge(sum_done, TB * (s + 1))
                                    nc.vector.tensor_reduce(xn[:, c, :], acc[:, TB * c:TB * (c + 1), :].rearrange("p t d -> p d t"),
                                                            X, ALU.add)

                            parts(0)
                            for s in range(STEPS):
                                if s + 1 < STEPS:
                                    parts(s + 1)
                                sums(s)
                    clear(*pair_sems)

                with nc.Fori(0, E0 // 2 - 1) as pair:
                    expert_pair(2 * pair, True, KPAIR * KC * pair)
                expert_pair(E0 - 2, False, KPAIR * KC * (E0 // 2 - 1))


        wgate = sb("wgate", [P, KD, E1 + 1])
        (z, ez, zmax, zsum, zrec, probs, top, topi, topf, dtop, etop, tsum, trec, wtop, hit, whit) = choice_buffers(ctx, TB)
        zs, ezs = sb("zs", [P, TB]), sb("ezs", [P, TB])
        comb = sb("comb", [P, TB, E1 + 1])
        gate_in = sem("gate_in")
        z_ready1, ez_ready1 = route_sems = sems("z_ready1 ez_ready1")

        def router(bank, m):
            for k in range(KD):
                mm = nc.tensor.matmul(ps[:, bank, m * 16:m * 16 + E1 + 1], xnT[:, k, m * P:(m + 1) * P], wgate[:, k, :],
                                      start=(k == 0), stop=(k == KD - 1))
            return mm

        def take_logits(ch, bank, taken):
            lg = ps[:, bank, 0:TB * 16].rearrange("p (i e) -> p i e", e=16)
            ch(nc.vector.tensor_copy(zs[:], lg[:, :, E1]))
            nc.vector.tensor_copy(z[:, 0:TB, 0:E1], lg[:, :, 0:E1]).then_inc(taken, 1)

        def route_exps(act):
            act.wait_ge(z_ready1, 1)
            nc.scalar.activation(ez[:, 0:TB, 0:E1], z[:, 0:TB, 0:E1], ACT.Exp).then_inc(ez_ready1, 1)
            nc.scalar.activation(ezs[:], zs[:], ACT.Exp, scale=-1.0).then_inc(ez_ready1, 1)

        def combine(dve, ch):
            ch(nc.vector.tensor_tensor(tsum[:], top[:, :, 0], top[:, :, 1], ALU.add))
            ch.wait()
            ch(nc.vector.reciprocal(trec[:], tsum[:]))
            ch.wait()
            ch(nc.vector.tensor_tensor(wtop[:, :, 0:TOP1], top[:, :, 0:TOP1], spread(trec, TB, TOP1), ALU.mult))
            ch.wait()
            for k in range(TOP1):
                ch(nc.vector.tensor_tensor(whit[:, k, :, 0:E1], hit[:, k, :, 0:E1],
                                           wtop[:, :, k:k + 1].to_broadcast([P, TB, E1]), ALU.mult))
            ch.wait()
            ch(nc.vector.tensor_tensor(comb[:, :, 0:E1], whit[:, 0, :, 0:E1], whit[:, 1, :, 0:E1], ALU.add))
            dve.wait_ge(ez_ready1, 2)
            ch(nc.vector.tensor_scalar(ezs[:], ezs[:], 1.0, None, ALU.add))
            ch.wait()
            ch(nc.vector.reciprocal(comb[:, :, E1], ezs[:]))

        with ExitStack() as l1:
            kst = [sb(f"kst{i}", [ROWS, HG, KEYS], BF16, l1) for i in range(2)]
            qst = [sb(f"qst{i}", [ROWS, HG, S], BF16, l1) for i in range(NB)]
            vnext = sb("vnext", [P, NKT, HG * DH], F32, l1)
            vcur = sb("vcur", [P, NKT, HG, VC], F32, l1)
            pring = sb("pring", [P, 2 * HG, S], F32, l1)
            osb = sb("osb", [P, S], F32, l1)
            orec = sb("orec", [P, TB, HG], F32, l1)
            maxp = sb("maxp", [P, HG, TB, KEYS // 512], F32, l1)
            mneg = sb("mneg", [P, HG * TB], F32, l1)
            mres = sb("mres", [HG * TB, P], F32, l1)
            mrow = sb("mrow", [HG * TB, PARTS, P], BF16, l1)
            q_loaded = [sem(f"q_loaded{i}") for i in range(NB)]
            v_loaded = sem("v_loaded")
            keys_in0, ones_set, max_mm, max_taken, max_turned = sems("keys_in0 ones_set max_mm max_taken max_turned")
            rows_in, max_done, rows_ready = maxima_sems = sems("rows_in max_done rows_ready")
            q_mm, q_taken, q_split, q_left, q_stored, x_done = query_sems = sems("q_mm q_taken q_split q_left q_stored x_done")

            def load_keys(sp, i, g, done):
                for s in range(SIDE):
                    src = kparts[K_PART[s]].rearrange("(h r) c -> r h c", r=DH)[:, bass.ds(g * HG, HG), :]
                    sp.dma_start(kst[i][s * DH:(s + 1) * DH], src).then_inc(done, 16)

            def load_values(sp, g):
                sp.dma_start(vnext[:], a["v"].rearrange("(t p) d -> p t d", p=P)[:, :, bass.ds(g * HG * DH, HG * DH)]
                             ).then_inc(v_loaded, 16)

            def load_queries(sp, i, g):
                for s in range(SIDE):
                    src = qparts[Q_PART[s]].rearrange("(h r) c -> r h c", r=DH)[:, bass.ds(g * HG, HG), i * S:(i + 1) * S]
                    sp.dma_start(qst[i][s * DH:(s + 1) * DH], src).then_inc(q_loaded[i], 16)

            def load_maxima(sp, i):
                for s in range(PARTS):
                    sp.dma_start(qst[i][SIDE * DH + s:SIDE * DH + s + 1].rearrange("o h s -> o (h s)"),
                                 mrow[:, s, :]).then_inc(rows_in, 16)

            NU = TB * (KEYS // 512) * (HG // 2)

            def max_unit(u, i, keys, base):
                qt, kb, hp = u // 16, (u % 16) // 2, u % 2
                for jj in range(2):
                    j = 2 * hp + jj
                    mm = nc.tensor.matmul(ps[:, base + jj, :], qst[i][0:SIDE * DH, j, qt * P:(qt + 1) * P],
                                          keys[0:SIDE * DH, j, kb * 512:(kb + 1) * 512], start=True, stop=True)
                return mm

            def max_reduce(u, base):
                qt, kb, hp = u // 16, (u % 16) // 2, u % 2
                return nc.vector.tensor_reduce(maxp[:, 2 * hp:2 * hp + 2, qt, kb], ps[:, base:base + 2, :], X, ALU.max)

            def max_total():
                return nc.vector.tensor_reduce(mneg[:], maxp[:].rearrange("p h t k -> p (h t) k"), X, ALU.max, negate=True)

            with ExitStack() as qs:
                qf = sb("qf", [P, KD, S], F32, qs)
                qsp = sb("qsp", [P, PARTS, KD, S], BF16, qs)

                def residual(dve, b):
                    for t in range(TB * b, TB * b + TB):
                        nc.vector.scalar_tensor_tensor(out=x[:, t, :], in0=acc[:, t, :], scalar=fac[:, b:b + 1],
                                                       in1=x[:, t, :], op0=ALU.mult, op1=ALU.add).then_inc(x_done, 1)

                def half_queries(m):
                    for k in range(KD):
                        mm = nc.tensor.matmul(ps[:, 2 + m, :], wqt[:, k, m * P:(m + 1) * P], xnT[:, k, :],
                                              start=(k == 0), stop=(k == KD - 1))
                    mm.then_inc(q_mm, 1)

                def take_queries(act, b, split):
                    for m in range(KD):
                        act.wait_ge(q_mm, KD * b + m + 1)
                        if b:
                            act.wait_ge(q_split, PARTS * (KD * (b - 1) + m + 1))
                        nc.scalar.copy(qf[:, m, :], ps[:, 2 + m, :]).then_inc(q_taken, 1)
                        if split:
                            act.wait_ge(q_stored, 16 * KD * b)
                            for s in range(PARTS):
                                if s:
                                    act.wait_ge(q_left, (PARTS - 1) * (KD * b + m) + s)
                                else:
                                    act.wait_ge(q_taken, KD * b + m + 1)
                                nc.scalar.copy(qsp[:, s, m], qf[:, m]).then_inc(q_split, 1)

                def leave(eng, ops, b, m, s):
                    eng.wait_ge(q_split, PARTS * (KD * b + m) + s + 1)
                    ops.tensor_tensor(qf[:, m], qf[:, m], qsp[:, s, m], ALU.subtract).then_inc(q_left, 1)

                def store_queries(sp, b):
                    for m in range(KD):
                        sp.wait_ge(q_split, PARTS * (KD * b + m + 1))
                        sp.dma_start(qparts[:, m * P:(m + 1) * P, b * S:(b + 1) * S].rearrange("s p c -> p s c"),
                                     qsp[:, :, m, :]).then_inc(q_stored, 16)
                        if m == 0:
                            sp.wait_ge(q_stored, 16 * (KD * b + 1))
                            if b < NB - 1:
                                load_queries(sp, b, 0)

                pooled = sb("pooled", [P, KD * NB], F32, qs)
                hp, gp, ephi, phi = (sb(n, [P, NB], F32, qs) for n in ("hp", "gp", "ephi", "phi"))
                phi_mm, ephi_done = sems("phi_mm ephi_done")

                STATS = {12: 2, 30: 3}
                APPLY = {14: 2, 32: 3}
                PIECE = {u0 + (i if i < TB else 5 + 2 * (i - TB)): (n, i) for u0, n in ((0, 1), (16, 2), (34, 3)) for i in range(TB + KD)}

                with nc.Block() as block:
                    @block.sync
                    def _(sp):
                        load_keys(sp, 1, 0, keys_in0)
                        store_queries(sp, 0)
                        load_values(sp, 0)
                        for b in range(1, NB):
                            store_queries(sp, b)
                        sp.wait_ge(q_stored, 16 * KD * NB)
                        sp.wait_ge(rows_ready, 1)
                        load_maxima(sp, 0)
                        sp.wait_ge(rows_in, 16 * PARTS)
                        for b in range(1, NB - 1):
                            sp.wait_ge(q_loaded[b], 16 * SIDE)
                        sp.wait_ge(v_loaded, 16)

                    @block.gpsimd
                    def _(pool):
                        norm_pool(pool, 0, main)
                        for b in range(1, NB):
                            norm_pool(pool, b, main)
                            for m in range(KD):
                                for s in range(PARTS - 1):
                                    leave(pool, nc.gpsimd, b, m, s)
                        pool.wait_ge(q_left, (PARTS - 1) * KD * NB)
                        nc.gpsimd.memset(kst[1][SIDE * DH:ROWS], 1.0).then_inc(ones_set, 1)
                        pool.wait_ge(ones_set, 1)
                        nc.gpsimd.memset(vcur[:, :, :, DH], 1.0)

                    @block.tensor
                    def _(pe):
                        for m in range(KD):
                            for b in range(NB):
                                mm = nc.tensor.matmul(ps[:, 0, m * NB + b:m * NB + b + 1], xn[:, b, m * P:(m + 1) * P],
                                                      ones[:, 0:1], start=True, stop=True)
                        mm.then_inc(phi_mm, 1)
                        pe.wait_ge(step, 1)
                        for m in range(KD):
                            mm = nc.tensor.matmul(ps[:, 1, 0:NB], wp1[:, m, :], pooled[:, m * NB:(m + 1) * NB],
                                                  start=(m == 0), stop=(m == KD - 1))
                        mm.then_inc(phi_mm, 1)
                        pe.wait_ge(step, 3)
                        nc.tensor.matmul(ps[:, 2, 0:NB], ones[:], gp[:], start=True, stop=True).then_inc(phi_mm, 1)
                        norm_tensor(pe, 0, main)
                        pe.wait_ge(main.taken, KD)
                        half_queries(0)
                        half_queries(1)
                        pe.wait_ge(keys_in0, 16 * SIDE)
                        pe.wait_ge(q_loaded[0], 16 * SIDE)
                        for u in range(NU):
                            if u in PIECE:
                                b, i = PIECE[u]
                                if i < TB:
                                    turn_tile(pe, b, i, main)
                                elif i == TB:
                                    pe.wait_ge(main.taken, KD * (b + 1))
                                    pe.wait_ge(q_taken, KD * b)
                                    half_queries(0)
                                else:
                                    half_queries(1)
                            if u >= 2:
                                pe.wait_ge(max_taken, u - 1)
                            max_unit(u, 0, kst[1], 4 + 2 * (u % 2)).then_inc(max_mm, 1)
                        pe.wait_ge(max_done, 1)
                        nc.tensor.transpose(ps[0:HG * TB, 0, 0:P], mneg[:], ident[:]).then_inc(max_turned, 1)

                    @block.scalar
                    def _(act):
                        act.wait_ge(step, 4)
                        nc.scalar.activation(ephi[:], phi[:], ACT.Exp, scale=-1.0).then_inc(ephi_done, 1)
                        for b in range(NB):
                            norm_scalar(act, b, main)
                            take_queries(act, b, b > 0)

                    @block.vector
                    def _(dve):
                        ch = Chain(dve)
                        dve.wait_ge(phi_mm, 1)
                        ch(nc.vector.tensor_scalar(pooled[:], ps[:, 0, 0:KD * NB], 1.0 / S, None, ALU.mult))
                        dve.wait_ge(phi_mm, 2)
                        ch(nc.vector.tensor_scalar(hp[:], ps[:, 1, 0:NB], bp1[:, 0:1], 0.0, ALU.add, ALU.max))
                        ch.wait()
                        ch(nc.vector.tensor_scalar(gp[:], hp[:], wp2[:, 0:1], None, ALU.mult))
                        dve.wait_ge(phi_mm, 3)
                        ch(nc.vector.tensor_scalar(phi[:], ps[:, 2, 0:NB], bp2[:, 0:1], None, ALU.add))
                        dve.wait_ge(ephi_done, 1)
                        ch(nc.vector.tensor_scalar(ephi[:], ephi[:], 1.0, None, ALU.add))
                        ch.wait()
                        ch(nc.vector.reciprocal(phi[:], ephi[:]))
                        ch.wait()
                        ch(nc.vector.tensor_scalar(fac[:], phi[:], 0.7, -0.8, ALU.is_gt, ALU.mult))
                        ch.wait()
                        ch(nc.vector.tensor_scalar(fac[:], fac[:], 1.0, None, ALU.add))
                        ch.wait()
                        def stats_of(b):
                            residual(dve, b)
                            dve.wait_ge(x_done, TB * (b + 1))
                            norm_stats(dve, b, lambda t: x[:, TB * b + t, :], main)

                        def apply_of(b):
                            norm_apply(dve, b, lambda t: x[:, TB * b + t, :], main)

                        stats_of(0)
                        apply_of(0)
                        stats_of(1)
                        for m in range(KD):
                            dve.wait_ge(q_taken, m + 1)
                            for s in range(PARTS):
                                nc.vector.tensor_copy(qsp[:, s, m], qf[:, m]).then_inc(q_split, 1)
                                if s < PARTS - 1:
                                    leave(dve, nc.vector, 0, m, s)
                                    dve.wait_ge(q_left, (PARTS - 1) * m + s + 1)
                        apply_of(1)
                        for u in range(NU):
                            if u in STATS:
                                stats_of(STATS[u])
                            if u in APPLY:
                                apply_of(APPLY[u])
                            dve.wait_ge(max_mm, u + 1)
                            max_reduce(u, 4 + 2 * (u % 2)).then_inc(max_taken, 1)
                        dve.wait_ge(max_taken, NU)
                        max_total().then_inc(max_done, 1)
                        dve.wait_ge(max_turned, 1)
                        src = ps[0:HG * TB, 0, 0:P]
                        for s in range(PARTS):
                            w = nc.vector.tensor_copy(mrow[:, s, :], src)
                            if s < PARTS - 1:
                                ch(w)
                                ch.wait()
                                ch(nc.vector.tensor_tensor(mres[:], src, mrow[:, s, :], ALU.subtract))
                                ch.wait()
                                src = mres[:]
                        w.then_inc(rows_ready, 1)
                clear(step, v_loaded, *q_loaded, *maxima_sems, *main.norm_sems)

            wgf, wuf = (sb(n, [P, KD, W1C], F32, arrivals, "right") for n in ("wgf", "wuf"))
            wdf = sb("wdf", [P, ND, D], F32, arrivals, "right")

            PIECES = 4
            FIRST = [4, 5, 7, 9, 13, 14, 17]
            EXPS = 21
            AHEAD = 2

            def schedule(nexts):
                plan = [[] for _ in range(NB * NKT)]
                for i, nxt in enumerate(nexts):
                    end = (i + 1) * NKT - AHEAD
                    begin = i * NKT - (AHEAD if i else 0)
                    if nxt is not None:
                        for u in range(NU):
                            plan[begin + u * (end - begin) // NU].append(("max", nxt, u))
                        plan[end].append(("turn_max", nxt, 0))
                    if i:
                        plan[i * NKT + 2].append(("turn_out", i - 1, 0))
                if nexts[-1] is None:
                    for n, kt in enumerate(FIRST):
                        plan[(NB - 1) * NKT + kt].append(("front", 0, n))
                return plan

            stage_in, score_mm, exp_done, keys_moved, values_moved, value_mm, sums_taken, unit_mm, unit_taken = group_sems = sems(
                "stage_in score_mm exp_done keys_moved values_moved value_mm sums_taken unit_mm unit_taken")

            def run_scores(g, last):
                nexts = [(i + 1) % NB if (i + 1 < NB or not last) else None for i in range(NB)]
                nth = lambda i: nexts.index(i) + 1
                plan = schedule(nexts)
                tail = ("turn_out", NB - 1, 0)

                with nc.Block() as block:
                    @block.sync
                    def _(sp):
                        load_queries(sp, NB - 1, g)
                        if last:
                            sp.dma_start(wgate[:], a["gateT"].rearrange("(k p) e -> p k e", p=P)).then_inc(gate_in, 16)
                            sp.dma_start(wgf[:], a["wg"].rearrange("(k p) e -> p k e", p=P)).then_inc(stage_in, 16)
                            sp.dma_start(wuf[:], a["wu"].rearrange("(k p) e -> p k e", p=P)).then_inc(stage_in, 16)
                            sp.dma_start(wdf[:, 0:ND - 1, :], a["wd"][0:(ND - 1) * P].rearrange("(k p) e -> p k e", p=P)
                                         ).then_inc(stage_in, 16)
                            sp.dma_start(wdf[0:DR, ND - 1, :], a["wd"][(ND - 1) * P:W1C]).then_inc(stage_in, 16)
                        if not last:
                            sp.wait_ge(keys_moved, PIECES)
                            load_keys(sp, 1, g + 1, stage_in)
                            sp.wait_ge(values_moved, PIECES)
                            load_values(sp, g + 1)
                        for i in range(NB):
                            if nexts[i] is not None:
                                sp.wait_ge(rows_ready, i + 1)
                                load_maxima(sp, nexts[i])
                                sp.wait_ge(rows_in, 16 * PARTS * (i + 1))
                            if not last and i < NB - 1:
                                sp.wait_ge(score_mm, NKT * HG * (i + 1))
                                load_queries(sp, i, g + 1)
                        if last:
                            sp.wait_ge(stage_in, 16 * 4)
                        else:
                            for i in range(NB - 1):
                                sp.wait_ge(q_loaded[i], 16 * SIDE)
                            sp.wait_ge(stage_in, 16 * SIDE)
                            sp.wait_ge(v_loaded, 16)

                    @block.gpsimd
                    def _(pool):
                        for n in range(PIECES):
                            tiles = slice(n * NKT // PIECES, (n + 1) * NKT // PIECES)
                            nc.gpsimd.tensor_copy(vcur[:, tiles, :, 0:DH], vnext[:, tiles, :].rearrange("p t (h d) -> p t h d", h=HG)
                                                  ).then_inc(values_moved, 1)
                        if last:
                            norm_pool(pool, 0, main)

                    @block.tensor
                    def _(pe):
                        units = 0

                        def scores(i, kt, j):
                            n = (i * NKT + kt) * HG + j
                            if n >= 3:
                                pe.wait_ge(exp_done, n - 2)
                            if i == 0 and j == 0 and kt % (NKT // PIECES) == 0:
                                pe.wait_ge(keys_moved, kt // (NKT // PIECES) + 1)
                            nc.tensor.matmul(ps[:, n % 3, :], kst[0][:, j, kt * P:(kt + 1) * P], qst[i][:, j, :],
                                             start=True, stop=True).then_inc(score_mm, 1)

                        def values(i, kt):
                            G = i * NKT + kt
                            if i == 0 and kt % (NKT // PIECES) == 0:
                                pe.wait_ge(values_moved, kt // (NKT // PIECES) + 1)
                            pe.wait_ge(exp_done, HG * (G + 1))
                            if kt == 0 and i:
                                pe.wait_ge(sums_taken, i)
                            for j in range(HG):
                                mm = nc.tensor.matmul(ps[32 * j:32 * j + VC, 7, :], vcur[:, kt, j, :],
                                                      pring[:, (G % 2) * HG + j, :], start=(kt == 0), stop=(kt == NKT - 1))
                            mm.then_inc(value_mm, 1)

                        def front_products(pe, n, bank):
                            if n in (2, 4, 6):
                                pe.wait_ge(unit_taken, units)
                            if n in (0, 1):
                                for t in range(TB):
                                    mm = nc.tensor.transpose(ps[:, bank, t * P:(t + 1) * P], acc[:, t, n * P:(n + 1) * P], ident[:])
                            elif n in (2, 3):
                                for t in range(2 * (n - 2), 2 * (n - 2) + 2):
                                    for k in range(KD):
                                        mm = nc.tensor.matmul(ps[:, bank, (t % 2) * D:(t % 2 + 1) * D], aT[:, k, t * P:(t + 1) * P],
                                                              wot[:, k, :], start=(k == 0), stop=(k == KD - 1))
                            elif n in (4, 5):
                                pe.wait_ge(main.norm_done, TB)
                                for t in range(TB):
                                    mm = nc.tensor.transpose(ps[:, bank, t * P:(t + 1) * P], xn[:, t, (n - 4) * P:(n - 3) * P], ident[:])
                            else:
                                pe.wait_ge(gate_in, 16)
                                for t in range(TB):
                                    mm = router(bank, t)
                            return mm

                        def unit(kind, i, u):
                            nonlocal units
                            base = 3 + 2 * (units % 2)
                            if units >= 2:
                                pe.wait_ge(unit_taken, units - 1)
                            if kind == "max":
                                if u == 0 and i == 0:
                                    pe.wait_ge(stage_in, 16 * SIDE)
                                    pe.wait_ge(q_loaded[0], 16 * SIDE)
                                if units < 16 and u % 2 == 0:
                                    pe.wait_ge(keys_moved, u // 2 * 512 // (KEYS // PIECES) + 1)
                                if u == 0 and i == NB - 1:
                                    pe.wait_ge(q_loaded[i], 16 * SIDE)
                                mm = max_unit(u, i, kst[1 if i == 0 else 0], base)
                            elif kind == "front":
                                mm = front_products(pe, u, base)
                            elif kind == "turn_max":
                                pe.wait_ge(max_done, nth(i))
                                mm = nc.tensor.transpose(ps[0:HG * TB, base, 0:P], mneg[:], ident[:])
                            else:
                                pe.wait_ge(sums_taken, i + 1)
                                for t in range(TB):
                                    mm = nc.tensor.transpose(ps[:, base, t * P:(t + 1) * P], osb[:, t * P:(t + 1) * P], ident[:])
                            mm.then_inc(unit_mm, 1)
                            units += 1

                        for i in range(NB):
                            if i:
                                pe.wait_ge(rows_in, 16 * PARTS * i)
                            for kt in range(NKT):
                                ev = plan[i * NKT + kt]
                                half = (len(ev) + 1) // 2
                                scores(i, kt, 0)
                                scores(i, kt, 1)
                                for e in ev[:half]:
                                    unit(*e)
                                scores(i, kt, 2)
                                scores(i, kt, 3)
                                for e in ev[half:]:
                                    unit(*e)
                                if kt:
                                    values(i, kt - 1)
                                elif i:
                                    values(i - 1, NKT - 1)
                        values(NB - 1, NKT - 1)
                        unit(*tail)

                    @block.scalar
                    def _(act):
                        for n in range(NB * NKT * HG):
                            G = n // HG
                            act.wait_ge(score_mm, n + 1)
                            if G >= 2 and n % HG == 0:
                                act.wait_ge(value_mm, G - 1)
                            nc.scalar.activation(pring[:, n % (2 * HG), :], ps[:, n % 3, :], ACT.Exp,
                                                 scale=float(DH) ** -0.5).then_inc(exp_done, 1)
                            if last and n == ((NB - 1) * NKT + EXPS) * HG:
                                route_exps(act)

                    @block.vector
                    def _(dve):
                        ch = Chain(dve)
                        units = 0
                        for n in range(PIECES):
                            cols = slice(n * KEYS // PIECES, (n + 1) * KEYS // PIECES)
                            nc.vector.tensor_copy(kst[0][:, :, cols], kst[1][:, :, cols]).then_inc(keys_moved, 1)

                        def unit(kind, i, u):
                            nonlocal units
                            base = 3 + 2 * (units % 2)
                            dve.wait_ge(unit_mm, units + 1)
                            if kind == "max":
                                max_reduce(u, base).then_inc(unit_taken, 1)
                                if u == NU - 1:
                                    dve.wait_ge(unit_taken, units + 1)
                                    max_total().then_inc(max_done, 1)
                            elif kind == "front":
                                front_results(u, base)
                            elif kind == "turn_max":
                                src = ps[0:HG * TB, base, 0:P]
                                if nth(i) > 1:
                                    dve.wait_ge(rows_in, 16 * PARTS * (nth(i) - 1))
                                for s in range(PARTS):
                                    part = nc.vector.tensor_copy(mrow[:, s, :], src)
                                    if s < PARTS - 1:
                                        ch(part)
                                        ch.wait()
                                        w = nc.vector.tensor_tensor(mres[:], src, mrow[:, s, :], ALU.subtract)
                                        if s == 0:
                                            w.then_inc(unit_taken, 1)
                                            dve.wait_ge(unit_taken, units + 1)
                                        else:
                                            ch(w)
                                            ch.wait()
                                        src = mres[:]
                                part.then_inc(rows_ready, 1)
                            else:
                                view = ps[:, base, :].rearrange("p (t h c) -> p t h c", t=TB, h=HG)
                                ch(nc.vector.reciprocal(orec[:], view[:, :, :, DH]))
                                ch.wait()
                                dst = acc[:, TB * i:TB * (i + 1), bass.ds(g * HG * DH, HG * DH)].rearrange(
                                    "p t (h d) -> p t h d", h=HG)
                                for t in range(TB):
                                    w = nc.vector.tensor_tensor(dst[:, t], view[:, t, :, 0:DH],
                                                                orec[:, t, :].unsqueeze(2).to_broadcast([P, HG, DH]), ALU.mult)
                                w.then_inc(unit_taken, 1)
                            units += 1

                        def front_results(n, bank):
                            rows = lambda t: x[:, t, :]
                            if n in (0, 1, 4, 5):
                                dst = aT if n < 2 else xnT
                                nc.vector.tensor_copy(dst[:, n % 2, :], ps[:, bank, :]).then_inc(unit_taken, 1)
                            elif n in (2, 3):
                                t = 2 * (n - 2)
                                nc.vector.tensor_tensor(x[:, t:t + 2, :].rearrange("p t d -> p (t d)"),
                                                        x[:, t:t + 2, :].rearrange("p t d -> p (t d)"), ps[:, bank, :],
                                                        ALU.add).then_inc(unit_taken, 1)
                                if n == 3:
                                    dve.wait_ge(unit_taken, units + 1)
                                    norm_vector(dve, 0, rows, main)
                            else:
                                take_logits(ch, bank, unit_taken)
                                dve.wait_ge(unit_taken, units + 1)
                                choose_start(ch, TB, E1, z_ready1)
                                choose_top(dve, ch, TB, E1, ez_ready1)
                                choose_hits(ch, TB, E1, TOP1)
                                combine(dve, ch)

                        def take_sums(i):
                            dve.wait_ge(value_mm, NKT * (i + 1))
                            if i:
                                dve.wait_ge(unit_taken, out_units[i - 1] + 1)
                            nc.vector.tensor_copy(osb[:], ps[:, 7, :]).then_inc(sums_taken, 1)

                        flat = [e for ev in plan for e in ev] + [tail]
                        out_units = {e[1]: n for n, e in enumerate(flat) if e[0] == "turn_out"}
                        for i in range(NB):
                            for kt in range(NKT):
                                if i and kt == 1:
                                    take_sums(i - 1)
                                for e in plan[i * NKT + kt]:
                                    unit(*e)
                        take_sums(NB - 1)
                        unit(*tail)

            with nc.Fori(0, NG - 1) as g:
                run_scores(g, False)
                clear(step, v_loaded, *q_loaded, *maxima_sems, *group_sems)
            aT = vnext[:].rearrange("p t c -> p (t c)")[:, 0:KD * S].rearrange("p (k s) -> p k s", k=KD)
            run_scores(NG - 1, True)
            clear(step, *route_sems, *main.norm_sems)

        with ExitStack() as l3:
            CR = PARTS * (E1 + 1)
            wgh, wgl, wuh, wul = (sb(n, [P, KD, W1C], F32R, l3) for n in ("wgh", "wgl", "wuh", "wul"))
            wdh, wdl = (sb(n, [P, ND, D], F32R, l3) for n in ("wdh", "wdl"))
            xh2, xl2 = ([sb(f"x{n}2{i}", [P, KD, S], F32R, l3) for i in range(2)] for n in "hl")
            combT = [sb(f"combT{i}", [CR, S], BF16, l3) for i in range(2)]
            owner = sb("owner", [CR, W1C], BF16, l3)
            cparts = sb("cparts", [P, TB, E1 + 1, PARTS], BF16, l3)
            cpartsf = sb("cpartsf", [P, TB, CR], F32, l3)
            ab = sb("ab", [P, TB, D], F32, l3)
            aT = sb("aT", [P, KD, S], F32, l3)
            wd_split, wu_split, owner_set = sems("wd_split wu_split owner_set")
            (front_mm, front_taken, front_x, ab_done, combT_done, gate_mm, bcast_mm, silu_done, m1_done, m2_done,
             high_done, low_done, down_mm, y_done, stored, cparts_done, yT_done, y_mm) = trip_sems = sems(
                "front_mm front_taken front_x ab_done combT_done gate_mm bcast_mm silu_done m1_done m2_done "
                "high_taken low_taken down_mm y_done stored cparts_done yT_done y_mm")
            RING = 3
            BACK = {0: 0, 1: 1}
            FRONT = {2: 0, 3: 1, 4: 2, 5: 3, 7: 4, 8: 5, 9: 6, 13: 7}

            def trip(b, ffn, front, first, back):
                nb = b + 1
                nxt = 0 if first else 1
                rows_n = lambda t: x[:, bass.ds(TB * nb + t, 1), :].rearrange("p o d -> p (o d)")
                height = lambda c: P if c < ND - 1 else DR

                with nc.Block() as block:
                    @block.sync
                    def _(sp):
                        outputs = ([b - 1] if back else []) + ([b] if ffn and not front else [])
                        for n, batch in enumerate(outputs):
                            sp.wait_ge(y_done, 2 * (n + 1))
                            sp.dma_start(out.rearrange("(t p) d -> p t d", p=P)[:, bass.ds(TB * batch, TB), :], yout[:]
                                         ).then_inc(stored, 16)
                            sp.wait_ge(stored, 16 * (n + 1))

                    @block.gpsimd
                    def _(pool):
                        if front and not first:
                            nc.gpsimd.tensor_copy(ab[:], acc[:, bass.ds(TB * nb, TB), :]).then_inc(ab_done, 1)
                            norm_pool(pool, 0, main)
                        if first:
                            routed = owner[:, 0:E1 * H1].rearrange("r (e h) -> r e h", e=E1)
                            nc.gpsimd.memset(owner[:], 1.0).then_inc(owner_set, 1)
                            pool.wait_ge(owner_set, 1)
                            nc.gpsimd.affine_select(out=routed, in_=routed, compare_op=ALU.is_ge, fill=0.0, base=0,
                                                    pattern=[[-PARTS, E1], [0, H1]], channel_multiplier=1).then_inc(owner_set, 1)
                            nc.gpsimd.affine_select(out=owner[:, E1 * H1:W1C], in_=owner[:, E1 * H1:W1C], compare_op=ALU.is_ge,
                                                    fill=0.0, base=-PARTS * E1, pattern=[[0, HS1]],
                                                    channel_multiplier=1).then_inc(owner_set, 1)
                            pool.wait_ge(owner_set, 3)
                            nc.gpsimd.affine_select(out=routed, in_=routed, compare_op=ALU.is_ge, fill=0.0, base=PARTS - 1,
                                                    pattern=[[PARTS, E1], [0, H1]], channel_multiplier=-1).then_inc(owner_set, 1)
                            pool.wait_ge(wd_split, 2)
                            nc.gpsimd.tensor_tensor(wdl[:, 0:ND - 1], wdf[:, 0:ND - 1], f32(wdh[:, 0:ND - 1]), ALU.subtract)
                            nc.gpsimd.tensor_tensor(wdl[0:DR, ND - 1], wdf[0:DR, ND - 1], f32(wdh[0:DR, ND - 1]), ALU.subtract)

                    @block.tensor
                    def _(pe):
                        def three(out_, ah, al, bh, bl, begin, end):
                            nc.tensor.matmul(out_, ah, bh, start=begin, stop=False)
                            nc.tensor.matmul(out_, ah, bl, start=False, stop=False)
                            return nc.tensor.matmul(out_, al, bh, start=False, stop=end)

                        def gate_up(c):
                            r = height(c)
                            if c >= 2:
                                pe.wait_ge(m1_done, c - 1)
                            for wh, wl, bank in ((wgh, wgl, 0), (wuh, wul, 2)):
                                for k in range(KD):
                                    col = slice(c * P, c * P + r)
                                    mm = three(ps[0:r, bank + c % 2, :], wh[:, k, col], wl[:, k, col], xh2[0][:, k, :],
                                               xl2[0][:, k, :], k == 0, k == KD - 1)
                                mm.then_inc(gate_mm, 1)

                        def weights(c):
                            if c:
                                pe.wait_ge(m2_done, c)
                            nc.tensor.matmul(ps[0:height(c), 4, :], owner[:, c * P:c * P + height(c)], combT[0][:],
                                             start=True, stop=True).then_inc(bcast_mm, 1)

                        def down(c):
                            r = height(c)
                            pe.wait_ge(low_done, c + 1)
                            for m in range(KD):
                                mm = three(ps[:, 5 + m, :], wdh[0:r, c, m * P:(m + 1) * P], wdl[0:r, c, m * P:(m + 1) * P],
                                           hh[0:r, c % RING, :], hl[0:r, c % RING, :], c == 0, c == ND - 1)
                            mm.then_inc(down_mm, 1)

                        def turn_back(m, bank):
                            for t in range(TB):
                                mm = nc.tensor.transpose(ps[:, bank, t * P:(t + 1) * P], yT[:, m, t * P:(t + 1) * P], ident[:])
                            mm.then_inc(y_mm, 1)

                        def front_step(n):
                            if n == 0:
                                pe.wait_ge(ab_done, 1)
                                if back:
                                    pe.wait_ge(y_done, KD)
                            elif n == 7:
                                pe.wait_ge(cparts_done, 1)
                            else:
                                pe.wait_ge(front_taken, n)
                            if n in (0, 1):
                                for t in range(TB):
                                    mm = nc.tensor.transpose(ps[:, 7, t * P:(t + 1) * P], ab[:, t, n * P:(n + 1) * P], ident[:])
                            elif n in (2, 3):
                                for t in range(2 * (n - 2), 2 * (n - 2) + 2):
                                    for k in range(KD):
                                        mm = nc.tensor.matmul(ps[:, 7, (t % 2) * D:(t % 2 + 1) * D], aT[:, k, t * P:(t + 1) * P],
                                                              wot[:, k, :], start=(k == 0), stop=(k == KD - 1))
                            elif n in (4, 5):
                                pe.wait_ge(main.norm_done, TB)
                                for t in range(TB):
                                    mm = nc.tensor.transpose(ps[:, 7, t * P:(t + 1) * P], xn[:, t, (n - 4) * P:(n - 3) * P], ident[:])
                            elif n == 6:
                                for t in range(TB):
                                    mm = router(7, t)
                            else:
                                for t in range(TB):
                                    mm = nc.tensor.transpose(ps[0:CR, 7, t * P:(t + 1) * P], cpartsf[:, t, :], ident[:])
                            mm.then_inc(front_mm, 1)

                        if not ffn:
                            front_step(7)
                            return
                        for c in range(ND):
                            gate_up(c)
                            weights(c)
                            if back and c in BACK:
                                if BACK[c]:
                                    pe.wait_ge(y_done, BACK[c])
                                turn_back(BACK[c], 7)
                            if front and c in FRONT:
                                front_step(FRONT[c])
                            if c >= 2:
                                down(c - 2)
                        down(ND - 2)
                        down(ND - 1)
                        if not front:
                            pe.wait_ge(yT_done, KD)
                            pe.wait_ge(m1_done, ND)
                            turn_back(0, 0)
                            turn_back(1, 1)

                    @block.scalar
                    def _(act):
                        def silu(c):
                            act.wait_ge(gate_mm, 2 * c + 1)
                            if c >= 2:
                                act.wait_ge(m2_done, c - 1)
                            r = height(c)
                            nc.scalar.activation(sg[0:r, c % 2, :], ps[0:r, c % 2, :], ACT.Silu).then_inc(silu_done, 1)

                        def high(c):
                            act.wait_ge(m2_done, c + 1)
                            if c >= RING:
                                act.wait_ge(down_mm, c - RING + 1)
                            r = height(c)
                            nc.scalar.copy(hh[0:r, c % RING, :], hf[0:r, c % 2, :]).then_inc(high_done, 1)

                        def take(n):
                            act.wait_ge(front_mm, 1 if first else n + 1)
                            dst = {0: aT, 1: aT, 4: xnT, 5: xnT}.get(n)
                            if n == 7:
                                nc.scalar.copy(combT[nxt][:], ps[0:CR, 7, :]).then_inc(combT_done, 1)
                            else:
                                nc.scalar.copy(dst[:, n % 2, :], ps[:, 7, :]).then_inc(front_taken, 1)

                        if not ffn:
                            nc.scalar.copy(wuh[:], wuf[:]).then_inc(wu_split, 1)
                            nc.scalar.copy(wdh[:, 0:ND - 1], wdf[:, 0:ND - 1]).then_inc(wd_split, 1)
                            nc.scalar.copy(wdh[0:DR, ND - 1], wdf[0:DR, ND - 1]).then_inc(wd_split, 1)
                            take(7)
                            return
                        for c in range(ND):
                            silu(c)
                            if c:
                                high(c - 1)
                            n = FRONT.get(c)
                            if front and n in (0, 1, 4, 5, 7):
                                take(n)
                            if front and n == 6:
                                route_exps(act)
                        high(ND - 1)
                        act.wait_ge(down_mm, ND)
                        nc.scalar.copy(yT[:, 0, :], ps[:, 5, :]).then_inc(yT_done, 1)

                    @block.vector
                    def _(dve):
                        ch = Chain(dve)

                        def gated(c):
                            r = height(c)
                            dve.wait_ge(silu_done, c + 1)
                            dve.wait_ge(gate_mm, 2 * c + 2)
                            nc.vector.tensor_tensor(sg[0:r, c % 2, :], sg[0:r, c % 2, :], ps[0:r, 2 + c % 2, :], ALU.mult).then_inc(m1_done, 1)
                            dve.wait_ge(m1_done, c + 1)
                            dve.wait_ge(bcast_mm, c + 1)
                            if c >= 2:
                                dve.wait_ge(low_done, c - 1)
                            nc.vector.tensor_tensor(hf[0:r, c % 2, :], sg[0:r, c % 2, :], ps[0:r, 4, :], ALU.mult).then_inc(m2_done, 1)

                        def low(c):
                            r = height(c)
                            dve.wait_ge(high_done, c + 1)
                            nc.vector.tensor_tensor(hl[0:r, c % RING, :], hf[0:r, c % 2, :], f32(hh[0:r, c % RING, :]),
                                                    ALU.subtract).then_inc(low_done, 1)

                        def add_projection(n):
                            dve.wait_ge(front_mm, n + 1)
                            for t in range(2 * (n - 2), 2 * (n - 2) + 2):
                                w = nc.vector.tensor_tensor(rows_n(t), rows_n(t), ps[:, 7, (t % 2) * D:(t % 2 + 1) * D], ALU.add)
                                if t % 2 == 0:
                                    w.then_inc(front_x, 1)
                            w.then_inc(front_taken, 1)

                        def next_stats():
                            dve.wait_ge(front_x, 2)
                            dve.wait_ge(front_taken, 4)
                            norm_stats(dve, 0, rows_n, main)

                        def next_parts():
                            if not first:
                                dve.wait_ge(front_taken, 6)
                            ch(nc.vector.tensor_copy(xh2[nxt][:], xnT[:]))
                            ch.wait()
                            ch(nc.vector.tensor_tensor(xl2[nxt][:], xnT[:], f32(xh2[nxt][:]), ALU.subtract))

                        def route_start():
                            dve.wait_ge(front_mm, 7)
                            take_logits(ch, 7, front_taken)
                            dve.wait_ge(front_taken, 7)
                            choose_start(ch, TB, E1, z_ready1)

                        def combine_parts():
                            for s in range(PARTS):
                                if ch.n:
                                    ch.wait()
                                ch(nc.vector.tensor_copy(cparts[:, :, :, s], comb[:]))
                                ch.wait()
                                if s < PARTS - 1:
                                    ch(nc.vector.tensor_tensor(comb[:], comb[:], cparts[:, :, :, s], ALU.subtract))
                            nc.vector.tensor_copy(cpartsf[:], cparts[:].rearrange("p t e s -> p t (e s)")).then_inc(cparts_done, 1)

                        if not ffn:
                            combine_parts()
                            next_parts()
                            ch(nc.vector.tensor_copy(wgh[:], wgf[:]))
                            ch.wait()
                            nc.vector.tensor_tensor(wgl[:], wgf[:], f32(wgh[:]), ALU.subtract)
                            dve.wait_ge(wu_split, 1)
                            nc.vector.tensor_tensor(wul[:], wuf[:], f32(wuh[:]), ALU.subtract)
                            return
                        def result(batch, m, bank, count):
                            dve.wait_ge(y_mm, count)
                            nc.vector.tensor_tensor(yout[:, :, m * P:(m + 1) * P], x[:, bass.ds(TB * batch, TB), m * P:(m + 1) * P],
                                                    ps[:, bank, :].rearrange("p (t d) -> p t d", t=TB), ALU.add).then_inc(y_done, 1)

                        for c in range(ND):
                            gated(c)
                            if c:
                                low(c - 1)
                            if back and c in BACK:
                                result(b - 1, BACK[c], 7, BACK[c] + 1)
                            if front:
                                if c == 4:
                                    add_projection(2)
                                elif c == 5:
                                    add_projection(3)
                                    next_stats()
                                elif c == 6:
                                    norm_apply(dve, 0, rows_n, main)
                                elif c == 8:
                                    next_parts()
                                elif c == 9:
                                    route_start()
                                elif c == 10:
                                    choose_top(dve, ch, TB, E1, ez_ready1)
                                elif c == 11:
                                    choose_hits(ch, TB, E1, TOP1)
                                    combine(dve, ch)
                                elif c == 12:
                                    combine_parts()
                        low(ND - 1)
                        if front:
                            dve.wait_ge(gate_mm, 2 * ND)
                            nc.vector.tensor_copy(xh2[0][:], f32(xh2[1][:]))
                            nc.vector.tensor_copy(xl2[0][:], f32(xl2[1][:]))
                            dve.wait_ge(bcast_mm, ND)
                            dve.wait_ge(combT_done, 1)
                            nc.vector.tensor_copy(combT[0][:], combT[1][:])
                        dve.wait_ge(down_mm, ND)
                        nc.vector.tensor_copy(yT[:, 1, :], ps[:, 6, :]).then_inc(yT_done, 1)
                        if not front:
                            if back:
                                dve.wait_ge(stored, 16)
                            before = KD if back else 0
                            result(b, 0, 0, before + 1)
                            result(b, 1, 1, before + 2)

            trip(-1, False, True, True, False)
            clear(step, *trip_sems, *route_sems, *main.norm_sems)
            arrivals.close()
            sg = sb("sg", [P, 2, S], F32, l3)
            hf = sb("hf1", [P, 2, S], F32, l3)
            hh, hl = (sb(n, [P, RING, S], F32R, l3) for n in ("hh", "hl"))
            yT = sb("yT", [P, KD, S], F32, l3)
            yout = sb("yout", [P, TB, D], F32, l3)
            trip(0, True, True, False, False)
            clear(step, *trip_sems, *route_sems, *main.norm_sems)
            with nc.Fori(0, NB - 2) as b:
                trip(b + 1, True, True, False, True)
                clear(step, *trip_sems, *route_sems, *main.norm_sems)
            trip(NB - 1, True, False, False, True)


def kernel(**inputs):
    import numpy as _np
    import concourse.bacc as _bacc
    from concourse import mybir as _mybir
    from concourse.bass_utils import run_bass_kernel_spmd as _run

    n = {k: _np.asarray(v) for k, v in inputs.items()}
    arrays = {k: n[k] for k in ("L0_attn_W_q", "L0_attn_W_k", "L0_attn_W_v", "L0_attn_W_o", "L0_ffn_Wr", "L0_ffn_br",
                                "L0_ffn_w1", "L0_ffn_w2", "L0_ffn_b2", "L0_ffn_Wp1", "L0_ffn_bp1", "L0_ffn_Wp2",
                                "L0_ffn_bp2")}
    arrays["x"] = n["L0_attn_x"].reshape(NB * S, D)
    arrays["b1T"] = n["L0_ffn_b1"].reshape(E0 * NI, P).T
    arrays["kT"] = n["L1_attn_kv_k"].reshape(KEYS, D).T
    arrays["v"] = n["L1_attn_kv_v"].reshape(KEYS, D)
    arrays["wqT"] = n["L1_attn_Wq"].T
    arrays["woT"] = n["L1_attn_Wo"].T
    arrays["gateT"] = _np.concatenate([n["L1_ffn_gate_w"], n["L1_ffn_shgate_w"][None]]).T
    for name, w, sh in (("wg", "w_gate", "shw_gate"), ("wu", "w_up", "shw_up")):
        arrays[name] = _np.concatenate([n["L1_ffn_" + w].transpose(1, 0, 2).reshape(D, E1 * H1), n["L1_ffn_" + sh]], 1)
    arrays["wd"] = _np.concatenate([n["L1_ffn_w_down"].reshape(E1 * H1, D), n["L1_ffn_shw_down"]])

    nc = _bacc.Bacc("TRN2", target_bir_lowering=False, num_devices=1)
    feed, aps = {}, {}
    for k, v in arrays.items():
        v = _np.ascontiguousarray(v)
        feed[f"in_{k}"] = v
        aps[k] = nc.dram_tensor(f"in_{k}", v.shape, _mybir.dt.from_np(v.dtype), kind="ExternalInput").ap()
    out = nc.dram_tensor("out_x", (NB * S, D), _mybir.dt.float32, kind="ExternalOutput").ap()
    build(nc, aps, out)
    r = _run(nc, [feed], core_ids=[0])
    return r.results[0]["out_x"].reshape(NB, S, D)
```
